# Optimizing a Trainium2 kernel written in Bass

```python
import numpy as np
import jax
import jax.numpy as jnp

def _softmax(x, axis=-1):
    return jax.nn.softmax(x, axis=axis)

def _gelu(x):
    return jax.nn.gelu(x, approximate=True)

def _silu(x):
    return jax.nn.silu(x)

def _sigmoid(x):
    return jax.nn.sigmoid(x)

def _layernorm(x, axis=-1, eps=1e-05):
    m = jnp.mean(x, axis=axis, keepdims=True)
    v = jnp.var(x, axis=axis, keepdims=True)
    return (x - m) / jnp.sqrt(v + eps)

def _scatter_add(tgt, idx, src, axis=0):
    return tgt.at[idx].add(src)

def _segment_sum(src, seg, n):
    return jax.ops.segment_sum(src, seg, n)
kernel_name = 'mk_perceiver_d2_seqx_r8_dd2622'

def setup_inputs(seed: int=0):
    np.random.seed(seed)
    _w = jnp.asarray

    def _rec_inputs():
        import jax
        import jax.numpy as jnp
        _rk = jax.random.key(seed)
        x = 0.0002417 + 0.9998 * jax.random.normal(jax.random.fold_in(_rk, 1), (4, 128, 128), jnp.float32)
        _lenS = 128 - jax.random.randint(jax.random.fold_in(_rk, 7), (4,), 0, max(1, 128 // 4) + 1, jnp.int32)
        _lenS2 = 2048 - jax.random.randint(jax.random.fold_in(_rk, 8), (4,), 0, max(1, 2048 // 4) + 1, jnp.int32)
        _ctx_1024P = jax.random.normal(jax.random.fold_in(_rk, 11), (4, 16, 128), jnp.float32)
        _ctx_1024c = jax.random.dirichlet(jax.random.fold_in(_rk, 511), 0.3 * jnp.ones((16,), jnp.float32), (4, 2048))
        _ctx_1024t = jnp.einsum('bsk,bkd->bsd', _ctx_1024c, _ctx_1024P)
        _ctx_1024t = _ctx_1024t * jax.lax.rsqrt(jnp.mean(jnp.square(_ctx_1024t)) + 1e-12) * 0.953939
        ctx_1024 = 7.22013e-05 + 1.00017 * (_ctx_1024t + 0.3 * jax.random.normal(jax.random.fold_in(_rk, 611), (4, 2048, 128), jnp.float32))
        _validS = jnp.arange(128)[None, :] < _lenS[:, None]
        _validS2 = jnp.arange(2048)[None, :] < _lenS2[:, None]
        _causal = jnp.tril(jnp.ones((128, 128), dtype=bool))
        mask_BxS2_if0 = jnp.where(jnp.ones((4, 2048), dtype=bool), 0, 1).astype(jnp.int32)
        mask_1x1xSxS2_ik0 = jnp.where(jnp.broadcast_to(_validS2[0:1, None, None, :], (1, 1, 128, 2048)), 0, 1).astype(jnp.int32)
        return (x, ctx_1024, mask_BxS2_if0, mask_1x1xSxS2_ik0)
    x, ctx_1024, mask_BxS2_if0, mask_1x1xSxS2_ik0 = _rec_inputs()

    def _L0_xattn_setup():
        import jax, jax.numpy as jnp
        import numpy as np
        import math
        B, M, D, H, NK = (4, 256, 128, 16, 5)
        HD = D // H

        def _gather_pad0(x, idx):
            Bx, Hx, W, hd = x.shape
            valid = (idx >= 0) & (idx < W)
            idxc = jnp.clip(idx, 0, W - 1).reshape(Bx, Hx, -1)
            g = jnp.take_along_axis(x, idxc[..., None], axis=2)
            g = g.reshape(idx.shape + (hd,))
            return g * valid[..., None].astype(x.dtype)
        key = jax.random.key(seed)
        ks = jax.random.split(key, 9)
        w = lambda k, shape: jax.random.normal(k, shape, jnp.float32) * 0.02
        return {'k': jax.random.normal(ks[0], (B, M, D), jnp.float32), 'v': jax.random.normal(ks[1], (B, M, D), jnp.float32), 'q': jax.random.normal(ks[2], (B, M, D), jnp.float32), 'mask': jnp.zeros((B, M), jnp.int32), 'Wk': w(ks[3], (D, D)), 'bk': jnp.zeros((D,), jnp.float32), 'Wv': w(ks[4], (D, D)), 'bv': jnp.zeros((D,), jnp.float32), 'Wq': w(ks[5], (D, D)), 'bq': jnp.zeros((D,), jnp.float32), 'Woff': w(ks[6], (H * NK, D)), 'boff': jnp.zeros((H * NK,), jnp.float32), 'Wo': w(ks[7], (D, D)), 'bo': jnp.zeros((D,), jnp.float32)}
    _L0_xattn_all = _L0_xattn_setup()
    _L0_xattn_in = {k: v for k, v in _L0_xattn_all.items() if k in ('Wk', 'bk', 'Wv', 'bv', 'Wq', 'bq', 'Woff', 'boff', 'Wo', 'bo')}
    del _L0_xattn_all

    def _L0_attn_setup():
        import jax, jax.numpy as jnp
        import numpy as np
        B, T, C, H = (2, 256, 128, 16)
        DH = C // H
        EPS = 1e-05

        def _rotary(t_len, d_head):
            inv_freq = 1.0 / 10000.0 ** (jnp.arange(0, d_head, 2, dtype=jnp.float32) / d_head)
            t = jnp.arange(t_len, dtype=jnp.float32)
            freqs = t[:, None] * inv_freq[None, :]
            emb = jnp.concatenate([freqs, freqs], axis=-1)
            return (jnp.cos(emb), jnp.sin(emb))

        def _apply_rope(x, cos, sin):
            d = x.shape[-1]
            x1, x2 = (x[..., :d // 2], x[..., d // 2:])
            x_rot = jnp.concatenate([-x2, x1], axis=-1)
            return x * cos + x_rot * sin

        def _decay_mask(t_len, n_head):
            gammas = 1.0 - 2.0 ** (-5.0 - jnp.arange(n_head, dtype=jnp.float32))
            n = jnp.arange(t_len)[:, None]
            m = jnp.arange(t_len)[None, :]
            dist = n - m
            decay = gammas[:, None, None] ** jnp.maximum(dist, 0).astype(jnp.float32)
            return jnp.where(dist[None] >= 0, decay, 0.0)
        key = jax.random.key(seed)
        ks = jax.random.split(key, 7)
        s = 1.0 / np.sqrt(C)
        return {'x': jax.random.normal(ks[0], (B, T, C), dtype=jnp.float32), 'Wq': jax.random.normal(ks[1], (C, C), dtype=jnp.float32) * s, 'Wk': jax.random.normal(ks[2], (C, C), dtype=jnp.float32) * s, 'Wv': jax.random.normal(ks[3], (C, C), dtype=jnp.float32) * s, 'Wo': jax.random.normal(ks[4], (C, C), dtype=jnp.float32) * s, 'gn_weight': jnp.ones((C,), dtype=jnp.float32), 'gn_bias': jnp.zeros((C,), dtype=jnp.float32)}
    _L0_attn_all = _L0_attn_setup()
    _L0_attn_in = {k: v for k, v in _L0_attn_all.items() if k in ('Wq', 'Wk', 'Wv', 'Wo', 'gn_weight', 'gn_bias')}
    del _L0_attn_all

    def _L0_ffn_setup():
        import jax, jax.numpy as jnp
        import numpy as np
        TOP_K = 2
        EPS = 1e-09
        key = jax.random.key(seed)
        ks = jax.random.split(key, 6)
        B, T, D, H, E = (4, 256, 128, 256, 8)
        x = jax.random.normal(ks[0], (B, T, D), dtype=jnp.float32)
        Wg = jax.random.normal(ks[1], (E, D), dtype=jnp.float32) * 0.02
        W1 = jax.random.normal(ks[2], (E, 2 * H, D), dtype=jnp.float32) * 0.02
        b1 = jax.random.normal(ks[3], (E, 2 * H), dtype=jnp.float32) * 0.02
        Wo = jax.random.normal(ks[4], (D, H), dtype=jnp.float32) * 0.02
        bo = jax.random.normal(ks[5], (D,), dtype=jnp.float32) * 0.02
        return {'x': x, 'Wg': Wg, 'W1': W1, 'b1': b1, 'Wo': Wo, 'bo': bo}
    _L0_ffn_all = _L0_ffn_setup()
    _L0_ffn_in = {k: v for k, v in _L0_ffn_all.items() if k in ('Wg', 'W1', 'b1', 'Wo', 'bo')}
    del _L0_ffn_all

    def _L1_xattn_setup():
        import jax, jax.numpy as jnp
        import numpy as np
        D_MODEL = 128
        NUM_HEADS = 16
        D_K = D_MODEL // NUM_HEADS
        SCALE = float(np.sqrt(D_K))
        B, S = (4, 256)
        key = jax.random.key(seed)
        ks = jax.random.split(key, 12)
        q = jax.random.normal(ks[0], (B, S, D_MODEL), dtype=jnp.float32)
        k = jax.random.normal(ks[1], (B, S, D_MODEL), dtype=jnp.float32)
        v = jax.random.normal(ks[2], (B, S, D_MODEL), dtype=jnp.float32)
        mask = jnp.tril(jnp.ones((S, S), dtype=jnp.int32))[None, None]
        std = 1.0 / np.sqrt(D_MODEL)
        Wq = jax.random.normal(ks[3], (D_MODEL, D_MODEL), dtype=jnp.float32) * std
        Wk = jax.random.normal(ks[4], (D_MODEL, D_MODEL), dtype=jnp.float32) * std
        Wv = jax.random.normal(ks[5], (D_MODEL, D_MODEL), dtype=jnp.float32) * std
        Wo = jax.random.normal(ks[6], (D_MODEL, D_MODEL), dtype=jnp.float32) * std
        bq = jax.random.normal(ks[7], (D_MODEL,), dtype=jnp.float32) * std
        bk = jax.random.normal(ks[8], (D_MODEL,), dtype=jnp.float32) * std
        bv = jax.random.normal(ks[9], (D_MODEL,), dtype=jnp.float32) * std
        bo = jax.random.normal(ks[10], (D_MODEL,), dtype=jnp.float32) * std
        return {'q': q, 'k': k, 'v': v, 'mask': mask, 'Wq': Wq, 'bq': bq, 'Wk': Wk, 'bk': bk, 'Wv': Wv, 'bv': bv, 'Wo': Wo, 'bo': bo}
    _L1_xattn_all = _L1_xattn_setup()
    _L1_xattn_in = {k: v for k, v in _L1_xattn_all.items() if k in ('Wq', 'bq', 'Wk', 'bk', 'Wv', 'bv', 'Wo', 'bo')}
    del _L1_xattn_all

    def _L1_attn_setup():
        import jax, jax.numpy as jnp
        import numpy as np
        D = 128
        H = 16
        DK = D // 2
        DV = D
        HDK = DK // H
        HDV = DV // H
        RATIO = 2
        FF = 352
        EPS = 1e-05
        ROPE_BASE = 10000.0

        def layernorm(x, w, b):
            mu = jnp.mean(x, axis=-1, keepdims=True)
            var = jnp.var(x, axis=-1, keepdims=True)
            return (x - mu) * jax.lax.rsqrt(var + EPS) * w + b

        def rope(t, cos, sin):
            half = HDK // 2
            t1, t2 = (t[..., :half], t[..., half:])
            return jnp.concatenate([t1 * cos - t2 * sin, t2 * cos + t1 * sin], axis=-1)

        def _forward(x, ln1_w, ln1_b, ln2_w, ln2_b, conv_w, Wq, Wk, Wv, Wg, Wout, router_w, w1, w3, w2):
            residual = x
            h = layernorm(x, ln1_w, ln1_b)
            h = jnp.transpose(h, (1, 0, 2))
            b, l, d = h.shape
            h_prev = jnp.pad(h, ((0, 0), (1, 0), (0, 0)))[:, :-1]
            h = jax.nn.silu(h_prev * conv_w[:, 0] + h * conv_w[:, 1])
            q = jax.nn.silu(h @ Wq)
            k = h @ Wk
            v = h @ Wv
            g = h @ Wg
            q = q.reshape(b, l, H, HDK).transpose(0, 2, 1, 3)
            k = k.reshape(b, l, H, HDK).transpose(0, 2, 1, 3)
            v = v.reshape(b, l, H, HDV).transpose(0, 2, 1, 3)
            half = HDK // 2
            inv_freq = 1.0 / ROPE_BASE ** (jnp.arange(0, half, dtype=jnp.float32) * 2.0 / HDK)
            freqs = jnp.arange(l, dtype=jnp.float32)[:, None] * inv_freq[None, :]
            cos, sin = (jnp.cos(freqs)[None, None], jnp.sin(freqs)[None, None])
            q = rope(q, cos, sin)
            k = rope(k, cos, sin)
            logits = jnp.einsum('bhld,hdr->bhlr', v, router_w)
            scores = jax.nn.softmax(logits, axis=-1)
            idx = jnp.argmax(scores, axis=-1)
            onehot = jnp.arange(RATIO) == idx[..., None]
            masked_scores = jnp.where(onehot, scores, 0.0)
            masked_indices = onehot.astype(q.dtype)
            sum_indices = jnp.cumsum(masked_indices, axis=2)
            norm_score = jnp.where(sum_indices == 0, 0.0, 1.0 / sum_indices)[..., None]
            q_exp = q[:, :, :, None, :] * masked_scores[..., None] * norm_score
            k_exp = k[:, :, :, None, :] * masked_indices[..., None]
            q_exp = q_exp.reshape(b, H, l, RATIO * HDK)
            k_exp = k_exp.reshape(b, H, l, RATIO * HDK)
            qk = jnp.einsum('bhld,bhmd->bhlm', q_exp, k_exp) * HDK ** (-0.5)
            causal = jnp.tril(jnp.ones((l, l), qk.dtype))
            qk = qk * causal
            o = jnp.einsum('bhlm,bhmd->bhld', qk, v)
            o = o.transpose(0, 2, 1, 3)
            mu = jnp.mean(o, axis=-1, keepdims=True)
            var = jnp.var(o, axis=-1, keepdims=True)
            o = (o - mu) * jax.lax.rsqrt(var + EPS)
            o = jax.nn.silu(g) * o.reshape(b, l, d)
            o = o @ Wout
            attn_out = jnp.transpose(o, (1, 0, 2)) + residual
            h2 = layernorm(attn_out, ln2_w, ln2_b)
            mlp_out = jax.nn.silu(h2 @ w1) * (h2 @ w3) @ w2
            return mlp_out + attn_out
        key = jax.random.key(seed)
        ks = jax.random.split(key, 16)
        l, b = (256, 2)
        s = 1.0 / np.sqrt(D)
        inp = {'x': jax.random.normal(ks[0], (l, b, D), jnp.float32), 'attention_mask': jnp.ones((b, l), jnp.bool_), 'ln1_w': jnp.ones((D,), jnp.float32), 'ln1_b': jnp.zeros((D,), jnp.float32), 'ln2_w': jnp.ones((D,), jnp.float32), 'ln2_b': jnp.zeros((D,), jnp.float32), 'conv_w': jax.random.normal(ks[1], (D, 2), jnp.float32) * 0.5, 'Wq': jax.random.normal(ks[2], (D, DK), jnp.float32) * s, 'Wk': jax.random.normal(ks[3], (D, DK), jnp.float32) * s, 'Wv': jax.random.normal(ks[4], (D, DV), jnp.float32) * s, 'Wg': jax.random.normal(ks[5], (D, DV), jnp.float32) * s, 'Wout': jax.random.normal(ks[6], (DV, D), jnp.float32) * s, 'router_w': jax.random.normal(ks[7], (H, HDV, RATIO), jnp.float32) * (1.0 / np.sqrt(HDV)), 'w1': jax.random.normal(ks[8], (D, FF), jnp.float32) * s, 'w3': jax.random.normal(ks[9], (D, FF), jnp.float32) * s, 'w2': jax.random.normal(ks[10], (FF, D), jnp.float32) * (1.0 / np.sqrt(FF))}
        return inp
    _L1_attn_all = _L1_attn_setup()
    _L1_attn_in = {k: v for k, v in _L1_attn_all.items() if k in ('attention_mask', 'ln1_w', 'ln1_b', 'ln2_w', 'ln2_b', 'conv_w', 'Wq', 'Wk', 'Wv', 'Wg', 'Wout', 'router_w', 'w1', 'w3', 'w2')}
    del _L1_attn_all

    def _L1_ffn_setup():
        import jax, jax.numpy as jnp
        import numpy as np
        N_EXPERTS = 8
        TOP_K = 2
        key = jax.random.key(seed)
        k1, k2, k3, k4 = jax.random.split(key, 4)
        B, T, C, H, E = (2, 256, 128, 512, N_EXPERTS)
        x = jax.random.normal(k1, (B, T, C), dtype=jnp.float32)
        router_w = jax.random.normal(k2, (E, C), dtype=jnp.float32) * 0.02
        w1 = jax.random.normal(k3, (E, C, H), dtype=jnp.float32) * (1.0 / np.sqrt(C))
        w2 = jax.random.normal(k4, (E, H, C), dtype=jnp.float32) * (1.0 / np.sqrt(H))
        return {'x': x, 'router_w': router_w, 'w1': w1, 'w2': w2}
    _L1_ffn_all = _L1_ffn_setup()
    _L1_ffn_in = {k: v for k, v in _L1_ffn_all.items() if k in ('router_w', 'w1', 'w2')}
    del _L1_ffn_all
    return {'x': x, 'ctx_1024': ctx_1024, 'mask_BxS2_if0': mask_BxS2_if0, 'mask_1x1xSxS2_ik0': mask_1x1xSxS2_ik0, 'L0_xattn_Wk': _L0_xattn_in['Wk'], 'L0_xattn_bk': _L0_xattn_in['bk'], 'L0_xattn_Wv': _L0_xattn_in['Wv'], 'L0_xattn_bv': _L0_xattn_in['bv'], 'L0_xattn_Wq': _L0_xattn_in['Wq'], 'L0_xattn_bq': _L0_xattn_in['bq'], 'L0_xattn_Woff': _L0_xattn_in['Woff'], 'L0_xattn_boff': _L0_xattn_in['boff'], 'L0_xattn_Wo': _L0_xattn_in['Wo'], 'L0_xattn_bo': _L0_xattn_in['bo'], 'L0_attn_Wq': _L0_attn_in['Wq'], 'L0_attn_Wk': _L0_attn_in['Wk'], 'L0_attn_Wv': _L0_attn_in['Wv'], 'L0_attn_Wo': _L0_attn_in['Wo'], 'L0_attn_gn_weight': _L0_attn_in['gn_weight'], 'L0_attn_gn_bias': _L0_attn_in['gn_bias'], 'L0_ffn_Wg': _L0_ffn_in['Wg'], 'L0_ffn_W1': _L0_ffn_in['W1'], 'L0_ffn_b1': _L0_ffn_in['b1'], 'L0_ffn_Wo': _L0_ffn_in['Wo'], 'L0_ffn_bo': _L0_ffn_in['bo'], 'L1_xattn_Wq': _L1_xattn_in['Wq'], 'L1_xattn_bq': _L1_xattn_in['bq'], 'L1_xattn_Wk': _L1_xattn_in['Wk'], 'L1_xattn_bk': _L1_xattn_in['bk'], 'L1_xattn_Wv': _L1_xattn_in['Wv'], 'L1_xattn_bv': _L1_xattn_in['bv'], 'L1_xattn_Wo': _L1_xattn_in['Wo'], 'L1_xattn_bo': _L1_xattn_in['bo'], 'L1_attn_attention_mask': _L1_attn_in['attention_mask'], 'L1_attn_ln1_w': _L1_attn_in['ln1_w'], 'L1_attn_ln1_b': _L1_attn_in['ln1_b'], 'L1_attn_ln2_w': _L1_attn_in['ln2_w'], 'L1_attn_ln2_b': _L1_attn_in['ln2_b'], 'L1_attn_conv_w': _L1_attn_in['conv_w'], 'L1_attn_Wq': _L1_attn_in['Wq'], 'L1_attn_Wk': _L1_attn_in['Wk'], 'L1_attn_Wv': _L1_attn_in['Wv'], 'L1_attn_Wg': _L1_attn_in['Wg'], 'L1_attn_Wout': _L1_attn_in['Wout'], 'L1_attn_router_w': _L1_attn_in['router_w'], 'L1_attn_w1': _L1_attn_in['w1'], 'L1_attn_w3': _L1_attn_in['w3'], 'L1_attn_w2': _L1_attn_in['w2'], 'L1_ffn_router_w': _L1_ffn_in['router_w'], 'L1_ffn_w1': _L1_ffn_in['w1'], 'L1_ffn_w2': _L1_ffn_in['w2']}

def reference(x, ctx_1024, mask_BxS2_if0, mask_1x1xSxS2_ik0, L0_xattn_Wk, L0_xattn_bk, L0_xattn_Wv, L0_xattn_bv, L0_xattn_Wq, L0_xattn_bq, L0_xattn_Woff, L0_xattn_boff, L0_xattn_Wo, L0_xattn_bo, L0_attn_Wq, L0_attn_Wk, L0_attn_Wv, L0_attn_Wo, L0_attn_gn_weight, L0_attn_gn_bias, L0_ffn_Wg, L0_ffn_W1, L0_ffn_b1, L0_ffn_Wo, L0_ffn_bo, L1_xattn_Wq, L1_xattn_bq, L1_xattn_Wk, L1_xattn_bk, L1_xattn_Wv, L1_xattn_bv, L1_xattn_Wo, L1_xattn_bo, L1_attn_attention_mask, L1_attn_ln1_w, L1_attn_ln1_b, L1_attn_ln2_w, L1_attn_ln2_b, L1_attn_conv_w, L1_attn_Wq, L1_attn_Wk, L1_attn_Wv, L1_attn_Wg, L1_attn_Wout, L1_attn_router_w, L1_attn_w1, L1_attn_w3, L1_attn_w2, L1_ffn_router_w, L1_ffn_w1, L1_ffn_w2):
    import jax
    import jax.numpy as jnp

    def _L0_xattn_ref(k, v, q, mask, Wk, bk, Wv, bv, Wq, bq, Woff, boff, Wo, bo):
        import jax, jax.numpy as jnp
        import numpy as np
        import math
        B, M, D, H, NK = (4, 256, 128, 16, 5)
        HD = D // H

        def _gather_pad0(x, idx):
            Bx, Hx, W, hd = x.shape
            valid = (idx >= 0) & (idx < W)
            idxc = jnp.clip(idx, 0, W - 1).reshape(Bx, Hx, -1)
            g = jnp.take_along_axis(x, idxc[..., None], axis=2)
            g = g.reshape(idx.shape + (hd,))
            return g * valid[..., None].astype(x.dtype)
        Bq, Q, _ = q.shape
        key_len = k.shape[1]
        K = jnp.einsum('bmd,ed->bme', k, Wk) + bk
        V = jnp.einsum('bmd,ed->bme', v, Wv) + bv
        Qp = jnp.einsum('bqd,ed->bqe', q, Wq) + bq
        off = jnp.einsum('bqd,ed->bqe', Qp, Woff) + boff
        off = off.reshape(Bq, Q, H, NK).transpose(0, 2, 1, 3)
        Kh = K.reshape(Bq, key_len, H, HD).transpose(0, 2, 1, 3)
        Vh = V.reshape(Bq, key_len, H, HD).transpose(0, 2, 1, 3)
        Qh = Qp.reshape(Bq, Q, H, HD).transpose(0, 2, 1, 3)
        loc = jnp.arange(Q, dtype=jnp.float32)[:, None]
        left = -NK // 2
        ref = jnp.arange(left, NK + left, dtype=jnp.float32)
        sign_lens = (1 - mask).sum(-1).astype(jnp.float32) - 1.0
        loc_x = jnp.mod(ref + off + loc, sign_lens[:, None, None, None])
        xg = loc_x / (key_len - 1) * 2.0 - 1.0
        ix = ((xg + 1.0) * key_len - 1.0) / 2.0
        x0 = jnp.floor(ix)
        dx = ix - x0
        i0 = x0.astype(jnp.int32)
        i1 = i0 + 1
        w0 = (1.0 - dx)[..., None]
        w1 = dx[..., None]
        sk = 0.5 * (w0 * _gather_pad0(Kh, i0) + w1 * _gather_pad0(Kh, i1))
        sv = 0.5 * (w0 * _gather_pad0(Vh, i0) + w1 * _gather_pad0(Vh, i1))
        scores = jnp.einsum('bhqd,bhqkd->bhqk', Qh / math.sqrt(HD), sk)
        attn = jax.nn.softmax(scores, axis=-1)
        ctx = jnp.einsum('bhqk,bhqkd->bhqd', attn, sv)
        ctx = ctx.transpose(0, 2, 1, 3).reshape(Bq, Q, H * HD)
        return jnp.einsum('bqd,ed->bqe', ctx, Wo) + bo

    def _L0_attn_ref(x, Wq, Wk, Wv, Wo, gn_weight, gn_bias):
        import jax, jax.numpy as jnp
        import numpy as np
        B, T, C, H = (2, 256, 128, 16)
        DH = C // H
        EPS = 1e-05

        def _rotary(t_len, d_head):
            inv_freq = 1.0 / 10000.0 ** (jnp.arange(0, d_head, 2, dtype=jnp.float32) / d_head)
            t = jnp.arange(t_len, dtype=jnp.float32)
            freqs = t[:, None] * inv_freq[None, :]
            emb = jnp.concatenate([freqs, freqs], axis=-1)
            return (jnp.cos(emb), jnp.sin(emb))

        def _apply_rope(x, cos, sin):
            d = x.shape[-1]
            x1, x2 = (x[..., :d // 2], x[..., d // 2:])
            x_rot = jnp.concatenate([-x2, x1], axis=-1)
            return x * cos + x_rot * sin

        def _decay_mask(t_len, n_head):
            gammas = 1.0 - 2.0 ** (-5.0 - jnp.arange(n_head, dtype=jnp.float32))
            n = jnp.arange(t_len)[:, None]
            m = jnp.arange(t_len)[None, :]
            dist = n - m
            decay = gammas[:, None, None] ** jnp.maximum(dist, 0).astype(jnp.float32)
            return jnp.where(dist[None] >= 0, decay, 0.0)
        b, t, c = x.shape

        def proj(W):
            return jnp.einsum('btc,oc->bto', x, W).reshape(b, t, H, DH).transpose(0, 2, 1, 3)
        q, k, v = (proj(Wq), proj(Wk), proj(Wv))
        cos, sin = _rotary(t, DH)
        q = _apply_rope(q, cos, sin)
        k = _apply_rope(k, cos, sin)
        decay = _decay_mask(t, H)
        qk = jnp.einsum('bhtd,bhsd->bhts', q, k) * (1.0 / np.sqrt(DH))
        qk = qk * decay[None]
        out = jnp.einsum('bhts,bhsd->bhtd', qk, v)
        out = out.transpose(0, 2, 1, 3)
        mu = jnp.mean(out, axis=-1, keepdims=True)
        var = jnp.mean((out - mu) ** 2, axis=-1, keepdims=True)
        out = (out - mu) * jax.lax.rsqrt(var + EPS)
        out = out * gn_weight.reshape(H, DH) + gn_bias.reshape(H, DH)
        out = out.reshape(b, t, c)
        return jnp.einsum('btc,oc->bto', out, Wo)

    def _L0_ffn_ref(x, Wg, W1, b1, Wo, bo):
        import jax, jax.numpy as jnp
        import numpy as np
        TOP_K = 2
        EPS = 1e-09
        E = Wg.shape[0]
        gate_logits = jnp.einsum('btd,ed->bte', x, Wg)
        gate_scores = jax.nn.softmax(gate_logits, axis=-1)
        topk_val, topk_idx = jax.lax.top_k(gate_scores, TOP_K)
        topk_val = topk_val / (topk_val.sum(axis=-1, keepdims=True) + EPS)
        comb = (jax.nn.one_hot(topk_idx, E, dtype=x.dtype) * topk_val[..., None]).sum(axis=-2)
        out = jnp.zeros_like(x)
        for e in range(E):
            h = jnp.einsum('btd,hd->bth', x, W1[e]) + b1[e]
            a, b = jnp.split(h, 2, axis=-1)
            g = a * jax.nn.sigmoid(b)
            eo = jnp.einsum('bth,dh->btd', g, Wo) + bo
            out = out + eo * comb[..., e:e + 1]
        return out

    def _L1_xattn_ref(q, k, v, mask, Wq, bq, Wk, bk, Wv, bv, Wo, bo):
        import jax, jax.numpy as jnp
        import numpy as np
        D_MODEL = 128
        NUM_HEADS = 16
        D_K = D_MODEL // NUM_HEADS
        SCALE = float(np.sqrt(D_K))
        B, S = (4, 256)
        Bsz = q.shape[0]

        def proj(x, W, b):
            y = x @ W.T + b
            return y.reshape(Bsz, -1, NUM_HEADS, D_K).transpose(0, 2, 1, 3)
        qh = proj(q, Wq, bq)
        kh = proj(k, Wk, bk)
        vh = proj(v, Wv, bv)
        scores = jnp.einsum('bhqd,bhkd->bhqk', qh, kh) / SCALE
        scores = jnp.where(mask == 0, jnp.float32(-1000000000.0), scores)
        attn = jax.nn.softmax(scores, axis=-1)
        out = jnp.einsum('bhqk,bhkd->bhqd', attn, vh)
        out = out.transpose(0, 2, 1, 3).reshape(Bsz, -1, D_MODEL)
        return out @ Wo.T + bo

    def _L1_attn_ref(x, attention_mask, ln1_w, ln1_b, ln2_w, ln2_b, conv_w, Wq, Wk, Wv, Wg, Wout, router_w, w1, w3, w2):
        import jax, jax.numpy as jnp
        import numpy as np
        D = 128
        H = 16
        DK = D // 2
        DV = D
        HDK = DK // H
        HDV = DV // H
        RATIO = 2
        FF = 352
        EPS = 1e-05
        ROPE_BASE = 10000.0

        def layernorm(x, w, b):
            mu = jnp.mean(x, axis=-1, keepdims=True)
            var = jnp.var(x, axis=-1, keepdims=True)
            return (x - mu) * jax.lax.rsqrt(var + EPS) * w + b

        def rope(t, cos, sin):
            half = HDK // 2
            t1, t2 = (t[..., :half], t[..., half:])
            return jnp.concatenate([t1 * cos - t2 * sin, t2 * cos + t1 * sin], axis=-1)

        def _forward(x, ln1_w, ln1_b, ln2_w, ln2_b, conv_w, Wq, Wk, Wv, Wg, Wout, router_w, w1, w3, w2):
            residual = x
            h = layernorm(x, ln1_w, ln1_b)
            h = jnp.transpose(h, (1, 0, 2))
            b, l, d = h.shape
            h_prev = jnp.pad(h, ((0, 0), (1, 0), (0, 0)))[:, :-1]
            h = jax.nn.silu(h_prev * conv_w[:, 0] + h * conv_w[:, 1])
            q = jax.nn.silu(h @ Wq)
            k = h @ Wk
            v = h @ Wv
            g = h @ Wg
            q = q.reshape(b, l, H, HDK).transpose(0, 2, 1, 3)
            k = k.reshape(b, l, H, HDK).transpose(0, 2, 1, 3)
            v = v.reshape(b, l, H, HDV).transpose(0, 2, 1, 3)
            half = HDK // 2
            inv_freq = 1.0 / ROPE_BASE ** (jnp.arange(0, half, dtype=jnp.float32) * 2.0 / HDK)
            freqs = jnp.arange(l, dtype=jnp.float32)[:, None] * inv_freq[None, :]
            cos, sin = (jnp.cos(freqs)[None, None], jnp.sin(freqs)[None, None])
            q = rope(q, cos, sin)
            k = rope(k, cos, sin)
            logits = jnp.einsum('bhld,hdr->bhlr', v, router_w)
            scores = jax.nn.softmax(logits, axis=-1)
            idx = jnp.argmax(scores, axis=-1)
            onehot = jnp.arange(RATIO) == idx[..., None]
            masked_scores = jnp.where(onehot, scores, 0.0)
            masked_indices = onehot.astype(q.dtype)
            sum_indices = jnp.cumsum(masked_indices, axis=2)
            norm_score = jnp.where(sum_indices == 0, 0.0, 1.0 / sum_indices)[..., None]
            q_exp = q[:, :, :, None, :] * masked_scores[..., None] * norm_score
            k_exp = k[:, :, :, None, :] * masked_indices[..., None]
            q_exp = q_exp.reshape(b, H, l, RATIO * HDK)
            k_exp = k_exp.reshape(b, H, l, RATIO * HDK)
            qk = jnp.einsum('bhld,bhmd->bhlm', q_exp, k_exp) * HDK ** (-0.5)
            causal = jnp.tril(jnp.ones((l, l), qk.dtype))
            qk = qk * causal
            o = jnp.einsum('bhlm,bhmd->bhld', qk, v)
            o = o.transpose(0, 2, 1, 3)
            mu = jnp.mean(o, axis=-1, keepdims=True)
            var = jnp.var(o, axis=-1, keepdims=True)
            o = (o - mu) * jax.lax.rsqrt(var + EPS)
            o = jax.nn.silu(g) * o.reshape(b, l, d)
            o = o @ Wout
            attn_out = jnp.transpose(o, (1, 0, 2)) + residual
            h2 = layernorm(attn_out, ln2_w, ln2_b)
            mlp_out = jax.nn.silu(h2 @ w1) * (h2 @ w3) @ w2
            return mlp_out + attn_out
        del attention_mask
        return _forward(x, ln1_w, ln1_b, ln2_w, ln2_b, conv_w, Wq, Wk, Wv, Wg, Wout, router_w, w1, w3, w2)

    def _L1_ffn_ref(x, router_w, w1, w2):
        import jax, jax.numpy as jnp
        import numpy as np
        N_EXPERTS = 8
        TOP_K = 2
        B, T, C = x.shape
        E = N_EXPERTS
        xf = x.reshape(-1, C)
        logits = jnp.einsum('nc,ec->ne', xf, router_w)
        probs = jax.nn.softmax(logits, axis=-1)
        top_w, top_i = jax.lax.top_k(probs, TOP_K)
        top_w = top_w / jnp.sum(top_w, axis=-1, keepdims=True)
        comb = jnp.einsum('nk,nke->ne', top_w, jax.nn.one_hot(top_i, E, dtype=xf.dtype))
        h = jax.nn.gelu(jnp.einsum('nc,ech->enh', xf, w1), approximate=False)
        y = jnp.einsum('enh,ehc->enc', h, w2)
        out = jnp.einsum('ne,enc->nc', comb, y)
        return out.reshape(B, T, C)
    x = x + _L0_xattn_ref(ctx_1024, ctx_1024, _layernorm(x, axis=-1), mask_BxS2_if0, L0_xattn_Wk, L0_xattn_bk, L0_xattn_Wv, L0_xattn_bv, L0_xattn_Wq, L0_xattn_bq, L0_xattn_Woff, L0_xattn_boff, L0_xattn_Wo, L0_xattn_bo)
    x = x + _L0_attn_ref(_layernorm(x, axis=-1), L0_attn_Wq, L0_attn_Wk, L0_attn_Wv, L0_attn_Wo, L0_attn_gn_weight, L0_attn_gn_bias)
    x = x + _L0_ffn_ref(_layernorm(x, axis=-1), L0_ffn_Wg, L0_ffn_W1, L0_ffn_b1, L0_ffn_Wo, L0_ffn_bo)
    x = x + _L1_xattn_ref(_layernorm(x, axis=-1), ctx_1024, ctx_1024, mask_1x1xSxS2_ik0, L1_xattn_Wq, L1_xattn_bq, L1_xattn_Wk, L1_xattn_bk, L1_xattn_Wv, L1_xattn_bv, L1_xattn_Wo, L1_xattn_bo)
    x = x + _L1_attn_ref(_layernorm(x, axis=-1), L1_attn_attention_mask, L1_attn_ln1_w, L1_attn_ln1_b, L1_attn_ln2_w, L1_attn_ln2_b, L1_attn_conv_w, L1_attn_Wq, L1_attn_Wk, L1_attn_Wv, L1_attn_Wg, L1_attn_Wout, L1_attn_router_w, L1_attn_w1, L1_attn_w3, L1_attn_w2)
    x = x + _L1_ffn_ref(_layernorm(x, axis=-1), L1_ffn_router_w, L1_ffn_w1, L1_ffn_w2)
    return x

_drawn_inputs = setup_inputs


def setup_inputs(seed=0):
    import zlib

    import numpy as np

    out = dict(_drawn_inputs(seed))
    spreads = {'L0_xattn_bk': (0.0, 0.8),
     'L0_xattn_bv': (0.0, 0.294),
     'L0_xattn_bq': (0.0, 0.8),
     'L0_xattn_boff': (0.0, 0.669),
     'L0_xattn_bo': (0.0, 0.1),
     'L0_attn_gn_weight': (1.0, 0.2),
     'L0_attn_gn_bias': (0.0, 0.1),
     'L1_attn_ln1_w': (1.0, 0.2),
     'L1_attn_ln1_b': (0.0, 0.1),
     'L1_attn_ln2_w': (1.0, 0.2),
     'L1_attn_ln2_b': (0.0, 0.1)}
    factors = {'L0_xattn_Wk': 8.0,
     'L0_xattn_Wq': 8.0,
     'L0_xattn_Woff': 7.117,
     'L0_ffn_b1': 8.0,
     'L1_xattn_bk': 8.0}
    for name, (base, spread) in spreads.items():
        noise = np.random.default_rng([zlib.crc32(name.encode()), seed]).standard_normal(out[name].shape)
        drawn = base * np.exp(spread * noise) if base else spread * noise
        out[name] = jnp.asarray(drawn.astype(out[name].dtype))
    for name, factor in factors.items():
        out[name] = (out[name] * factor).astype(out[name].dtype)
    return out
```

```python
from contextlib import ExitStack

import concourse.bass as bass
import numpy as np
from concourse import mybir

F32 = mybir.dt.float32
BF16 = mybir.dt.bfloat16
I32 = mybir.dt.int32
ALU = mybir.AluOpType
ACT = mybir.ActivationFunctionType
AX = mybir.AxisListType
RMAX = bass.bass_isa.ReduceOp.max

P = 128
B = 4
D = 128
S2 = 2048
H = 16
HD = D // H
NK = 5
E1 = H * NK
QH = 64
NE = 8
HID0 = 256
HID1 = 512
FF = 352
FFT = [(0, 128), (128, 128), (256, 96)]
EPS = 1e-5
NEG = -1e9
KEPT = 3e38
TOK = B * P
BACK_AT = (9, 12, 15, 18)
LN_A, LN_B, LN_C, LN_D, LN_E0, LN_E1, LN_E2, LN_F = range(8)


def bf16_bits(a):
    return (np.ascontiguousarray(a).view(np.uint32) >> 16).astype(np.uint16)


def constants():
    c = {}
    c["c_ident"] = np.eye(P, dtype=np.float32)
    m = np.arange(P)
    coord = np.stack([np.where(m < 32, m - 33, m - 32), m + 32])
    sel = np.zeros((99, 32, P), np.float32)
    for i in range(32):
        sel[[i, 32 + i, 64 + i], i, :] = 1.0
    sel[96:98] = -coord[:, None, :]
    sel[98] = -0.5
    half = np.zeros((3, 3, B, 2, QH), np.float32)
    half[0, :, :, 0] = half[1, :, :, 1] = half[2] = 1.0
    c["c_sel"] = bf16_bits(sel)
    c["c_half"] = bf16_bits(half.reshape(3, 3, TOK))
    e = 32 * np.arange(3)[None, :] + (np.arange(96) % 32)[:, None]
    c["c_ref"] = np.where(e < E1, e % NK - 3, 0).astype(np.float32)
    q = np.arange(TOK) % P
    c["c_loc"] = np.ascontiguousarray(np.broadcast_to(q, (96, TOK))).astype(np.float32)
    c["c_mid"] = np.ascontiguousarray(np.broadcast_to(q // QH * QH + 31.5, (96, TOK))).astype(np.float32)
    inv = 1.0 / 10000.0 ** (np.arange(0, HD, 2, dtype=np.float32) / np.float32(HD))
    fr = np.arange(P, dtype=np.float32)[:, None] * inv[None, :].astype(np.float32)
    emb = np.concatenate([fr, fr], 1).astype(np.float32)
    cos, sin = np.cos(emb), np.sin(emb) * np.where(np.arange(HD) < HD // 2, -1, 1)
    cosT, sinT = np.tile(cos.T, (H, 1)), np.tile(sin.T, (H, 1))
    sc = 1.0 / np.sqrt(HD)
    c["c_rope0"] = np.stack([cosT * sc, sinT * sc, cosT, sinT], 1).astype(np.float32)
    gam = 1.0 - 2.0 ** (-5.0 - np.arange(H, dtype=np.float32))
    dist = np.arange(P)[None, :] - np.arange(P)[:, None]
    dec = np.where(dist[:, None] >= 0, gam[None, :, None].astype(np.float64) ** np.maximum(dist, 0)[:, None], 0.0)
    c["c_decay"] = dec.astype(np.float32)
    c["c_pos"] = -(P * np.arange(S2 // P)[None, :] + np.arange(P)[:, None]).astype(np.float32)
    c["c_head16"] = (np.arange(P)[:, None] // HD == np.arange(H)[None, :]).astype(np.float32)
    c["c_head"] = (np.arange(P)[:, None] // HD % 4 == np.arange(4)[None, :]).astype(np.float32)
    g = np.kron(np.eye(H), np.full((HD, HD), 1.0 / HD))
    c["c_group"] = np.stack([np.eye(P) - g, g], 1).astype(np.float32)
    hdk = 4
    inv = 1.0 / 10000.0 ** (np.arange(0, 2, dtype=np.float32) * 2.0 / hdk)
    fr = np.arange(B, dtype=np.float32)[:, None] * inv[None, :].astype(np.float32)
    t = np.zeros((2, B, 2, H, 2, 2), np.float32)
    t[0] = np.cos(fr)[:, None, None, None, :]
    t[1, ..., 0, :] = -np.sin(fr)[:, None, None, :]
    t[1, ..., 1, :] = np.sin(fr)[:, None, None, :]
    t[:, :, 0] *= hdk ** -0.5
    causal = np.broadcast_to((np.arange(B)[:, None] >= np.arange(B)[None, :])[:, :, None], (B, B, H))
    tri = np.arange(NE)[:, None] > np.arange(NE)[None, :]
    c["c_rows"] = np.concatenate([t.reshape(-1), causal.reshape(-1), tri.reshape(-1)]).astype(np.float32)[None]
    return c


ROWS = {}
_at = 0
for _n, _w in (("bkv", 256), ("bq", D), ("bo", D), ("ff_bo", D), ("x_bv", D), ("x_bo", D), ("ln1_w", D),
               ("ln1_b", D), ("ln2_w", D), ("ln2_b", D), ("conv0", D), ("conv1", D), ("rw", 2 * D)):
    ROWS[_n] = slice(_at, _at + _w)
    _at += _w
NROWS = _at
ROPE1 = slice(0, 1024)
CAUSAL1 = slice(1024, 1280)
BEFORE = slice(1280, 1344)
COLS = {n: i for i, n in enumerate(
    ["bq", "gn_w", "gn_b", "x_bq", "x_bk", "eps", "mhalf", "ff_bo"])}
B1COL = len(COLS)
NCOLS = B1COL + NE * 4


def layouts(i):
    f = lambda n: np.asarray(i[n])
    a = {}
    a["x"] = f("x").transpose(1, 0, 2)
    ctxT = f("ctx_1024").transpose(2, 0, 1)
    a["ctxT"] = ctxT
    a["mask_b"] = f("mask_BxS2_if0").astype(np.int32)
    a["mask_q"] = f("mask_1x1xSxS2_ik0")[0, 0].astype(np.int32)
    wk = f("L0_xattn_Wk").T.reshape(D, H, 1, HD)
    wv = f("L0_xattn_Wv").T.reshape(D, H, 1, HD)
    wkv = np.concatenate([wk, wv], 2).reshape(D, 2 * D)
    woff = np.concatenate([f("L0_xattn_Woff").T, np.zeros((D, 16), np.float32)], 1).reshape(D, 3, 1, 32)
    woff = np.broadcast_to(woff, (D, 3, 3, 32)).reshape(D, 288)
    a["w_a"] = np.concatenate([wkv, f("L0_xattn_Wq").T, woff, f("L0_xattn_Wo").T], 1)
    boff = np.concatenate([f("L0_xattn_boff"), np.zeros(16, np.float32)]).reshape(3, 1, 32)
    a["boff"] = np.broadcast_to(boff, (3, 3, 32)).reshape(3, 96).T
    rot = lambda w: w.T.reshape(D, H, 2, HD // 2)[:, :, ::-1].reshape(D, D)
    a["w_b"] = np.concatenate([f("L0_attn_Wq").T, rot(f("L0_attn_Wq")), f("L0_attn_Wk").T, rot(f("L0_attn_Wk")),
                               f("L0_attn_Wv").T, f("L0_attn_Wo").T], 1)
    a["w_c"] = np.concatenate([f("L0_ffn_Wg").T, f("L0_ffn_Wo").T.reshape(2, P, D).transpose(1, 0, 2).reshape(P, 2 * D)], 1)
    a["w_c1"] = f("L0_ffn_W1").transpose(2, 0, 1).reshape(D, NE * 2 * HID0)
    a["w_d"] = np.concatenate([f("L1_xattn_W" + n).T for n in "kvqo"], 1)
    a["w_e"] = np.concatenate([f("L1_attn_W" + n) for n in ("q", "k", "v", "g", "out")] + [f("L1_attn_w1"), f("L1_attn_w3")], 1)
    w2 = np.concatenate([f("L1_attn_w2"), np.zeros((3 * P - FF, D), np.float32)]).reshape(3, P, D)
    a["w_e2"] = w2.transpose(1, 0, 2)
    a["w_f"] = f("L1_ffn_router_w").T
    a["w_f1"] = f("L1_ffn_w1").transpose(1, 0, 2).reshape(D, NE * HID1)
    a["w_f2"] = f("L1_ffn_w2").reshape(NE, 4, P, D).transpose(2, 0, 1, 3).reshape(P, NE * 4 * D)
    bkv = np.concatenate([f("L0_xattn_bk").reshape(H, 1, HD), f("L0_xattn_bv").reshape(H, 1, HD)], 1)
    cw = f("L1_attn_conv_w").T
    a["rows"] = np.concatenate([bkv.reshape(-1), f("L0_xattn_bq"), f("L0_xattn_bo"), f("L0_ffn_bo"), f("L1_xattn_bv"), f("L1_xattn_bo"),
                                f("L1_attn_ln1_w"), f("L1_attn_ln1_b"), f("L1_attn_ln2_w"), f("L1_attn_ln2_b"),
                                cw[0], cw[1], f("L1_attn_router_w").transpose(2, 0, 1).reshape(-1)])[None]
    cols = [f("L0_xattn_bq"), f("L0_attn_gn_weight"), f("L0_attn_gn_bias"), f("L1_xattn_bq"), f("L1_xattn_bk"),
            np.full(D, EPS, np.float32), np.full(D, -0.5, np.float32), f("L0_ffn_bo")]
    a["cols"] = np.concatenate([np.stack(cols, 1), f("L0_ffn_b1").reshape(NE * 4, P).T], 1)
    a.update(constants())
    return {k: np.ascontiguousarray(v) for k, v in a.items()}


def program(nc, t, out, stages="ABCDEF", general=False):
    ctx = ExitStack()
    with ctx:
        def sb(name, shape, dt=F32):
            return ctx.enter_context(nc.sbuf_tensor(name, shape, dt))

        def sem(name):
            return ctx.enter_context(nc.semaphore(name))

        FLA = sb("FLA", [P, 2])
        FLD = sb("FLD", [P, 2])
        GNA = sb("GNA", [P, 2])
        FAI = sb("FAI", [1, 1], I32)
        FDI = sb("FDI", [1, 1], I32)
        VM3 = sb("VM3", [96, 3])
        MKB = sb("MKB", [P, B, S2 // P], I32)
        pos = sb("pos_sb", [P, S2 // P])
        head16 = sb("head16_sb", [P, H])
        X = sb("X", [P, B, D])
        XH = sb("XH", [P, B, D])
        XT = sb("XT", [P, TOK])
        XB = sb("XB", [P, B, D])
        STAT = sb("STAT", [P, B, 6])
        MV = sb("MV", [P, B, 2])
        VE = sb("VE", [P, B])
        RSTD = sb("RSTD", [P, B])
        MHALF = sb("MHALF", [P, B])
        ident = sb("ident", [P, P])
        rows = sb("rows_sb", [P, NROWS])
        crows = sb("crows_sb", [P, 1344])
        cols = sb("cols_sb", [P, NCOLS])
        head = sb("head_sb", [P, 4])
        row = lambda n: rows[:, ROWS[n]]
        col = lambda n: cols[:, COLS[n]:COLS[n] + 1]
        w_a = sb("w_a_sb", [P, 256 + D + 288 + D])
        w_b = sb("w_b_sb", [P, 6 * D])
        w_c = sb("w_c_sb", [P, 8 + 2 * D])
        w_d = sb("w_d_sb", [P, 4 * D])
        w_e = sb("w_e_sb", [P, 512 + 2 * FF])
        w_e2 = sb("w_e2_sb", [P, 3, D])
        w_f = sb("w_f_sb", [P, 8])
        def room(tile, width):
            at = [0]

            def take(shape):
                n = int(np.prod(shape[1:]))
                v = tile[:, at[0]:at[0] + n]
                at[0] += n
                assert at[0] <= width
                names = "abcd"[:len(shape) - 1]
                return v.rearrange(f"p ({' '.join(names)}) -> p {' '.join(names)}", **dict(zip(names, shape[1:])))

            return take

        SCR = sb("SCR", [P, 5120])
        before_b = room(SCR, 5120)
        KVW = sb("KVW", [P, 2 * B, 2 * D + 16])
        boff = sb("boff_sb", [96, 3])
        refc = sb("refc", [96, 3])
        ybias = sb("ybias", [96, 3])
        loc = before_b([P, TOK])[0:96]
        mid = before_b([P, TOK])[0:96]
        QpT = before_b([P, TOK])
        Qq = before_b([P, B, D])
        Y = before_b([P, 3, TOK])[0:96]
        YW = before_b([P, TOK])[0:96]
        IX = before_b([P, TOK])[0:96]
        Rm = before_b([P, TOK])[0:96]
        Rh = sb("Rh", [96, TOK], BF16)
        R = sb("R", [99, 3, TOK], BF16)
        SELR = sb("SELR", [P, 2048])
        SEL = SELR[:, :].bitcast(BF16)[0:99].rearrange("p (e m) -> p e m", e=32)
        after_sel = room(SELR, 2048)
        WT = sb("WT", [P, 2, 4, 2 * B, NK, QH])
        KEEP = sb("KEEP", [P, 5120])

        WTF = WT[:, :, :, :, :, :].rearrange("p a h i k q -> p (a h i k q)")
        first = room(WTF, 20480)
        WIN = first([P, B, 192])
        TAIL = first([P, B, P])
        MKF = first([P, S2]).bitcast(I32)
        ga = room(WTF, 20480)
        GCH = ga([P, P])
        GKV = ga([P, 2 * D + 16])
        GW = ga([P, 4, NK, P])
        GIX = ga([P, 3, TOK])[0:96]
        GT1 = ga([P, 3, TOK])[0:96]
        GSM = ga([P, 4, B])
        GPOS = ga([P, 1])
        gd = room(WTF, 12288)
        GK = gd([P, S2])
        GV = gd([P, S2 // P, D])
        GSC = gd([P, S2])
        GP = gd([P, S2 // P, P])
        GM = gd([P, S2])
        GMI = GM.bitcast(I32)
        GC = gd([P, P])
        GQ = gd([P, P])
        GO = gd([P, D])
        GR = gd([P, 4])
        later = room(WTF, 20480)
        PT = later([P, 2, H, P])
        keep = room(KEEP, 5120)
        after = room(KEEP, 5120)
        w_c1 = later([P, NE * 2 * HID0])
        after_c = room(w_c1, 4096)
        after_a = room(SCR, 5120)
        GT = later([P, 2, 4, TOK])
        w_f1 = later([P, NE * HID1])
        w_f2 = later([P, NE * 4 * D])
        SK = keep([P, B, NK, P])
        PRD = sb("PRD", [P, NK, 4, HD])
        SCO = sb("SCO", [P, B, H, NK])
        GSK = SK.rearrange("p b k q -> p b (k q)")
        VS = keep([P, B, H, NK * HD]).rearrange("p b h (k d) -> p b h k d", k=NK)
        PV = WTF[:, 0:B * H * NK * HD].rearrange("p (b h k d) -> p b h k d", b=B, h=H, k=NK)
        SM1 = sb("SM1", [P, B, H])
        SM2 = sb("SM2", [P, B, H])
        CT = sb("CT", [P, B, D])
        CTT = sb("CTT", [P, TOK])
        rope0 = sb("rope0", [P, 4, P])
        group = sb("group_sb", [P, 2, P])
        decay = sb("decay", [P, H, P])
        T0 = after([P, B, P])
        T1 = after([P, B, P])
        qT = after([P, B, P])
        kT = after([P, B, P])
        vq = after([P, B, P])
        BLK = after([P, 2, 4, P])
        OM = after([P, 4, P])
        PR = sb("PR", [P, B, NE])
        EX = sb("EX", [P, B, NE])
        CMP = after_sel([P, B, NE, NE])
        CMQ = after_sel([P, B, NE, NE])
        RK = sb("RK", [P, B, NE])
        S1 = sb("S1", [P, B])
        CW = sb("CW", [P, B, NE])
        CWT = after_a([P, TOK])[0:NE]
        CB = after_sel([P, 2, TOK])
        SG = room(KVW[:, :, :].rearrange("p i n -> p (i n)"), 2176)([P, 2, 2, TOK])
        PO = SG.rearrange("p a j n -> p (a j n)").rearrange("p (l m n) -> p l m n", l=B, m=B)
        YE = after_a([P, 2, TOK])
        ACC = after_sel([P, TOK])
        mtail = sb("mtail", [P, P], I32)
        MB = sb("MB", [P, P])
        kTd = sb("kTd", [P, B, P])
        vd = sb("vd", [P, B, P])
        SS = GT.rearrange("p a j n -> p (a j n)").rearrange("p (a h k) -> p a h k", a=2, h=H)
        MX = sb("MX", [P, B, H])
        ones = sb("ones", [P, P])
        DN = after([P, 4, P])
        XN = after_c([P, B, D])
        HH = after_c([P, B, D])
        HP = after_c([P, B, D])
        QK = after_a([P, B, 2, 64])
        QR = after_a([P, B, 2, 64])
        Q2 = after_a([P, B, 2, 64])
        VV = after_c([P, B, D])
        GS = after_c([P, B, D])
        LGT = sb("LGT", [P, 2, B, H])
        LGE = sb("LGE", [P, 2, B, H])
        LP = after_a([P, 2, B, D])
        OH = sb("OH", [P, B, H])
        SMM = after_a([P, B, B, H])
        DT = after_a([P, B, B, H])
        PDT = LP.rearrange("p r b n -> p (r b n)").rearrange("p (l m n) -> p l m n", l=B, m=B)
        OO = after_c([P, B, D])
        OQ = after_c([P, B, D])
        HF = room(decay[:, :, :].rearrange("p h t -> p (h t)"), 2048)([P, 3, TOK])

        BK = ctx.enter_context(nc.psum_tensor("BK", [P, 8, 512], F32))
        bank = lambda i: BK[:, i, :]

        loads = {n: sem("in_" + n) for n in (
            "x", "ident", "rows", "crows", "cols", "w_a", "win", "tail", "pos", "sel", "w_b", "w_c",
            "w_c1", "w_d", "w_e", "w_f1", "w_f2", "decay", "flags")}
        dve_chain = sem("dve_chain")
        act_chain = sem("act_chain")
        pool_chain = sem("pool_chain")
        ln_var, ln_rstd, ln_xhat = sem("ln_var"), sem("ln_rstd"), sem("ln_xhat")
        ln_xT_ps, ln_xT = sem("ln_xT_ps"), sem("ln_xT")
        consts_ready = sem("consts_ready")
        kvw_ps, kvw_ready = sem("kvw_ps"), sem("kvw_ready")
        kd_ps, kd_ready, vd_ready = sem("kd_ps"), sem("kd_ready"), sem("vd_ready")
        a_q_ps, a_qT, a_qq, a_off_ps, a_y, a_r = (sem("a_" + n) for n in ("q_ps", "qT", "qq", "off_ps", "y", "r"))
        a_ix_ps, a_abs, a_w = sem("a_ix_ps"), sem("a_abs"), sem("a_w")
        a_samp_ps, a_sk, a_tr_ps, a_prod, a_vs = (sem("a_" + n) for n in ("samp_ps", "sk", "tr_ps", "prod", "vs"))
        a_z, a_exp = sem("a_z"), sem("a_exp")
        ctx_ready, ctxT_ps, ctxT_ready, proj_ps = (sem(n) for n in ("ctx_ready", "ctxT_ps", "ctxT_ready", "proj_ps"))
        xb_ready, x_ready = sem("xb_ready"), sem("x_ready")
        b_qk_ps, b_v_ps, b_rot, b_v = (sem("b_" + n) for n in ("qk_ps", "v_ps", "rot", "v"))
        b_blk, b_s_ps, b_pt, b_o_ps, b_oT, b_oc_ps = (sem("b_" + n) for n in ("blk", "s_ps", "pt", "o_ps", "oT", "oc_ps"))
        b_sq, b_var_ps, b_std, b_on = (sem("b_" + n) for n in ("sq", "var_ps", "std", "on"))
        r_lg_ps, r_z, r_exp, r_cw, r_cwT_ps, r_cwT, r_cb_ps, r_cb = (
            sem("r_" + n) for n in ("lg_ps", "z", "exp", "cw", "cwT_ps", "cwT", "cb_ps", "cb"))
        e_h_ps, e_act, e_g, e_y_ps, e_ys, e_acc, e_accT_ps = (
            sem("e_" + n) for n in ("h_ps", "act", "g", "y_ps", "ys", "acc", "accT_ps"))
        d_mb, d_q_ps, d_q, d_blk, d_s_ps, d_ss, d_mx, d_sub, d_exp = (
            sem("d_" + n) for n in ("mb", "q_ps", "q", "blk", "s_ps", "ss", "mx", "sub", "exp"))
        d_pT_ps, d_pT, d_o_ps, d_om = (sem("d_" + n) for n in ("pT_ps", "pT", "o_ps", "om"))
        l_hc, l_silu, l_hT_ps, l_hT, l_qkv_ps, l_vkqg = (
            sem("l_" + n) for n in ("hc", "silu", "hT_ps", "hT", "qkv_ps", "vkqg"))
        l_ld, l_le, l_oc, l_sq, l_vs, l_std, l_h2, l_ff_ps, l_ffs, l_ff, l_xa = (
            sem("l_" + n) for n in ("ld", "le", "oc", "sq", "vs", "std", "h2", "ff_ps", "ffs", "ff", "xa"))
        l_hp, l_h1 = sem("l_hp"), sem("l_h1")
        flag_rows, flag_all, flag_a, flag_d = (sem("flag_" + n) for n in ("rows", "all", "a", "d"))
        ga_chain = sem("ga_chain")
        ga_in, ga_sum_ps, ga_pos, ga_ix, ga_abs, ga_w, ga_kv_ps, ga_kv = (
            sem("ga_" + n) for n in ("in", "sum_ps", "pos", "ix", "abs", "w", "kv_ps", "kv"))
        ga_samp, ga_add, ga_zero, ga_tr, ga_prod, ga_out = (
            sem("ga_" + n) for n in ("samp", "add", "zero", "tr", "prod", "out"))
        gd_in, gd_mask, gd_m0, gd_kv_ps, gd_k, gd_v = (sem("gd_" + n) for n in ("in", "mask", "m0", "kv_ps", "k", "v"))
        gd_q, gd_s_ps, gd_chain, gd_neg, gd_exp, gd_tr, gd_p, gd_o_ps, gd_o, gd_oT_ps, gd_oT = (
            sem("gd_" + n) for n in ("q", "s_ps", "chain", "neg", "exp", "tr", "p", "o_ps", "o", "oT_ps", "oT"))
        stored = sem("stored")

        PROJ = [s for s in "ABDE" if s in stages]
        BIASED = [s for s in "ADE" if s in stages]
        FFNS = [s for s in "CF" if s in stages]
        CTXT = [s for s in "AE" if s in stages]
        nx = {s: i for i, s in enumerate(stages)}

        block = ctx.enter_context(nc.Block())

        def flagged(eng, ready, tile):
            eng.wait_ge(ready, 1)
            return eng.value_load(tile[0:1, 0:1]) != 0

        lns = [n for n, q in enumerate("ABCDEEEF") if q in stages]
        transposed = [n for n in lns if n not in (LN_E0, LN_E1)]
        xhat_count = lambda n: 4 * lns.index(n) + 4
        xT_count = lambda n: transposed.index(n) + 1

        def vcopy(act, u):
            G, b = u // 4, u % 4
            act.wait_ge(a_prod, u + 1)
            src = BK[:, 5:7, :].rearrange("p a n -> p (a n)")[:, 0:NK * P].rearrange("p (k h r) -> p h k r", k=NK, h=4)
            act.activation(VS[:, b, 4 * G:4 * G + 4, :, :], src[:, :, :, HD:2 * HD], ACT.Copy).then_inc(a_vs, 1)

        def weigh(dve, s, k, e):
            n = k * NE + e
            dve.wait_ge(e_y_ps, n + 1)
            dve.wait_ge(r_cb, n + 1)
            if n >= 2:
                dve.wait_ge(e_acc, n - 1)
            if s == "C":
                dve.scalar_tensor_tensor(out=YE[:, e % 2, :], in0=bank(4 + e % 2), scalar=col("ff_bo"),
                                         in1=CB[:, e % 2, :], op0=ALU.add, op1=ALU.mult).then_inc(e_ys, 1)
            else:
                dve.tensor_tensor(YE[:, e % 2, :], bank(4 + e % 2), CB[:, e % 2, :], ALU.mult).then_inc(e_ys, 1)


        loaded = {'rows':16,'crows':16,'sel':32,'decay':48}
        @block.sync
        def _(sp):
            def load(dst, src, s):
                loaded[s] = loaded.get(s, 0) + 16
                sp.dma_start(dst, src).then_inc(loads[s], 16)

            load(X[:, :, :], t["x"], "x")
            load(ident[:, :], t["c_ident"], "ident")
            load(w_a[:, :], t["w_a"], "w_a")
            load(WIN[:, :, 0:32], t["ctxT"][:, :, S2 - 32:S2], "win")
            load(WIN[:, :, 32:192], t["ctxT"][:, :, 0:160], "win")
            load(cols[:, :], t["cols"], "cols")
            load(boff[:, :], t["boff"], "pos")
            load(refc[:, :], t["c_ref"], "pos")
            load(loc[:, :], t["c_loc"], "pos")
            load(mid[:, :], t["c_mid"], "pos")
            load(TAIL[:, :, :], t["ctxT"][:, :, S2 - P:S2], "tail")
            load(w_d[:, :], t["w_d"], "w_d")
            load(w_b[:, :], t["w_b"], "w_b")
            load(head[:, :], t["c_head"], "decay")
            load(MKB[:, :, :], t["mask_b"].rearrange("b (p j) -> p b j", p=P), "flags")
            load(MKF, t["mask_q"], "flags")
            load(pos[:, :], t["c_pos"], "flags")
            load(head16[:, :], t["c_head16"], "flags")
            load(mtail[:, :], t["mask_q"][:, S2 - P:S2], "flags")
            load(w_c[:, :], t["w_c"], "w_c")
            load(w_e[:, :], t["w_e"], "w_e")
            load(w_e2[:, :, :], t["w_e2"], "w_e")
            load(w_f[:, :], t["w_f"], "w_e")
            if "A" in stages:
                with sp.If(flagged(sp, flag_a, FAI)):
                    with sp.Fori(0, B) as b:
                        with sp.Fori(0, S2 // P) as c:
                            sp.wait_ge(ga_kv_ps, 1 + b * (S2 // P) + c)
                            sp.dma_start(GCH, t["ctxT"][:, bass.ds(b, 1), bass.ds(c * P, P)].rearrange("p b n -> p (b n)"))\
                              .then_inc(ga_in, 16)
                    sp.wait_ge(ga_out, 1 + 4 * B)
                sp.wait_ge(a_z, 1)
            else:
                sp.wait_ge(kd_ps, 2)
            sp.wait_ge(flag_d, 1)
            if "C" in stages:
                load(w_c1, t["w_c1"], "w_c1")
            if "F" in stages:
                load(w_f1, t["w_f1"], "w_f1")
                load(w_f2, t["w_f2"], "w_f2")
            if "D" in stages:
                with sp.If(flagged(sp, flag_d, FDI)):
                    sp.wait_ge(d_om, B)
                    sp.dma_start(GMI, t["mask_q"]).then_inc(gd_mask, 16)
                    with sp.Fori(0, B) as b:
                        with sp.Fori(0, S2 // P) as c:
                            sp.wait_ge(gd_kv_ps, 1 + b * (S2 // P) + c)
                            sp.dma_start(GC, t["ctxT"][:, bass.ds(b, 1), bass.ds(c * P, P)].rearrange("p b n -> p (b n)"))\
                              .then_inc(gd_in, 16)
            sp.wait_ge(x_ready, len(stages))
            sp.dma_start(out, X[:, :, :]).then_inc(stored, 16)
            sp.wait_ge(stored, 16)
            if len(stages) < 6:
                for q, v in loaded.items():
                    sp.wait_ge(loads[q], v)

        @block.gpsimd
        def _(pool):
            pool.memset(MHALF[:, :], -0.5).then_inc(consts_ready, 1)
            pool.memset(KVW[:, :, 2 * D:2 * D + 16], 0.0).then_inc(consts_ready, 1)
            pool.memset(ones[:, :], 1.0).then_inc(consts_ready, 1)
            pool.wait_ge(consts_ready, 3)

            def power(n):
                pool.wait_ge(ln_var, lns.index(n) + 1)
                pool.tensor_tensor(RSTD[:, :], VE[:, :], MHALF[:, :], ALU.pow).then_inc(ln_rstd, 1)

            def with_bias(n, name):
                pool.wait_ge(x_ready, n) if n else pool.wait_ge(loads["x"], 16)
                pool.wait_ge(loads["rows"], 16)
                pool.tensor_tensor(XB[:, :, :], X[:, :, :], row(name).unsqueeze(1).to_broadcast([P, B, D]),
                                   ALU.add).then_inc(xb_ready, 1)

            if stages[0] == "A":
                power(LN_A)
            pool.wait_ge(flag_rows, 1)
            pool.partition_all_reduce(FLD[:, 1:2], FLD[:, 0:1], P, RMAX).then_inc(flag_all, 1)
            for s in stages:
                if s == "A":
                    with_bias(nx[s], "bo")
                    pool.wait_ge(flag_rows, 2)
                    pool.partition_all_reduce(FLA[:, 1:2], FLA[:, 0:1], P, RMAX).then_inc(flag_all, 1)
                if s == "B":
                    power(LN_B)
                if s in "CF":
                    power(LN_C if s == "C" else LN_F)
                    k = FFNS.index(s)
                    for e in range(NE):
                        pool.wait_ge(e_ys, k * NE + e + 1)
                        if e:
                            pool.wait_ge(e_acc, k * NE + e)
                            pool.tensor_tensor(ACC[:, :], ACC[:, :], YE[:, e % 2, :], ALU.add).then_inc(e_acc, 1)
                        else:
                            pool.tensor_copy(ACC[:, :], YE[:, 0, :]).then_inc(e_acc, 1)
                if s == "D":
                    power(LN_D)
                    with_bias(nx[s], "x_bo")
                    for b in range(B):
                        pool.wait_ge(d_mx, b + 1)
                        ss = SS[:, b % 2]
                        pool.tensor_tensor(ss, ss, MX[:, b].unsqueeze(2).to_broadcast([P, H, P]),
                                           ALU.subtract).then_inc(d_sub, 1)
                if s == "E":
                    power(LN_E0)
                    power(LN_E1)
                    pool.wait_ge(l_h1, 1)
                    pool.tensor_tensor(HP[:, 0:3], HH[:, 0:3], row("conv0").unsqueeze(1).to_broadcast([P, 3, D]),
                                       ALU.mult).then_inc(l_hp, 1)
                    power(LN_E2)
                    pool.wait_ge(l_xa, 1)
                    pool.tensor_tensor(XB[:, :, :], X[:, :, :], CT[:, :, :], ALU.add).then_inc(xb_ready, 1)

        @block.scalar
        def _(act):
            chain = [0]

            def settle(ins):
                chain[0] += 1
                ins.then_inc(act_chain, 1)
                act.wait_ge(act_chain, chain[0])

            def load(dst, src, s):
                act.dma_start(dst, src).then_inc(loads[s], 16)

            load(SEL[:, :, :], t["c_sel"].bitcast(BF16), "sel")
            load(R[96:99, :, :], t["c_half"].bitcast(BF16), "sel")
            load(rows[:, :], t["rows"].to_broadcast([P, NROWS]), "rows")
            load(rope0[:, :, :], t["c_rope0"], "decay")
            load(group[:, :, :], t["c_group"], "decay")
            load(decay[:, :, :], t["c_decay"], "decay")
            load(crows[:, :], t["c_rows"].to_broadcast([P, 1344]), "crows")

            def norm_T(n, bk):
                act.wait_ge(ln_xT_ps, xT_count(n))
                act.activation(XT[:, :], bank(bk), ACT.Copy).then_inc(ln_xT, 1)

            def ctx_T(s, bk):
                k = CTXT.index(s)
                act.wait_ge(ctxT_ps, k + 1)
                act.activation(CTT[:, :], bank(bk), ACT.Copy).then_inc(ctxT_ready, 1)

            act.wait_ge(kd_ps, 1)
            act.wait_ge(loads["cols"], 16)
            act.activation(kTd[:, :, :], bank(4), ACT.Identity, bias=col("x_bk")).then_inc(kd_ready, 1)

            for s in stages:
                if s == "A":
                    norm_T(LN_A, 5)
                    act.wait_ge(a_q_ps, 1)
                    act.activation(QpT[:, :], bank(6), ACT.Identity, bias=col("bq")).then_inc(a_qT, 1)
                    for e in range(E1):
                        G = e // 20
                        act.wait_ge(a_ix_ps, e + 1)
                        if G >= 2 and e % 20 == 0:
                            act.wait_ge(a_samp_ps, 8 * (G - 1))
                        act.activation(WT[:, G % 2, e % 20 // NK, :, e % NK, :], bank(e % 3), ACT.Abs)\
                           .then_inc(a_abs, 1)
                        if G and e % 20 - 1 in BACK_AT:
                            vcopy(act, 4 * (G - 1) + BACK_AT.index(e % 20 - 1))
                    for u in range(12, 16):
                        vcopy(act, u)
                    with act.If(flagged(act, flag_a, FAI)):
                        act.sem_inc(ga_abs, 1)
                        act.wait_ge(ga_pos, 1)
                        with act.Fori(0, B) as b:
                            with act.Fori(0, S2 // P) as c:
                                it = b * (S2 // P) + c
                                act.wait_ge(ga_kv, 1 + 2 * it + 2)
                                for e in range(E1):
                                    if e % 20 == 0:
                                        act.wait_ge(ga_samp, 1 + it * 4 + e // 20)
                                    act.wait_ge(ga_ix, it * E1 + e + 1)
                                    act.activation(GW[:, e % 20 // NK, e % NK, :], BK[:, 0, 0:P], ACT.Abs,
                                                   bias=GPOS).then_inc(ga_abs, 1)
                    act.wait_ge(a_z, 1)
                    act.activation(SCO[:, :, :, :], SCO[:, :, :, :], ACT.Exp).then_inc(a_exp, 1)
                    ctx_T("A", 6)
                if s == "B":
                    norm_T(LN_B, 7)
                    act.wait_ge(b_v_ps, 1)
                    act.activation(vq[:, :, :], bank(4), ACT.Copy).then_inc(b_v, 1)
                    act.wait_ge(b_oc_ps, 1)
                    act.activation(T0[:, :, :], bank(4), ACT.Square).then_inc(b_sq, 1)
                    act.wait_ge(b_var_ps, 1)
                    act.activation(T1[:, :, :], bank(5), ACT.Sqrt, bias=col("eps")).then_inc(b_std, 1)
                if s in "CF":
                    k = FFNS.index(s)
                    norm_T(LN_C if s == "C" else LN_F, 7)
                    act.wait_ge(r_z, k + 1)
                    act.activation(EX[:, :, :], EX[:, :, :], ACT.Exp).then_inc(r_exp, 1)
                    act.wait_ge(r_cwT_ps, k + 1)
                    act.activation(CWT[:, :], BK[0:NE, 6, :], ACT.Copy).then_inc(r_cwT, 1)

                    def cb_copy(e):
                        act.wait_ge(r_cb_ps, k * NE + e + 1)
                        if e >= 2:
                            act.wait_ge(e_ys, k * NE + e - 1)
                        act.activation(CB[:, e % 2, :], bank(6 + e % 2), ACT.Copy).then_inc(r_cb, 1)

                    cb_copy(0)
                    for e in range(NE):
                        n = k * NE + e
                        act.wait_ge(e_h_ps, n + 1)
                        if e >= 2:
                            act.wait_ge(e_g, n - 1) if s == "C" else act.wait_ge(e_y_ps, n - 1)
                        if s == "C":
                            for j in range(2):
                                bb = cols[:, B1COL + 4 * e + 2 + j:B1COL + 4 * e + 3 + j]
                                ins = act.activation(SG[:, e % 2, j, :], bank(2 + j), ACT.Sigmoid, bias=bb)
                        else:
                            for j in range(4):
                                ins = act.activation(GT[:, e % 2, j, :], bank(j), ACT.Gelu)
                        ins.then_inc(e_act, 1)
                        if e + 1 < NE:
                            cb_copy(e + 1)
                if s == "D":
                    norm_T(LN_D, 7)
                    act.wait_ge(d_q_ps, 1)
                    act.activation(qT[:, :, :], bank(6), ACT.Identity, bias=col("x_bq")).then_inc(d_q, 1)
                    for b in range(B):
                        act.wait_ge(d_sub, b + 1)
                        act.activation(SS[:, b % 2], SS[:, b % 2], ACT.Exp).then_inc(d_exp, 1)
                        for g in range(4):
                            n = 4 * b + g
                            act.wait_ge(d_pT_ps, n + 1)
                            if b >= 2 and g == 0:
                                act.wait_ge(d_o_ps, b - 1)
                            act.activation(PT[:, b % 2, 4 * g:4 * g + 4, :], bank(4 + n % 2), ACT.Copy)\
                               .then_inc(d_pT, 1)
                    with act.If(flagged(act, flag_d, FDI)):
                        act.sem_inc(gd_k, 1)
                        act.wait_ge(d_om, B)
                        with act.Fori(0, B) as b:
                            with act.Fori(0, S2 // P) as c:
                                it = b * (S2 // P) + c
                                act.wait_ge(gd_kv_ps, 1 + it + 1)
                                act.activation(GK[:, bass.ds(c * P, P)], BK[:, 0, 0:P], ACT.Identity, bias=col("x_bk"))\
                                   .then_inc(gd_k, 1)
                            with act.Fori(0, H) as h:
                                it = b * H + h
                                act.wait_ge(gd_neg, it + 1)
                                act.activation(GSC, GSC, ACT.Exp, bias=GR[:, 0:1], accum_out=GR[:, 1:2]).then_inc(gd_exp, 1)
                                for j in range(4):
                                    act.wait_ge(gd_tr, 4 * it + j + 1)
                                    act.activation(GP[:, 4 * j:4 * j + 4, :], bank(4 + j), ACT.Copy).then_inc(gd_p, 1)
                if s == "E":
                    act.wait_ge(l_hc, 1)
                    act.activation(HH[:, :, :], HH[:, :, :], ACT.Silu).then_inc(l_silu, 1)
                    act.wait_ge(l_hT_ps, 1)
                    act.activation(XT[:, :], bank(7), ACT.Copy).then_inc(l_hT, 1)
                    act.wait_ge(l_qkv_ps, 1)
                    qkvg = BK[:, 0:4, :]
                    act.activation(VV[:, :, :], qkvg[:, :, 128:256], ACT.Copy).then_inc(l_vkqg, 1)
                    act.activation(QK[:, :, 1, :], qkvg[:, :, 64:128], ACT.Copy).then_inc(l_vkqg, 1)
                    act.activation(QK[:, :, 0, :], qkvg[:, :, 0:64], ACT.Silu).then_inc(l_vkqg, 1)
                    act.activation(GS[:, :, :], qkvg[:, :, 256:384], ACT.Silu).then_inc(l_vkqg, 1)
                    act.wait_ge(l_ld, 1)
                    act.activation(LGE[:, :, :, :], LGT[:, :, :, :], ACT.Exp).then_inc(l_le, 1)
                    act.wait_ge(l_oc, 1)
                    act.activation(OQ[:, :, :], OO[:, :, :], ACT.Square).then_inc(l_sq, 1)
                    act.wait_ge(l_vs, 1)
                    act.activation(SM2[:, :, :], SM1[:, :, :], ACT.Sqrt, bias=col("eps"), scale=1.0 / HD)\
                       .then_inc(l_std, 1)
                    ctx_T("E", 7)
                    norm_T(LN_E2, 5)
                    for j, (o, w) in enumerate(FFT):
                        act.wait_ge(l_ff_ps, j + 1)
                        act.activation(HF[0:w, j, :], BK[0:w, j, :], ACT.Silu).then_inc(l_ffs, 1)

        @block.vector
        def _(dve):
            chain = [0]

            def settle(ins):
                chain[0] += 1
                ins.then_inc(dve_chain, 1)
                dve.wait_ge(dve_chain, chain[0])

            def stats(n, src):
                for b in range(B):
                    ins = dve.bn_stats(STAT[:, b, :], src[:, b, :])
                settle(ins)
                for b in range(B):
                    ins = dve.bn_aggr(MV[:, b, :], STAT[:, b, :])
                settle(ins)
                dve.tensor_scalar(VE[:, :], MV[:, :, 1], EPS, None, ALU.add).then_inc(ln_var, 1)

            def norm(n, src, dst, final=True):
                dve.wait_ge(ln_rstd, lns.index(n) + 1)
                for b in range(B):
                    ins = dve.tensor_scalar(dst[:, b, :], src[:, b, :], MV[:, b, 0:1], RSTD[:, b:b + 1],
                                            ALU.subtract, ALU.mult)
                    if final:
                        ins.then_inc(ln_xhat, 1)
                if final:
                    dve.wait_ge(ln_xhat, xhat_count(n))
                else:
                    settle(ins)

            def residual(s, other):
                k = PROJ.index(s)
                dve.wait_ge(proj_ps, k + 1)
                dve.tensor_tensor(X[:, :, :], bank(7), other, ALU.add).then_inc(x_ready, 1)
                dve.wait_ge(x_ready, nx[s] + 1)

            def over(ap, n, axis=1):
                v = ap.unsqueeze(axis)
                shape = list(v.shape)
                shape[axis] = n
                return v.to_broadcast(shape)

            dve.wait_ge(loads["x"], 16)
            if stages[0] == "A":
                stats(LN_A, X)
                norm(LN_A, X, XH)
            dve.wait_ge(loads["flags"], 80)
            settle(dve.tensor_reduce(GNA[:, 0:1], MKF[:, 0:S2 - P], AX.X, ALU.max, apply_absolute_value=True))
            settle(dve.tensor_reduce(GNA[:, 1:2], MKF[:, S2 - P:S2], AX.X, ALU.max, apply_absolute_value=True))
            settle(dve.tensor_scalar(GNA[:, 0:1], GNA[:, 0:1], 0.0, None, ALU.not_equal))
            settle(dve.tensor_scalar(GNA[:, 1:2], GNA[:, 1:2], 0.0, None, ALU.is_equal))
            dve.tensor_tensor(FLD[:, 0:1], GNA[:, 0:1], GNA[:, 1:2], ALU.max).then_inc(flag_rows, 1)
            dve.wait_ge(loads["rows"], 16)
            for j in range(4):
                dve.wait_ge(kvw_ps, j + 1)
                dve.tensor_tensor(KVW[:, 2 * j:2 * j + 2, 0:2 * D], bank(j).rearrange("p (a n) -> p a n", a=2),
                                  over(row("bkv"), 2), ALU.add).then_inc(kvw_ready, 1)
            dve.wait_ge(kd_ps, 2)
            dve.tensor_tensor(vd[:, :, :], bank(7).rearrange("p (b n) -> p b n", b=B), over(row("x_bv"), B),
                              ALU.add).then_inc(vd_ready, 1)
            dve.wait_ge(flag_all, 1)
            if general:
                dve.memset(FDI[:, :], 1).then_inc(flag_d, 1)
            else:
                dve.tensor_copy(FDI[:, :], FLD[0:1, 1:2]).then_inc(flag_d, 1)

            for s in stages:
                if s == "A":
                    dve.wait_ge(loads["pos"], 64)
                    settle(dve.tensor_tensor(ybias[:, :], boff[:, :], refc[:, :], ALU.add))
                    dve.wait_ge(a_q_ps, 2)
                    dve.tensor_tensor(Qq[:, :, :], bank(4).rearrange("p (b n) -> p b n", b=B), over(row("bq"), B),
                                      ALU.add).then_inc(a_qq, 1)
                    for g in range(3):
                        dve.wait_ge(a_off_ps, g + 1)
                        settle(dve.scalar_tensor_tensor(out=Y[:, g, :], in0=BK[0:96, g, :], scalar=ybias[:, g:g + 1],
                                                        in1=loc[:, :], op0=ALU.add, op1=ALU.add))
                        settle(dve.tensor_scalar(YW[:, :], Y[:, g, :], 0.0, -1.0, ALU.is_lt, ALU.mult))
                        settle(dve.scalar_tensor_tensor(out=IX[:, :], in0=Y[:, g, :], scalar=float(S2) / (S2 - 1),
                                                        in1=YW[:, :], op0=ALU.mult, op1=ALU.add))
                        if g == 0:
                            dve.wait_ge(loads["sel"], 32)
                        settle(dve.tensor_copy(R[0:96, g, :], IX[:, :]))
                        settle(dve.tensor_tensor(IX[:, :], IX[:, :], R[0:96, g, :], ALU.subtract))
                        settle(dve.tensor_copy(Rh[:, :], IX[:, :]))
                        settle(dve.tensor_tensor(Rm[:, :], IX[:, :], Rh[:, :], ALU.subtract))
                        dve.tensor_copy(R[32:64, g, :], Rh[32:64, :])
                        dve.tensor_copy(R[64:96, g, :], Rm[64:96, :]).then_inc(a_r, 1)
                    def reach(g):
                        settle(dve.tensor_tensor(YW[:, :], Y[:, g, :], mid[:, :], ALU.subtract))
                        settle(dve.tensor_reduce(VM3[:, g:g + 1], YW[:, :], AX.X, ALU.max, apply_absolute_value=True))

                    def uncovered():
                        settle(dve.tensor_reduce(FLA[:, 0:1], MKB[:, :, :], AX.XY, ALU.max, apply_absolute_value=True))
                        settle(dve.tensor_scalar(FLA[:, 0:1], FLA[:, 0:1], 0.0, None, ALU.not_equal))
                        settle(dve.tensor_reduce(GNA[0:96, 0:1], VM3[:, :], AX.X, ALU.max))
                        settle(dve.tensor_scalar(GNA[0:96, 0:1], GNA[0:96, 0:1], 62.5, None, ALU.is_gt))
                        dve.tensor_tensor(FLA[0:96, 0:1], FLA[0:96, 0:1], GNA[0:96, 0:1], ALU.max).then_inc(flag_rows, 1)

                    def evac(G, i):
                        n = 8 * G + i
                        dve.wait_ge(a_samp_ps, n + 1)
                        if G and i == 0:
                            dve.wait_ge(a_tr_ps, 4 * G)
                        b, hf = i // 2, i % 2
                        dve.tensor_copy(SK[:, b, :, QH * hf:QH * hf + QH],
                                        BK[:, 3 + n % 2, 0:NK * QH].rearrange("p (k q) -> p k q", k=NK))\
                           .then_inc(a_sk, 1)

                    def score(u):
                        G, b = u // 4, u % 4
                        dve.wait_ge(a_tr_ps, u + 1)
                        src = BK[:, 5:7, :].rearrange("p a n -> p (a n)")[:, 0:NK * P]
                        src = src.rearrange("p (k h r) -> p k h r", k=NK, h=4)[:, :, :, 0:HD]
                        qv = Qq[:, b, 32 * G:32 * G + 32].rearrange("p (h d) -> p h d", h=4)
                        if u == 0:
                            dve.wait_ge(a_qq, 1)
                        dve.tensor_tensor(PRD[:, :, :, :], src, over(qv, NK), ALU.mult).then_inc(a_prod, 1)
                        dve.wait_ge(a_prod, u + 1)
                        settle(dve.tensor_reduce(SCO[:, b, 4 * G:4 * G + 4, :], PRD[:, :, :, :].rearrange("p k h d -> p h k d"),
                                                 AX.X, ALU.add))

                    for e in range(E1):
                        G = e // 20
                        dve.wait_ge(a_abs, e + 1)
                        w = WT[:, G % 2, e % 20 // NK, :, e % NK, :]
                        dve.tensor_scalar(w, w, 1.0, -1.0, ALU.min, ALU.add).then_inc(a_w, 1)
                        if e in (4, 7, 10):
                            reach((4, 7, 10).index(e))
                        if e == 12:
                            uncovered()
                        if G and e % 20 < 8:
                            evac(G - 1, e % 20)
                        if G and e % 20 - 1 in BACK_AT:
                            score(4 * (G - 1) + BACK_AT.index(e % 20 - 1))
                    for i in range(8):
                        evac(3, i)
                    for u in range(12, 16):
                        score(u)
                    dve.wait_ge(flag_all, 2)
                    if general:
                        dve.memset(FAI[:, :], 1).then_inc(flag_a, 1)
                    else:
                        dve.tensor_copy(FAI[:, :], FLA[0:1, 1:2]).then_inc(flag_a, 1)
                    dve.wait_ge(a_vs, 16)
                    with dve.If(flagged(dve, flag_a, FAI)):
                        dve.sem_inc(ga_kv, 1)
                        dve.sem_inc(ga_add, 1)
                        dve.sem_inc(ga_prod, 1)
                        dve.sem_inc(ga_out, 1)
                        chain_a = [0]

                        def settle_a(ins):
                            chain_a[0] += 1
                            ins.then_inc(ga_chain, 1)
                            dve.wait_ge(ga_chain, chain_a[0])

                        cnt, L, rL = GSM[:, 0, :], GSM[0:96, 1, :], GSM[0:96, 2, :]
                        by_b = lambda v: v.unsqueeze(2).to_broadcast([96, B, P])
                        gv = lambda a, g: a[:, g, :].rearrange("p (b q) -> p b q", b=B)
                        settle_a(dve.tensor_reduce(cnt, MKB[:, :, :], AX.X, ALU.add))
                        dve.tensor_copy(GSM[:, 3, :], cnt).then_inc(ga_zero, 1)
                        dve.wait_ge(ga_sum_ps, 1)
                        settle_a(dve.tensor_scalar(L, BK[0:96, 0, 0:B], -1.0, float(S2 - 1), ALU.mult, ALU.add))
                        settle_a(dve.reciprocal(rL, L))
                        for g in range(3):
                            gx, gt = gv(GIX, g), gv(GT1, g)
                            settle_a(dve.tensor_tensor(gt, gv(Y, g), by_b(rL), ALU.mult))
                            settle_a(dve.tensor_scalar(gt, gt, 12582912.0, None, ALU.add))
                            settle_a(dve.tensor_scalar(gt, gt, -12582912.0, None, ALU.add))
                            settle_a(dve.tensor_tensor(gt, gt, by_b(L), ALU.mult))
                            settle_a(dve.tensor_tensor(gx, gv(Y, g), gt, ALU.subtract))
                            settle_a(dve.tensor_tensor(gt, gx, by_b(L), ALU.mult))
                            settle_a(dve.tensor_scalar(gt, gt, 0.0, None, ALU.is_lt))
                            settle_a(dve.tensor_tensor(gt, gt, by_b(L), ALU.mult))
                            settle_a(dve.tensor_tensor(gx, gx, gt, ALU.add))
                            settle_a(dve.tensor_scalar(gx, gx, float(S2) / (S2 - 1), -0.5, ALU.mult, ALU.add))
                        dve.memset(GKV[:, 2 * D:2 * D + 16], 0.0).then_inc(ga_pos, 1)
                        with dve.Fori(0, B) as b:
                            dve.wait_ge(ga_prod, 1 + b * 4)
                            dve.memset(GSK, 0.0).then_inc(ga_zero, 1)
                            with dve.Fori(0, S2 // P) as c:
                                it = b * (S2 // P) + c
                                dve.wait_ge(ga_zero, b + 2)
                                dve.wait_ge(ga_samp, 1 + it * 4)
                                dve.wait_ge(ga_kv_ps, 1 + it + 1)
                                dve.tensor_tensor(GKV[:, 0:2 * D], BK[:, 7, 0:2 * D], row("bkv"), ALU.add).then_inc(ga_kv, 1)
                                dve.tensor_copy(GPOS, pos[:, bass.ds(c, 1)]).then_inc(ga_kv, 1)
                                for e in range(E1):
                                    dve.wait_ge(ga_abs, 1 + it * E1 + e + 1)
                                    w = GW[:, e % 20 // NK, e % NK, :]
                                    dve.tensor_scalar(w, w, 1.0, -1.0, ALU.min, ALU.add).then_inc(ga_w, 1)
                                    if e % 20 == 19:
                                        G = e // 20
                                        dve.wait_ge(ga_samp, 1 + it * 4 + G + 1)
                                        dve.wait_ge(ga_add, 1 + it * 4 + G)
                                        dve.tensor_tensor(GSK[:, G, :], GSK[:, G, :], BK[:, 3:5, :].rearrange("p a n -> p (a n)")[:, 0:NK * P],
                                                          ALU.add).then_inc(ga_add, 1)
                            for G in range(4):
                                dve.wait_ge(ga_tr, b * 4 + G + 1)
                                src = BK[:, 5:7, :].rearrange("p a n -> p (a n)")[:, 0:NK * P]
                                src = src.rearrange("p (k h r) -> p k h r", k=NK, h=4)
                                qv = Qq[:, bass.ds(b, 1), 32 * G:32 * G + 32].rearrange("p b (h d) -> p (b h) d", h=4)
                                dve.wait_ge(ga_out, 1 + b * 4 + G)
                                dve.tensor_tensor(PRD[:, :, :, :], src[:, :, :, 0:HD], over(qv, NK), ALU.mult)\
                                   .then_inc(ga_prod, 1)
                                for k in range(NK):
                                    dve.tensor_copy(VS[:, bass.ds(b, 1), 4 * G:4 * G + 4, k, :].rearrange("p b h d -> p (b h) d"),
                                                    src[:, k, :, HD:2 * HD])
                                dve.wait_ge(ga_prod, 1 + b * 4 + G + 1)
                                dve.tensor_reduce(SCO[:, bass.ds(b, 1), 4 * G:4 * G + 4, :].rearrange("p b h k -> p (b h) k"),
                                                  PRD[:, :, :, :].rearrange("p k h d -> p h k d"), AX.X, ALU.add)\
                                   .then_inc(ga_out, 1)
                        dve.wait_ge(ga_out, 1 + 4 * B)
                    z = SCO[:, :, :, :].rearrange("p b h k -> p (b h) k")
                    m1 = SM1[:, :, :].rearrange("p b h -> p (b h)")
                    m2 = SM2[:, :, :].rearrange("p b h -> p (b h)")
                    settle(dve.tensor_scalar(z, z, -0.5 / np.sqrt(HD), None, ALU.mult))
                    settle(dve.tensor_reduce(m1, z, AX.X, ALU.max))
                    dve.tensor_tensor(z, z, over(m1, NK, 2), ALU.subtract).then_inc(a_z, 1)
                    dve.wait_ge(a_exp, 1)
                    settle(dve.tensor_reduce(m1, z, AX.X, ALU.add))
                    settle(dve.reciprocal(m2, m1))
                    settle(dve.tensor_scalar(m1, m2, -0.5, None, ALU.mult))
                    settle(dve.tensor_tensor(z, z, over(m1, NK, 2), ALU.mult))
                    vs = VS.rearrange("p b h k d -> p (b h) k d")
                    pv = PV.rearrange("p b h k d -> p (b h) k d")
                    settle(dve.tensor_tensor(pv, vs, over(z, HD, 3), ALU.mult))
                    dve.tensor_reduce(CT[:, :, :].rearrange("p b (h d) -> p (b h) d", h=H),
                                      pv.rearrange("p n k d -> p n d k"), AX.X, ALU.add).then_inc(ctx_ready, 1)
                    dve.wait_ge(xb_ready, 1)
                    residual("A", XB[:, :, :])
                if s == "B":
                    stats(LN_B, X)
                    norm(LN_B, X, XH)
                    dve.wait_ge(loads["decay"], 64)
                    for j, dst in ((0, qT), (2, kT)):
                        dve.wait_ge(b_qk_ps, j + 1)
                        dve.tensor_tensor(T0[:, :, :], bank(j), over(rope0[:, j, :], B), ALU.mult)
                        dve.wait_ge(b_qk_ps, j + 2)
                        settle(dve.tensor_tensor(T1[:, :, :], bank(j + 1), over(rope0[:, j + 1, :], B), ALU.mult))
                        dve.tensor_tensor(dst[:, :, :], T0[:, :, :], T1[:, :, :], ALU.add)\
                           .then_inc(b_rot, 1)
                        dve.wait_ge(b_rot, 2 if j else 1)

                    def blk(b):
                        if b >= 2:
                            dve.wait_ge(b_s_ps, 4 * (b - 1))
                        dve.tensor_tensor(BLK[:, b % 2], over(qT[:, b, :], 4), over(head[:, :], P, 2), ALU.mult)\
                           .then_inc(b_blk, 1)

                    def extract(b):
                        dve.wait_ge(b_o_ps, b + 1)
                        settle(dve.tensor_tensor(OM, bank(4 + b % 2).rearrange("p (h t) -> p h t", h=4),
                                                 over(head[:, :], P, 2), ALU.mult))
                        dve.tensor_reduce(CT[:, b, :], OM.rearrange("p h t -> p t h"), AX.X, ALU.add)\
                           .then_inc(b_oT, 1)
                        dve.wait_ge(b_oT, b + 1)

                    blk(0)
                    blk(1)
                    for b in range(B):
                        for g in range(4):
                            dve.wait_ge(b_s_ps, 4 * b + g + 1)
                            if b >= 2 and g == 0:
                                dve.wait_ge(b_o_ps, b - 1)
                            dve.tensor_tensor(PT[:, b % 2, 4 * g:4 * g + 4, :], bank(g).rearrange("p (h t) -> p h t", h=4),
                                              decay[:, 4 * g:4 * g + 4, :], ALU.mult).then_inc(b_pt, 1)
                        if b + 2 < B:
                            blk(b + 2)
                        if b:
                            extract(b - 1)
                    extract(B - 1)
                    dve.wait_ge(b_oc_ps, 1)
                    dve.wait_ge(b_std, 1)
                    settle(dve.reciprocal(T1[:, :, :], T1[:, :, :]))
                    settle(dve.tensor_tensor(T1[:, :, :], bank(4), T1[:, :, :], ALU.mult))
                    dve.tensor_scalar(CTT[:, :], T1[:, :, :].rearrange("p b t -> p (b t)"), col("gn_w"), col("gn_b"),
                                      ALU.mult, ALU.add).then_inc(b_on, 1)
                    residual("B", X[:, :, :])
                if s in "CF":
                    k = FFNS.index(s)
                    ln = LN_C if s == "C" else LN_F
                    stats(ln, X)
                    norm(ln, X, XH)
                    dve.wait_ge(r_lg_ps, k + 1)
                    lg = BK[:, 4, 0:B * NE].rearrange("p (b e) -> p b e", b=B)
                    settle(dve.tensor_reduce(S1[:, :], lg, AX.X, ALU.max))
                    dve.tensor_tensor(EX[:, :, :], lg, over(S1[:, :], NE, 2), ALU.subtract).then_inc(r_z, 1)
                    dve.wait_ge(r_exp, k + 1)
                    settle(dve.tensor_reduce(S1[:, :], EX[:, :, :], AX.X, ALU.add))
                    settle(dve.reciprocal(S1[:, :], S1[:, :]))
                    settle(dve.tensor_tensor(PR[:, :, :], EX[:, :, :], over(S1[:, :], NE, 2), ALU.mult))
                    other, own = over(PR[:, :, :], NE, 2), over(PR[:, :, :], NE, 3)
                    dve.tensor_tensor(CMP[:, :, :, :], other, own, ALU.is_gt)
                    settle(dve.tensor_tensor(CMQ[:, :, :, :], other, own, ALU.is_equal))
                    if not k:
                        dve.wait_ge(loads["crows"], 16)
                    before = crows[:, BEFORE].rearrange("p (e f) -> p e f", e=NE)
                    settle(dve.tensor_tensor(CMQ[:, :, :, :], CMQ[:, :, :, :], over(before, B), ALU.mult))
                    settle(dve.tensor_tensor(CMP[:, :, :, :], CMP[:, :, :, :], CMQ[:, :, :, :], ALU.add))
                    settle(dve.tensor_reduce(RK[:, :, :], CMP[:, :, :, :], AX.X, ALU.add))
                    settle(dve.scalar_tensor_tensor(out=PR[:, :, :], in0=RK[:, :, :], scalar=1.5, in1=PR[:, :, :],
                                                    op0=ALU.is_lt, op1=ALU.mult))
                    settle(dve.tensor_reduce(S1[:, :], PR[:, :, :], AX.X, ALU.add))
                    if s == "C":
                        settle(dve.tensor_scalar(S1[:, :], S1[:, :], 1e-9, None, ALU.add))
                    settle(dve.reciprocal(S1[:, :], S1[:, :]))
                    dve.tensor_tensor(CW[:, :, :], PR[:, :, :], over(S1[:, :], NE, 2), ALU.mult).then_inc(r_cw, 1)
                    for e in range(NE):
                        n = k * NE + e
                        if s == "C":
                            dve.wait_ge(e_act, n + 1)
                            if e >= 2:
                                dve.wait_ge(e_y_ps, n - 1)
                            for j in range(2):
                                ba = cols[:, B1COL + 4 * e + j:B1COL + 4 * e + 1 + j]
                                ins = dve.scalar_tensor_tensor(out=GT[:, e % 2, j, :], in0=bank(j), scalar=ba,
                                                               in1=SG[:, e % 2, j, :], op0=ALU.add, op1=ALU.mult)
                            ins.then_inc(e_g, 1)
                        if e:
                            weigh(dve, s, k, e - 1)
                    weigh(dve, s, k, NE - 1)
                    dve.wait_ge(e_accT_ps, k + 1)
                    dve.tensor_tensor(X[:, :, :], bank(7), X[:, :, :], ALU.add).then_inc(x_ready, 1)
                    dve.wait_ge(x_ready, nx[s] + 1)
                if s == "D":
                    stats(LN_D, X)
                    norm(LN_D, X, XH)
                    settle(dve.tensor_scalar(MB[:, :], mtail[:, :], 0, KEPT, ALU.not_equal, ALU.mult))
                    settle(dve.tensor_scalar(MB[:, :], MB[:, :], NEG, None, ALU.add))
                    dve.wait_ge(kd_ready, 1)

                    def blk(b):
                        if b >= 2:
                            dve.wait_ge(d_s_ps, 4 * (b - 1))
                        dve.tensor_tensor(BLK[:, b % 2], over(kTd[:, b, :], 4), over(head[:, :], P, 2), ALU.mult)\
                           .then_inc(d_blk, 1)

                    def extract(b):
                        dve.wait_ge(d_o_ps, b + 1)
                        dve.tensor_tensor(OM, bank(6).rearrange("p (h t) -> p h t", h=4),
                                          over(head[:, :], P, 2), ALU.mult)
                        settle(dve.tensor_tensor(DN, bank(7).rearrange("p (h t) -> p h t", h=4),
                                                 over(head[:, :], P, 2), ALU.mult))
                        dve.tensor_reduce(T0[:, b, :], OM.rearrange("p h t -> p t h"), AX.X, ALU.add)
                        settle(dve.tensor_reduce(T1[:, b, :], DN.rearrange("p h t -> p t h"), AX.X, ALU.add))
                        settle(dve.reciprocal(T1[:, b, :], T1[:, b, :]))
                        dve.tensor_tensor(CTT[:, b * P:(b + 1) * P], T0[:, b, :], T1[:, b, :], ALU.mult)\
                           .then_inc(d_om, 1)
                        dve.wait_ge(d_om, b + 1)

                    blk(0)
                    blk(1)
                    for b in range(B):
                        for g in range(4):
                            dve.wait_ge(d_s_ps, 4 * b + g + 1)
                            if b >= 2 and g == 0:
                                dve.wait_ge(d_pT_ps, 4 * (b - 1))
                            ins = dve.scalar_tensor_tensor(
                                out=SS[:, b % 2, 4 * g:4 * g + 4, :], in0=bank(g).rearrange("p (h t) -> p h t", h=4),
                                scalar=float(1.0 / np.sqrt(HD)), in1=over(MB[:, :], 4), op0=ALU.mult, op1=ALU.min)
                            ins.then_inc(d_ss, 1)
                        dve.wait_ge(d_ss, 4 * b + 4)
                        dve.tensor_reduce(MX[:, b, :], SS[:, b % 2], AX.X, ALU.max).then_inc(d_mx, 1)
                        if b + 2 < B:
                            blk(b + 2)
                        if b:
                            extract(b - 1)
                    extract(B - 1)
                    with dve.If(flagged(dve, flag_d, FDI)):
                        dve.sem_inc(gd_v, 1)
                        dve.sem_inc(gd_oT, 1)
                        dve.sem_inc(gd_o, 1)
                        dve.wait_ge(gd_mask, 16)
                        dve.tensor_scalar(GM, GMI, 0, KEPT, ALU.not_equal, ALU.mult).then_inc(gd_m0, 1)
                        dve.wait_ge(gd_m0, 1)
                        dve.tensor_scalar(GM, GM, NEG, None, ALU.add).then_inc(gd_m0, 1)
                        dve.wait_ge(gd_m0, 2)
                        with dve.Fori(0, B) as b:
                            with dve.Fori(0, S2 // P) as c:
                                it = b * (S2 // P) + c
                                dve.wait_ge(gd_kv_ps, 1 + it + 1)
                                dve.tensor_tensor(GV[:, bass.ds(c, 1), :].rearrange("p c n -> p (c n)"), BK[:, 1, 0:P],
                                                  row("x_bv"), ALU.add).then_inc(gd_v, 1)
                            with dve.Fori(0, H) as h:
                                it = b * H + h
                                dve.wait_ge(gd_s_ps, 1 + it)
                                dve.tensor_scalar(GQ, qT[:, bass.ds(b, 1), :].rearrange("p b n -> p (b n)"),
                                                  head16[:, bass.ds(h, 1)], None, ALU.mult).then_inc(gd_q, 1)
                                dve.wait_ge(gd_s_ps, 1 + it + 1)
                                dve.scalar_tensor_tensor(out=GSC, in0=BK[:, 0:4, :].rearrange("p a n -> p (a n)"),
                                                         scalar=float(1.0 / np.sqrt(HD)), in1=GM, op0=ALU.mult,
                                                         op1=ALU.min).then_inc(gd_chain, 1)
                                dve.wait_ge(gd_chain, 3 * it + 1)
                                dve.tensor_reduce(GR[:, 2:3], GSC, AX.X, ALU.max).then_inc(gd_chain, 1)
                                dve.wait_ge(gd_chain, 3 * it + 2)
                                dve.tensor_scalar(GR[:, 0:1], GR[:, 2:3], -1.0, None, ALU.mult).then_inc(gd_neg, 1)
                                dve.wait_ge(gd_o_ps, it + 1)
                                dve.reciprocal(GR[:, 3:4], GR[:, 1:2]).then_inc(gd_chain, 1)
                                dve.wait_ge(gd_chain, 3 * it + 3)
                                dve.tensor_scalar(GO[:, bass.ds(h * HD, HD)], BK[:, 0, bass.ds(h * HD, HD)], GR[:, 3:4],
                                                  None, ALU.mult).then_inc(gd_o, 1)
                            dve.wait_ge(gd_oT_ps, b + 1)
                            dve.tensor_copy(CTT[:, bass.ds(b * P, P)], BK[:, 1, 0:P]).then_inc(gd_oT, 1)
                        dve.wait_ge(gd_oT, 1 + B)
                    dve.wait_ge(xb_ready, BIASED.index("D") + 1)
                    residual("D", XB[:, :, :])
                if s == "E":
                    stats(LN_E0, X)
                    norm(LN_E0, X, XN)
                    stats(LN_E1, XN)
                    norm(LN_E1, XN, XH)
                    settle(dve.tensor_tensor(HH[:, :, :], XH[:, :, :], over(row("ln1_w"), B), ALU.mult))
                    dve.tensor_tensor(HH[:, :, :], HH[:, :, :], over(row("ln1_b"), B), ALU.add).then_inc(l_h1, 1)
                    dve.wait_ge(l_h1, 1)
                    settle(dve.tensor_tensor(XH[:, :, :], HH[:, :, :], over(row("conv1"), B), ALU.mult))
                    dve.wait_ge(l_hp, 1)
                    dve.tensor_copy(HH[:, 0, :], XH[:, 0, :])
                    dve.tensor_tensor(HH[:, 1:4, :], XH[:, 1:4, :], HP[:, 0:3, :], ALU.add).then_inc(l_hc, 1)
                    dve.wait_ge(loads["crows"], 16)
                    dve.wait_ge(l_vkqg, 1)
                    rw = rows[:, ROWS["rw"]].rearrange("p (r n) -> p r n", r=2)
                    for r in range(2):
                        ins = dve.tensor_tensor(LP[:, r], VV[:, :, :], over(rw[:, r, :], B), ALU.mult)
                    settle(ins)
                    lg = LGT[:, :, :, :].rearrange("p r b h -> p r (b h)")
                    settle(dve.tensor_reduce(LGT[:, :, :, :].rearrange("p r b h -> p (r b h)"),
                                             LP[:, :, :, :].rearrange("p r b (h d) -> p (r b h) d", h=H), AX.X, ALU.add))
                    settle(dve.tensor_tensor(OH[:, :, :], LGT[:, 0], LGT[:, 1], ALU.is_ge))
                    settle(dve.tensor_tensor(SM1[:, :, :], LGT[:, 0], LGT[:, 1], ALU.max))
                    dve.tensor_tensor(LGT[:, :, :, :], LGT[:, :, :, :], over(SM1[:, :, :], 2), ALU.subtract)\
                       .then_inc(l_ld, 1)
                    settle(dve.tensor_tensor(SMM[:, :, :, :], over(OH[:, :, :], B, 2), over(OH[:, :, :], B, 1), ALU.is_equal))
                    cz = crows[:, CAUSAL1].rearrange("p (l m h) -> p l m h", l=B, m=B)
                    settle(dve.tensor_tensor(SMM[:, :, :, :], SMM[:, :, :, :], cz, ALU.mult))
                    settle(dve.tensor_reduce(OH[:, :, :], SMM[:, :, :, :].rearrange("p l m h -> p l h m"), AX.X, ALU.add))
                    dve.wait_ge(l_le, 1)
                    settle(dve.tensor_tensor(SM1[:, :, :], LGE[:, 0], LGE[:, 1], ALU.add))
                    settle(dve.tensor_tensor(SM1[:, :, :], SM1[:, :, :], OH[:, :, :], ALU.mult))
                    settle(dve.reciprocal(SM2[:, :, :], SM1[:, :, :]))
                    settle(dve.tensor_tensor(SMM[:, :, :, :], SMM[:, :, :, :], over(SM2[:, :, :], B, 2), ALU.mult))
                    dve.wait_ge(l_vkqg, 3)
                    cs = crows[:, ROPE1].rearrange("p (a n) -> p a n", a=2)
                    qk = QK[:, :, :, :].rearrange("p b a n -> p (b a n)")
                    dve.tensor_tensor(QR[:, :, :, :].rearrange("p b a n -> p (b a n)"), qk, cs[:, 0, :], ALU.mult)
                    halves = lambda a: a.rearrange("p (n f i) -> p n f i", f=2, i=2)
                    q2 = Q2[:, :, :, :].rearrange("p b a n -> p (b a n)")
                    for f in range(2):
                        ins = dve.tensor_tensor(halves(q2)[:, :, f, :], halves(qk)[:, :, 1 - f, :],
                                                halves(cs[:, 1, :])[:, :, f, :], ALU.mult)
                    settle(ins)
                    settle(dve.tensor_tensor(QR[:, :, :, :], QR[:, :, :, :], Q2[:, :, :, :], ALU.add))
                    for l in range(B):
                        ins = dve.tensor_tensor(PDT[:, l], over(QR[:, l, 0, :], B), QR[:, :, 1, :], ALU.mult)
                    settle(ins)
                    settle(dve.tensor_reduce(DT[:, :, :, :].rearrange("p l m h -> p (l m h)"),
                                             PDT[:, :, :, :].rearrange("p l m (h d) -> p (l m h) d", h=H), AX.X, ALU.add))
                    settle(dve.tensor_tensor(DT[:, :, :, :], DT[:, :, :, :], SMM[:, :, :, :], ALU.mult))
                    for l in range(B):
                        ins = dve.tensor_tensor(PO[:, l, 0:l + 1].rearrange("p m (h d) -> p (m h) d", h=H),
                                                over(DT[:, l, 0:l + 1, :].rearrange("p m h -> p (m h)"), HD, 2),
                                                VV[:, 0:l + 1, :].rearrange("p m (h d) -> p (m h) d", h=H), ALU.mult)
                    settle(ins)
                    dve.tensor_copy(OO[:, 0, :], PO[:, 0, 0, :])
                    for l in range(1, B):
                        ins = dve.tensor_reduce(OO[:, l, :], PO[:, l, 0:l + 1, :].rearrange("p m n -> p n m"), AX.X, ALU.add)
                    settle(ins)
                    hv = lambda a: a[:, :, :].rearrange("p b (h d) -> p (b h) d", h=H)
                    m1 = SM1[:, :, :].rearrange("p b h -> p (b h)")
                    m2 = SM2[:, :, :].rearrange("p b h -> p (b h)")
                    settle(dve.tensor_reduce(m1, hv(OO), AX.X, ALU.add))
                    settle(dve.tensor_scalar(m2, m1, 1.0 / HD, None, ALU.mult))
                    dve.tensor_tensor(hv(OO), hv(OO), over(m2, HD, 2), ALU.subtract).then_inc(l_oc, 1)
                    dve.wait_ge(l_sq, 1)
                    dve.tensor_reduce(m1, hv(OQ), AX.X, ALU.add).then_inc(l_vs, 1)
                    dve.wait_ge(l_std, 1)
                    settle(dve.reciprocal(m1, m2))
                    settle(dve.tensor_tensor(hv(OO), hv(OO), over(m1, HD, 2), ALU.mult))
                    dve.wait_ge(l_vkqg, 4)
                    dve.tensor_tensor(CT[:, :, :], OO[:, :, :], GS[:, :, :], ALU.mult).then_inc(ctx_ready, 1)
                    dve.wait_ge(proj_ps, PROJ.index("E") + 1)
                    dve.tensor_tensor(CT[:, :, :], bank(6), XN[:, :, :], ALU.add).then_inc(l_xa, 1)
                    dve.wait_ge(l_xa, 1)
                    stats(LN_E2, CT)
                    norm(LN_E2, CT, XH)
                    settle(dve.tensor_tensor(XH[:, :, :], XH[:, :, :], over(row("ln2_w"), B), ALU.mult))
                    dve.tensor_tensor(XH[:, :, :], XH[:, :, :], over(row("ln2_b"), B), ALU.add).then_inc(l_h2, 1)
                    for j, (o, w) in enumerate(FFT):
                        dve.wait_ge(l_ffs, j + 1)
                        dve.wait_ge(l_ff_ps, 3 + j + 1)
                        dve.tensor_tensor(HF[0:w, j, :], BK[0:w, (3, 4, 6)[j], :], HF[0:w, j, :], ALU.mult).then_inc(l_ff, 1)
                    dve.wait_ge(xb_ready, BIASED.index("E") + 1)
                    dve.wait_ge(proj_ps, PROJ.index("E") + 2)
                    dve.tensor_tensor(X[:, :, :], bank(7), XB[:, :, :], ALU.add).then_inc(x_ready, 1)
                    dve.wait_ge(x_ready, nx[s] + 1)

        @block.tensor
        def _(pe):
            def norm_T(n, bk, src=XH):
                for b in range(B):
                    pe.wait_ge(ln_xhat, xhat_count(n) - 3 + b)
                    ins = pe.transpose(BK[:, bk, b * P:(b + 1) * P], src[:, b, :], ident[:, :])
                ins.then_inc(ln_xT_ps, 1)

            def transposes(src, bk, s):
                for b in range(B):
                    ins = pe.transpose(BK[:, bk, b * P:(b + 1) * P], src[:, b, :], ident[:, :])
                ins.then_inc(s, 1)

            def project(w, bk=7):
                for b in range(B):
                    ins = pe.matmul(BK[:, bk, b * P:(b + 1) * P], CTT[:, b * P:(b + 1) * P], w, start=True, stop=True)
                ins.then_inc(proj_ps, 1)

            pe.wait_ge(loads["ident"], 16)
            if stages[0] == "A":
                norm_T(LN_A, 5)
            pe.wait_ge(loads["w_a"], 16)
            pe.wait_ge(loads["win"], 32)
            for j in range(8):
                b, hf = j // 2, j % 2
                ins = pe.matmul(BK[:, j // 2, 256 * (j % 2):256 * (j % 2) + 256], WIN[:, b, QH * hf:QH * hf + P],
                                w_a[:, 0:256], start=True, stop=True)
                if j % 2:
                    ins.then_inc(kvw_ps, 1)
            pe.wait_ge(loads["w_d"], 16)
            pe.wait_ge(loads["tail"], 16)
            pe.matmul(bank(4), w_d[:, 0:D], TAIL.rearrange("p b n -> p (b n)"), start=True, stop=True)\
              .then_inc(kd_ps, 1)
            for b in range(B):
                ins = pe.matmul(BK[:, 7, b * P:(b + 1) * P], TAIL[:, b, :], w_d[:, D:2 * D], start=True, stop=True)
            ins.then_inc(kd_ps, 1)

            for s in stages:
                if s == "A":
                    pe.wait_ge(ln_xT, xT_count(LN_A))
                    wq, woff, wo = w_a[:, 256:384], w_a[:, 384:672].rearrange("p (g n) -> p g n", g=3), w_a[:, 672:800]
                    pe.matmul(bank(6), wq, XT[:, :], start=True, stop=True).then_inc(a_q_ps, 1)
                    pe.wait_ge(kd_ready, 1)
                    for b in range(B):
                        ins = pe.matmul(BK[:, 4, b * P:(b + 1) * P], XT[:, b * P:(b + 1) * P], wq, start=True, stop=True)
                    ins.then_inc(a_q_ps, 1)
                    pe.wait_ge(a_qT, 1)
                    pe.wait_ge(kvw_ready, 4)
                    for g in range(3):
                        pe.matmul(BK[0:96, g, :], woff[:, g, :], QpT[:, :], start=True, stop=True).then_inc(a_off_ps, 1)

                    def spread(e):
                        if e < 3:
                            pe.wait_ge(a_r, e + 1)
                        else:
                            pe.wait_ge(a_abs, e - 2)
                        pe.matmul(bank(e % 3), SEL[:, e % 32, :], R[:, e // 32, :], start=True, stop=True)\
                          .then_inc(a_ix_ps, 1)

                    def sample(G, i):
                        if i == 0:
                            pe.wait_ge(a_w, 20 * G + 20)
                            pe.wait_ge(a_qq, 1)
                        n = 8 * G + i
                        if n >= 2:
                            pe.wait_ge(a_sk, n - 1)
                        for h in range(4):
                            c = 16 * (4 * G + h)
                            ins = pe.matmul(BK[32 * h:32 * h + 32, 3 + n % 2, 0:NK * QH], KVW[:, i, c:c + 32],
                                            WT[:, G % 2, h, i, :, :].rearrange("p k q -> p (k q)"),
                                            start=True, stop=True)
                        ins.then_inc(a_samp_ps, 1)

                    def back(G, b):
                        u = 4 * G + b
                        pe.wait_ge(a_sk, 8 * G + 2 * b + 2)
                        if u:
                            pe.wait_ge(a_vs, u)
                            pe.wait_ge(a_prod, u)
                        for k in range(NK):
                            ins = pe.transpose(BK[:, 5 + k // 4, k % 4 * P:k % 4 * P + P], SK[:, b, k, :],
                                               ident[:, :])
                        ins.then_inc(a_tr_ps, 1)

                    for i in range(20):
                        spread(i)
                    for G in range(1, 5):
                        for i in range(20):
                            if G < 4:
                                spread(20 * G + i)
                            if i < 8:
                                sample(G - 1, i)
                            if i in BACK_AT:
                                back(G - 1, BACK_AT.index(i))
                    with pe.If(flagged(pe, flag_a, FAI)):
                        pe.sem_inc(ga_kv_ps, 1)
                        pe.sem_inc(ga_samp, 1)
                        pe.wait_ge(ga_zero, 1)
                        pe.matmul(BK[0:96, 0, 0:B], ones[:, 0:96], GSM[:, 3, :], start=True, stop=True).then_inc(ga_sum_ps, 1)
                        pe.wait_ge(ga_pos, 1)
                        with pe.Fori(0, B) as b:
                            with pe.Fori(0, S2 // P) as c:
                                it = b * (S2 // P) + c
                                pe.wait_ge(ga_in, it * 16 + 16)
                                pe.wait_ge(ga_kv, 1 + 2 * it)
                                pe.matmul(BK[:, 7, 0:2 * D], GCH, w_a[:, 0:2 * D], start=True, stop=True)\
                                  .then_inc(ga_kv_ps, 1)
                                for e in range(E1):
                                    g, i, G = e // 32, e % 32, e // 20
                                    pe.wait_ge(ga_abs, 1 + it * E1 + e)
                                    pe.matmul(BK[:, 0, 0:P], ident[0:96, i:i + 1].to_broadcast([96, P]),
                                              GIX[:, g, bass.ds(b * P, P)], start=True, stop=True).then_inc(ga_ix, 1)
                                    if e % 20 == 19:
                                        pe.wait_ge(ga_kv, 1 + 2 * it + 1)
                                        pe.wait_ge(ga_w, it * E1 + e + 1)
                                        pe.wait_ge(ga_add, 1 + it * 4 + G)
                                        for h in range(4):
                                            for k in range(NK):
                                                o = 16 * (4 * G + h)
                                                ins = pe.matmul(BK[32 * h:32 * h + 32, 3 + k // 4, k % 4 * P:k % 4 * P + P],
                                                                GKV[:, o:o + 32], GW[:, h, k, :], start=True, stop=True)
                                        ins.then_inc(ga_samp, 1)
                            for G in range(4):
                                pe.wait_ge(ga_add, 1 + b * (4 * S2 // P) + 4 * (S2 // P))
                                pe.wait_ge(ga_out, 1 + b * 4 + G)
                                for k in range(NK):
                                    ins = pe.transpose(BK[:, 5 + k // 4, k % 4 * P:k % 4 * P + P],
                                                       GSK[:, G, k * P:(k + 1) * P], ident[:, :])
                                ins.then_inc(ga_tr, 1)
                    pe.wait_ge(ctx_ready, 1)
                    transposes(CT, 6, ctxT_ps)
                    pe.wait_ge(ctxT_ready, 1)
                    pe.wait_ge(vd_ready, 1)
                    project(wo)
                if s == "B":
                    norm_T(LN_B, 7)
                    pe.wait_ge(ln_xT, xT_count(LN_B))
                    pe.wait_ge(loads["w_b"], 16)
                    for j in range(4):
                        pe.matmul(bank(j), w_b[:, j * D:(j + 1) * D], XT[:, :], start=True, stop=True).then_inc(b_qk_ps, 1)
                    for b in range(B):
                        ins = pe.matmul(BK[:, 4, b * P:(b + 1) * P], XT[:, b * P:(b + 1) * P], w_b[:, 4 * D:5 * D],
                                        start=True, stop=True)
                    ins.then_inc(b_v_ps, 1)
                    pe.wait_ge(b_rot, 2)
                    pe.wait_ge(b_v, 1)

                    def scores(b):
                        pe.wait_ge(b_blk, b + 1)
                        for g in range(4):
                            if b:
                                pe.wait_ge(b_pt, 4 * (b - 1) + g + 1)
                            o = 32 * g
                            pe.matmul(bank(g), kT[o:o + 32, b, :], BLK[o:o + 32, b % 2].rearrange("p h t -> p (h t)"),
                                      start=True, stop=True).then_inc(b_s_ps, 1)

                    def values(b):
                        pe.wait_ge(b_pt, 4 * b + 4)
                        if b >= 2:
                            pe.wait_ge(b_oT, b - 1)
                        for g in range(4):
                            o = 32 * g
                            ins = pe.matmul(BK[o:o + 32, 4 + b % 2, :], vq[:, b, o:o + 32],
                                            PT[:, b % 2, 4 * g:4 * g + 4, :].rearrange("p h t -> p (h t)"),
                                            start=True, stop=True)
                        ins.then_inc(b_o_ps, 1)

                    scores(0)
                    for b in range(B):
                        if b + 1 < B:
                            scores(b + 1)
                        values(b)
                    pe.wait_ge(b_oT, 4)
                    ct = CT[:, :, :].rearrange("p b t -> p (b t)")
                    pe.matmul(bank(4), group[:, 0, :], ct, start=True, stop=True).then_inc(b_oc_ps, 1)
                    pe.wait_ge(b_sq, 1)
                    pe.matmul(bank(5), group[:, 1, :], T0[:, :, :].rearrange("p b t -> p (b t)"), start=True, stop=True)\
                      .then_inc(b_var_ps, 1)
                    pe.wait_ge(b_on, 1)
                    project(w_b[:, 5 * D:6 * D])
                if s in "CF":
                    k = FFNS.index(s)
                    ln = LN_C if s == "C" else LN_F
                    norm_T(ln, 7)
                    pe.wait_ge(ln_xT, xT_count(ln))
                    wg = w_c[:, 0:8] if s == "C" else w_f[:, :]
                    w1 = w_c1 if s == "C" else w_f1
                    pe.wait_ge(loads["w_c" if s == "C" else "w_e"], 16 if s == "C" else 48)
                    for b in range(B):
                        ins = pe.matmul(BK[:, 4, b * NE:(b + 1) * NE], XT[:, b * P:(b + 1) * P], wg, start=True, stop=True)
                    ins.then_inc(r_lg_ps, 1)
                    pe.wait_ge(loads["w_c1" if s == "C" else "w_f1"], 16)
                    if s == "F":
                        pe.wait_ge(loads["w_f2"], 16)

                    def up(e):
                        n = k * NE + e
                        if e:
                            pe.wait_ge(e_g, n) if s == "C" else pe.wait_ge(e_act, n)
                        for j in range(4):
                            o = (4 * e + j) * P
                            ins = pe.matmul(bank(j), w1[:, o:o + P], XT[:, :], start=True, stop=True)
                        ins.then_inc(e_h_ps, 1)

                    def down(e):
                        n = k * NE + e
                        pe.wait_ge(e_g, n + 1) if s == "C" else pe.wait_ge(e_act, n + 1)
                        pe.wait_ge(r_z, k + 1)
                        if e >= 2:
                            pe.wait_ge(e_ys, n - 1)
                        m = 2 if s == "C" else 4
                        for j in range(m):
                            w = w_c[:, 8 + j * D:8 + (j + 1) * D] if s == "C" else w_f2[:, (4 * e + j) * D:(4 * e + j + 1) * D]
                            ins = pe.matmul(bank(4 + e % 2), w, GT[:, e % 2, j, :], start=(j == 0), stop=(j == m - 1))
                        ins.then_inc(e_y_ps, 1)

                    def spread_cw(e):
                        if e >= 2:
                            pe.wait_ge(r_cb, k * NE + e - 1)
                        pe.matmul(bank(6 + e % 2), ident[0:NE, e:e + 1].to_broadcast([NE, P]), CWT[:, :],
                                  start=True, stop=True).then_inc(r_cb_ps, 1)

                    up(0)
                    pe.wait_ge(r_cw, k + 1)
                    for b in range(B):
                        ins = pe.transpose(BK[0:NE, 6, b * P:(b + 1) * P], CW[:, b, :], ident[:, :])
                    ins.then_inc(r_cwT_ps, 1)
                    pe.wait_ge(r_cwT, k + 1)
                    spread_cw(0)
                    spread_cw(1)
                    for e in range(NE):
                        if e + 1 < NE:
                            up(e + 1)
                        down(e)
                        if e + 2 < NE:
                            spread_cw(e + 2)
                    pe.wait_ge(e_acc, k * NE + NE)
                    pe.wait_ge(r_cb, k * NE + NE)
                    for b in range(B):
                        ins = pe.transpose(BK[:, 7, b * P:(b + 1) * P], ACC[:, b * P:(b + 1) * P], ident[:, :])
                    ins.then_inc(e_accT_ps, 1)
                if s == "D":
                    norm_T(LN_D, 7)
                    pe.wait_ge(ln_xT, xT_count(LN_D))
                    pe.matmul(bank(6), w_d[:, 2 * D:3 * D], XT[:, :], start=True, stop=True).then_inc(d_q_ps, 1)
                    pe.wait_ge(d_q, 1)

                    def scores(b):
                        pe.wait_ge(d_blk, b + 1)
                        for g in range(4):
                            if b:
                                pe.wait_ge(d_ss, 4 * (b - 1) + g + 1)
                            o = 32 * g
                            pe.matmul(bank(g), qT[o:o + 32, b, :], BLK[o:o + 32, b % 2].rearrange("p h t -> p (h t)"),
                                      start=True, stop=True).then_inc(d_s_ps, 1)

                    def values(b):
                        pe.wait_ge(d_exp, b + 1)
                        for g in range(4):
                            n = 4 * b + g
                            if n >= 2:
                                pe.wait_ge(d_pT, n - 1)
                            for h in range(4):
                                ins = pe.transpose(BK[:, 4 + n % 2, h * P:(h + 1) * P], SS[:, b % 2, 4 * g + h, :], ident[:, :])
                            ins.then_inc(d_pT_ps, 1)
                        pe.wait_ge(d_pT, 4 * b + 4)
                        if b:
                            pe.wait_ge(d_om, b)
                        for dst, w in ((6, None), (7, ones)):
                            for g in range(4):
                                o = 32 * g
                                lhs = vd[:, b, o:o + 32] if w is None else ones[:, 0:32]
                                ins = pe.matmul(BK[o:o + 32, dst, :], lhs,
                                                PT[:, b % 2, 4 * g:4 * g + 4, :].rearrange("p h t -> p (h t)"),
                                                start=True, stop=True)
                        ins.then_inc(d_o_ps, 1)

                    scores(0)
                    for b in range(B):
                        if b + 1 < B:
                            scores(b + 1)
                        values(b)
                    pe.wait_ge(d_om, 4)
                    with pe.If(flagged(pe, flag_d, FDI)):
                        pe.sem_inc(gd_kv_ps, 1)
                        pe.sem_inc(gd_s_ps, 1)
                        pe.wait_ge(gd_m0, 2)
                        with pe.Fori(0, B) as b:
                            with pe.Fori(0, S2 // P) as c:
                                it = b * (S2 // P) + c
                                pe.wait_ge(gd_in, it * 16 + 16)
                                pe.wait_ge(gd_k, 1 + it)
                                pe.wait_ge(gd_v, 1 + it)
                                pe.wait_ge(gd_oT, 1 + b)
                                pe.matmul(BK[:, 0, 0:P], w_d[:, 0:D], GC, start=True, stop=True)
                                pe.matmul(BK[:, 1, 0:P], GC, w_d[:, D:2 * D], start=True, stop=True).then_inc(gd_kv_ps, 1)
                            with pe.Fori(0, H) as h:
                                it = b * H + h
                                pe.wait_ge(gd_k, 1 + b * (S2 // P) + S2 // P)
                                pe.wait_ge(gd_v, 1 + b * (S2 // P) + S2 // P)
                                pe.wait_ge(gd_q, it + 1)
                                pe.wait_ge(gd_o, 1 + it)
                                for j in range(4):
                                    ins = pe.matmul(bank(j), GQ, GK[:, j * 512:(j + 1) * 512], start=True, stop=True)
                                ins.then_inc(gd_s_ps, 1)
                                pe.wait_ge(gd_exp, it + 1)
                                for c in range(S2 // P):
                                    ins = pe.transpose(BK[:, 4 + c // 4, c % 4 * P:c % 4 * P + P], GSC[:, c * P:(c + 1) * P],
                                                       ident[:, :])
                                    if c % 4 == 3:
                                        ins.then_inc(gd_tr, 1)
                                pe.wait_ge(gd_p, 4 * it + 4)
                                for c in range(S2 // P):
                                    ins = pe.matmul(BK[:, 0, 0:D], GP[:, c, :], GV[:, c, :], start=(c == 0),
                                                    stop=(c == S2 // P - 1))
                                ins.then_inc(gd_o_ps, 1)
                            pe.wait_ge(gd_o, 1 + b * H + H)
                            pe.transpose(BK[:, 1, 0:P], GO, ident[:, :]).then_inc(gd_oT_ps, 1)
                        pe.wait_ge(gd_oT, 1 + B)
                    project(w_d[:, 3 * D:4 * D])
                if s == "E":
                    pe.wait_ge(l_silu, 1)
                    transposes(HH, 7, l_hT_ps)
                    pe.wait_ge(l_hT, 1)
                    pe.wait_ge(loads["w_e"], 48)
                    for b in range(B):
                        ins = pe.matmul(BK[:, b, 0:384], XT[:, b * P:(b + 1) * P], w_e[:, 0:384], start=True, stop=True)
                    ins.then_inc(l_qkv_ps, 1)
                    pe.wait_ge(ctx_ready, len([q for q in stages if q in "AE"]))
                    transposes(CT, 7, ctxT_ps)
                    pe.wait_ge(ctxT_ready, len([q for q in stages if q in "AE"]))
                    project(w_e[:, 384:512], 6)
                    pe.wait_ge(l_h2, 1)
                    transposes(XH, 5, ln_xT_ps)
                    pe.wait_ge(ln_xT, xT_count(LN_E2))
                    for c in range(2):
                        for j, (o, w) in enumerate(FFT):
                            bk = j if c == 0 else (3, 4, 6)[j]
                            pe.matmul(BK[0:w, bk, :], w_e[:, 512 + FF * c + o:512 + FF * c + o + w], XT[:, :],
                                      start=True, stop=True).then_inc(l_ff_ps, 1)
                    pe.wait_ge(l_ff, 3)
                    for b in range(B):
                        for j, (o, w) in enumerate(FFT):
                            ins = pe.matmul(BK[:, 7, b * P:(b + 1) * P], HF[0:w, j, b * P:(b + 1) * P], w_e2[0:w, j, :],
                                            start=(j == 0), stop=(j == 2))
                    ins.then_inc(proj_ps, 1)


_OUT = ((P, B, D), "float32")


def kernel(**inputs):
    import concourse.bacc as bacc
    from concourse.bass_utils import run_bass_kernel_spmd

    nc = bacc.Bacc("TRN2", target_bir_lowering=False, num_devices=1)
    arrays = layouts(inputs)
    t = {n: nc.dram_tensor(n + "_dram", a.shape, mybir.dt.from_np(a.dtype), kind="ExternalInput").ap()
         for n, a in arrays.items()}
    out = nc.dram_tensor("out_dram", (P, B, D), F32, kind="ExternalOutput").ap()
    program(nc, t, out)
    r = run_bass_kernel_spmd(nc, [{n + "_dram": a for n, a in arrays.items()}], core_ids=[0])
    return np.ascontiguousarray(r.results[0]["out_dram"].transpose(1, 0, 2))
```

```python
from contextlib import ExitStack

import concourse.bass as bass
import numpy as np
from concourse import mybir

F32 = mybir.dt.float32
BF16 = mybir.dt.bfloat16
I32 = mybir.dt.int32
ALU = mybir.AluOpType
ACT = mybir.ActivationFunctionType
AX = mybir.AxisListType
RMAX = bass.bass_isa.ReduceOp.max

P = 128
B = 4
D = 128
S2 = 2048
H = 16
HD = D // H
NK = 5
E1 = H * NK
QH = 64
NE = 8
HID0 = 256
HID1 = 512
FF = 352
FFT = [(0, 128), (128, 128), (256, 96)]
EPS = 1e-5
NEG = -1e9
KEPT = 3e38
TOK = B * P
SAMPLE_AT = 4
BACK_AT = (10, 13, 16, 19)
LN_A, LN_B, LN_C, LN_D, LN_E0, LN_E1, LN_E2, LN_F = range(8)


def bf16_bits(a):
    return (np.ascontiguousarray(a).view(np.uint32) >> 16).astype(np.uint16)


def constants():
    c = {}
    c["c_ident"] = np.eye(P, dtype=np.float32)
    m = np.arange(P)
    coord = np.stack([np.where(m < 32, m - 33, m - 32), m + 32])
    sel = np.zeros((99, 32, P), np.float32)
    for i in range(32):
        sel[[i, 32 + i, 64 + i], i, :] = 1.0
    sel[96:98] = -coord[:, None, :]
    sel[98] = -0.5
    half = np.zeros((3, 3, B, 2, QH), np.float32)
    half[0, :, :, 0] = half[1, :, :, 1] = half[2] = 1.0
    c["c_sel"] = bf16_bits(sel)
    c["c_half"] = bf16_bits(half.reshape(3, 3, TOK))
    e = 32 * np.arange(3)[None, :] + (np.arange(96) % 32)[:, None]
    c["c_ref"] = np.where(e < E1, e % NK - 3, 0).astype(np.float32)
    q = np.arange(P)
    c["c_loc"] = np.ascontiguousarray(np.broadcast_to(q, (96, P))).astype(np.float32)
    c["c_mid"] = np.ascontiguousarray(np.broadcast_to(q // QH * QH + 31.5, (96, P))).astype(np.float32)
    inv = 1.0 / 10000.0 ** (np.arange(0, HD, 2, dtype=np.float32) / np.float32(HD))
    fr = np.arange(P, dtype=np.float32)[:, None] * inv[None, :].astype(np.float32)
    emb = np.concatenate([fr, fr], 1).astype(np.float32)
    cos, sin = np.cos(emb), np.sin(emb) * np.where(np.arange(HD) < HD // 2, -1, 1)
    cosT, sinT = np.tile(cos.T, (H, 1)), np.tile(sin.T, (H, 1))
    sc = 1.0 / np.sqrt(HD)
    c["c_rope0"] = np.stack([cosT * sc, sinT * sc, cosT, sinT], 1).astype(np.float32)
    gam = 1.0 - 2.0 ** (-5.0 - np.arange(H, dtype=np.float32))
    dist = np.arange(P)[None, :] - np.arange(P)[:, None]
    dec = np.where(dist[:, None] >= 0, gam[None, :, None].astype(np.float64) ** np.maximum(dist, 0)[:, None], 0.0)
    c["c_decay"] = dec.astype(np.float32)
    c["c_pos"] = -(P * np.arange(S2 // P)[None, :] + np.arange(P)[:, None]).astype(np.float32)
    c["c_head16"] = (np.arange(P)[:, None] // HD == np.arange(H)[None, :]).astype(np.float32)
    c["c_head"] = (np.arange(P)[:, None] // HD % 4 == np.arange(4)[None, :]).astype(np.float32)
    g = np.kron(np.eye(H), np.full((HD, HD), 1.0 / HD))
    c["c_group"] = np.stack([np.eye(P) - g, g], 1).astype(np.float32)
    hdk = 4
    inv = 1.0 / 10000.0 ** (np.arange(0, 2, dtype=np.float32) * 2.0 / hdk)
    fr = np.arange(B, dtype=np.float32)[:, None] * inv[None, :].astype(np.float32)
    t = np.zeros((2, B, 2, H, 2, 2), np.float32)
    t[0] = np.cos(fr)[:, None, None, None, :]
    t[1, ..., 0, :] = -np.sin(fr)[:, None, None, :]
    t[1, ..., 1, :] = np.sin(fr)[:, None, None, :]
    t[:, :, 0] *= hdk ** -0.5
    causal = np.broadcast_to((np.arange(B)[:, None] >= np.arange(B)[None, :])[:, :, None], (B, B, H))
    tri = np.arange(NE)[:, None] > np.arange(NE)[None, :]
    c["c_rows"] = np.concatenate([t.reshape(-1), causal.reshape(-1), tri.reshape(-1)]).astype(np.float32)[None]
    return c


ROWS = {}
_at = 0
for _n, _w in (("bkv", 256), ("bq", D), ("bo", D), ("ff_bo", D), ("x_bv", D), ("x_bo", D), ("ln1_w", D),
               ("ln1_b", D), ("ln2_w", D), ("ln2_b", D), ("conv0", D), ("conv1", D), ("rw", 2 * D)):
    ROWS[_n] = slice(_at, _at + _w)
    _at += _w
NROWS = _at
EARLY = ROWS["bo"].stop
ROPE1 = slice(0, 1024)
CAUSAL1 = slice(1024, 1280)
BEFORE = slice(1280, 1344)
COLS = {n: i for i, n in enumerate(
    ["bq", "gn_w", "gn_b", "x_bq", "x_bk", "eps"])}
B1COL = len(COLS)
NCOLS = B1COL + NE * 4


def layouts(i):
    f = lambda n: np.asarray(i[n])
    a = {}
    a["x"] = f("x").transpose(1, 0, 2)
    ctxT = f("ctx_1024").transpose(2, 0, 1)
    a["ctxT"] = ctxT
    a["mask_b"] = f("mask_BxS2_if0").astype(np.int32)
    a["mask_q"] = f("mask_1x1xSxS2_ik0")[0, 0].astype(np.int32)
    wk = f("L0_xattn_Wk").T.reshape(D, H, 1, HD)
    wv = f("L0_xattn_Wv").T.reshape(D, H, 1, HD)
    wkv = np.concatenate([wk, wv], 2).reshape(D, 2 * D)
    woff = np.concatenate([f("L0_xattn_Woff").T, np.zeros((D, 16), np.float32)], 1).reshape(D, 3, 1, 32)
    woff = np.broadcast_to(woff, (D, 3, 3, 32)).reshape(D, 288)
    a["w_a"] = np.concatenate([wkv, f("L0_xattn_Wq").T, woff, f("L0_xattn_Wo").T], 1)
    boff = np.concatenate([f("L0_xattn_boff"), np.zeros(16, np.float32)]).reshape(3, 1, 32)
    a["boff"] = np.broadcast_to(boff, (3, 3, 32)).reshape(3, 96).T
    rot = lambda w: w.T.reshape(D, H, 2, HD // 2)[:, :, ::-1].reshape(D, D)
    a["w_b"] = np.concatenate([f("L0_attn_Wq").T, rot(f("L0_attn_Wq")), f("L0_attn_Wk").T, rot(f("L0_attn_Wk")),
                               f("L0_attn_Wv").T, f("L0_attn_Wo").T], 1)
    a["w_c"] = np.concatenate([f("L0_ffn_Wg").T, f("L0_ffn_Wo").T.reshape(2, P, D).transpose(1, 0, 2).reshape(P, 2 * D)], 1)
    a["w_c1"] = f("L0_ffn_W1").transpose(2, 0, 1).reshape(D, NE * 2 * HID0)
    a["w_d"] = np.concatenate([f("L1_xattn_W" + n).T for n in "kvqo"], 1)
    a["w_e"] = np.concatenate([f("L1_attn_W" + n) for n in ("q", "k", "v", "g", "out")] + [f("L1_attn_w1"), f("L1_attn_w3")], 1)
    w2 = np.concatenate([f("L1_attn_w2"), np.zeros((3 * P - FF, D), np.float32)]).reshape(3, P, D)
    a["w_e2"] = w2.transpose(1, 0, 2)
    a["w_f"] = f("L1_ffn_router_w").T
    a["w_f1"] = f("L1_ffn_w1").transpose(1, 0, 2).reshape(D, NE * HID1)
    a["w_f2"] = f("L1_ffn_w2").reshape(NE, 4, P, D).transpose(2, 0, 1, 3).reshape(P, NE * 4 * D)
    bkv = np.concatenate([f("L0_xattn_bk").reshape(H, 1, HD), f("L0_xattn_bv").reshape(H, 1, HD)], 1)
    cw = f("L1_attn_conv_w").T
    a["rows"] = np.concatenate([bkv.reshape(-1), f("L0_xattn_bq"), f("L0_xattn_bo"), f("L0_ffn_bo"), f("L1_xattn_bv"), f("L1_xattn_bo"),
                                f("L1_attn_ln1_w"), f("L1_attn_ln1_b"), f("L1_attn_ln2_w"), f("L1_attn_ln2_b"),
                                cw[0], cw[1], f("L1_attn_router_w").transpose(2, 0, 1).reshape(-1)])[None]
    cols = [f("L0_xattn_bq"), f("L0_attn_gn_weight"), f("L0_attn_gn_bias"), f("L1_xattn_bq"), f("L1_xattn_bk"),
            np.full(D, EPS, np.float32)]
    a["cols"] = np.concatenate([np.stack(cols, 1), f("L0_ffn_b1").reshape(NE * 4, P).T], 1)
    a.update(constants())
    return {k: np.ascontiguousarray(v) for k, v in a.items()}


def program(nc, t, out, stages="ABCDEF", general=False):
    ctx = ExitStack()
    with ctx:
        def sb(name, shape, dt=F32):
            return ctx.enter_context(nc.sbuf_tensor(name, shape, dt))

        def sem(name):
            return ctx.enter_context(nc.semaphore(name))

        FLA = sb("FLA", [P, 2])
        FLD = sb("FLD", [P, 2])
        GNA = sb("GNA", [P, 2])
        FAI = sb("FAI", [1, 1], I32)
        FDI = sb("FDI", [1, 1], I32)
        VM3 = sb("VM3", [96, 3])
        MKB = sb("MKB", [P, B, S2 // P], I32)
        pos = sb("pos_sb", [P, S2 // P])
        head16 = sb("head16_sb", [P, H])
        X = sb("X", [P, B, D])
        XH = sb("XH", [P, B, D])
        XT = sb("XT", [P, TOK])
        XB = sb("XB", [P, B, D])
        STAT = sb("STAT", [P, B, 6])
        MV = sb("MV", [P, B, 2])
        VE = sb("VE", [P, B])
        RSTD = sb("RSTD", [P, B])
        MHALF = sb("MHALF", [P, B])
        ident = sb("ident", [P, P])
        rows = sb("rows_sb", [P, NROWS])
        crows = sb("crows_sb", [P, 1344])
        cols = sb("cols_sb", [P, NCOLS])
        head = sb("head_sb", [P, 4])
        row = lambda n: rows[:, ROWS[n]]
        col = lambda n: cols[:, COLS[n]:COLS[n] + 1]
        w_a = sb("w_a_sb", [P, 256 + D + 288 + D])
        w_b = sb("w_b_sb", [P, 6 * D])
        w_c = sb("w_c_sb", [P, 8 + 2 * D])
        w_d = sb("w_d_sb", [P, 4 * D])
        w_e = sb("w_e_sb", [P, 512 + 2 * FF])
        w_e2 = sb("w_e2_sb", [P, 3, D])
        w_f = sb("w_f_sb", [P, 8])
        def room(tile, width):
            at = [0]

            def take(shape):
                n = int(np.prod(shape[1:]))
                v = tile[:, at[0]:at[0] + n]
                at[0] += n
                assert at[0] <= width
                names = "abcd"[:len(shape) - 1]
                return v.rearrange(f"p ({' '.join(names)}) -> p {' '.join(names)}", **dict(zip(names, shape[1:])))

            return take

        SCR = sb("SCR", [P, 5120])
        before_b = room(SCR, 5120)
        KVW = sb("KVW", [P, 2 * B, 2 * D + 16])
        boff = sb("boff_sb", [96, 3])
        refc = sb("refc", [96, 3])
        ybias = sb("ybias", [96, 3])
        loc = before_b([P, P])[0:96]
        mid = before_b([P, P])[0:96]
        QpT = before_b([P, TOK])
        Qq = before_b([P, B, D])
        Y = before_b([P, 3, TOK])[0:96]
        YW, YW2 = before_b([P, TOK])[0:96], before_b([P, TOK])[0:96]
        IX, IX2 = before_b([P, TOK])[0:96], before_b([P, TOK])[0:96]
        Rh2 = before_b([P, TOK // 2])[0:96].bitcast(BF16)
        Rh = sb("Rh", [96, TOK], BF16)
        R = sb("R", [99, 3, TOK], BF16)
        SELR = sb("SELR", [P, 2048])
        SEL = SELR[:, :].bitcast(BF16)[0:99].rearrange("p (e m) -> p e m", e=32)
        after_sel = room(SELR, 2048)
        WT = sb("WT", [P, 2, 4, 2 * B, NK, QH])
        KEEP = sb("KEEP", [P, 5120])

        WTF = WT[:, :, :, :, :, :].rearrange("p a h i k q -> p (a h i k q)")
        first = room(WTF, 20480)
        WIN = first([P, B, 192])
        ga = room(WTF, 20480)
        GCH = ga([P, P])
        GKV = ga([P, 2 * D + 16])
        GW = ga([P, 4, NK, P])
        GIX = ga([P, 3, TOK])[0:96]
        GT1 = ga([P, 3, TOK])[0:96]
        GSM = ga([P, 4, B])
        GPOS = ga([P, 1])
        gd = room(WTF, 12288)
        GK = gd([P, S2])
        GV = gd([P, S2 // P, D])
        GSC = gd([P, S2])
        GP = gd([P, S2 // P, P])
        GM = gd([P, S2])
        GMI = GM.bitcast(I32)
        GC = gd([P, P])
        GQ = gd([P, P])
        GO = gd([P, D])
        GR = gd([P, 4])
        later = room(WTF, 20480)
        PT = later([P, 2, H, P])
        keep = room(KEEP, 5120)
        after = room(KEEP, 5120)
        w_c1 = later([P, NE * 2 * HID0])
        after_c = room(w_c1, 4096)
        after_a = room(SCR, 5120)
        GT = later([P, 2, 4, TOK])
        w_f1 = later([P, NE * HID1])
        w_f2 = later([P, NE * 4 * D])
        early = room(KEEP[:, B * NK * P:5120], 5120 - B * NK * P)
        TAIL = early([P, B, P])
        MKF = early([P, S2]).bitcast(I32)
        SK = keep([P, B, NK, P])
        PRD = sb("PRD", [P, NK, 4, HD])
        SCO = sb("SCO", [P, B, H, NK])
        GSK = SK.rearrange("p b k q -> p b (k q)")
        VS = keep([P, B, H, NK * HD]).rearrange("p b h (k d) -> p b h k d", k=NK)
        PV = WTF[:, 0:B * H * NK * HD].rearrange("p (b h k d) -> p b h k d", b=B, h=H, k=NK)
        SM1 = sb("SM1", [P, B, H])
        SM2 = sb("SM2", [P, B, H])
        CT = sb("CT", [P, B, D])
        CTT = sb("CTT", [P, TOK])
        rope0 = sb("rope0", [P, 4, P])
        group = sb("group_sb", [P, 2, P])
        decay = sb("decay", [P, H, P])
        T0 = after([P, B, P])
        T1 = after([P, B, P])
        qT = after([P, B, P])
        kT = after([P, B, P])
        vq = after([P, B, P])
        BLK = after([P, 2, 4, P])
        OM = after([P, 4, P])
        PR = sb("PR", [P, B, NE])
        EX = sb("EX", [P, B, NE])
        CMP = after_sel([P, B, NE, NE])
        CMQ = after_sel([P, B, NE, NE])
        RK = sb("RK", [P, B, NE])
        S1 = sb("S1", [P, B])
        CW = sb("CW", [P, B, NE])
        SG = room(KVW[:, :, :].rearrange("p i n -> p (i n)"), 2176)([P, 2, 2, TOK])
        PO = SG.rearrange("p a j n -> p (a j n)").rearrange("p (l m n) -> p l m n", l=B, m=B)
        mtail = sb("mtail", [P, P], I32)
        MB = sb("MB", [P, P])
        kTd = sb("kTd", [P, B, P])
        vd = sb("vd", [P, B, P])
        SS = GT.rearrange("p a j n -> p (a j n)").rearrange("p (a h k) -> p a h k", a=2, h=H)
        MX = sb("MX", [P, B, H])
        ones = sb("ones", [P, P])
        DN = after([P, 4, P])
        XN = after_c([P, B, D])
        HH = after_c([P, B, D])
        HP = after_c([P, B, D])
        QK = after_a([P, B, 2, 64])
        QR = after_a([P, B, 2, 64])
        Q2 = after_a([P, B, 2, 64])
        VV = after_c([P, B, D])
        GS = after_c([P, B, D])
        LGT = sb("LGT", [P, 2, B, H])
        LGE = sb("LGE", [P, 2, B, H])
        LP = after_a([P, 2, B, D])
        OH = sb("OH", [P, B, H])
        SMM = after_a([P, B, B, H])
        DT = after_a([P, B, B, H])
        PDT = LP.rearrange("p r b n -> p (r b n)").rearrange("p (l m n) -> p l m n", l=B, m=B)
        OO = after_c([P, B, D])
        OQ = after_c([P, B, D])
        HF = room(decay[:, :, :].rearrange("p h t -> p (h t)"), 2048)([P, 3, TOK])

        BK = ctx.enter_context(nc.psum_tensor("BK", [P, 8, 512], F32))
        bank = lambda i: BK[:, i, :]

        loads = {n: sem("in_" + n) for n in (
            "x", "ident", "rows", "crows", "cols", "w_a", "win", "tail", "pos", "sel", "w_b", "w_c",
            "w_c1", "w_d", "w_e", "w_f1", "w_f2", "decay", "flags")}
        dve_chain = sem("dve_chain")
        act_chain = sem("act_chain")
        pool_chain = sem("pool_chain")
        ln_var, ln_rstd, ln_xhat = sem("ln_var"), sem("ln_rstd"), sem("ln_xhat")
        ln_xT_ps, ln_xT = sem("ln_xT_ps"), sem("ln_xT")
        consts_ready = sem("consts_ready")
        kvw_ps, kvw_ready = sem("kvw_ps"), sem("kvw_ready")
        kd_ps, kd_ready, vd_ready = sem("kd_ps"), sem("kd_ready"), sem("vd_ready")
        a_q_ps, a_qT, a_qq, a_off_ps, a_y, a_r = (sem("a_" + n) for n in ("q_ps", "qT", "qq", "off_ps", "y", "r"))
        a_ix_ps, a_abs, a_w = sem("a_ix_ps"), sem("a_abs"), sem("a_w")
        a_samp_ps, a_sk, a_tr_ps, a_prod, a_vs = (sem("a_" + n) for n in ("samp_ps", "sk", "tr_ps", "prod", "vs"))
        a_z, a_exp, a_dev, a_sco = (sem("a_" + n) for n in ("z", "exp", "dev", "sco"))
        ctx_ready, ctxT_ps, ctxT_ready, proj_ps = (sem(n) for n in ("ctx_ready", "ctxT_ps", "ctxT_ready", "proj_ps"))
        xb_ready, x_ready = sem("xb_ready"), sem("x_ready")
        b_qk_ps, b_v_ps, b_rot, b_v = (sem("b_" + n) for n in ("qk_ps", "v_ps", "rot", "v"))
        b_blk, b_s_ps, b_pt, b_o_ps, b_oT, b_oc_ps = (sem("b_" + n) for n in ("blk", "s_ps", "pt", "o_ps", "oT", "oc_ps"))
        b_sq, b_var_ps, b_std, b_on = (sem("b_" + n) for n in ("sq", "var_ps", "std", "on"))
        r_lg_ps, r_z, r_exp, r_cw = (sem("r_" + n) for n in ("lg_ps", "z", "exp", "cw"))
        e_h_ps, e_act, e_g, e_y_ps, e_sum = (sem("e_" + n) for n in ("h_ps", "act", "g", "y_ps", "sum"))
        d_mb, d_q_ps, d_q, d_blk, d_s_ps, d_ss, d_mx, d_sub, d_exp = (
            sem("d_" + n) for n in ("mb", "q_ps", "q", "blk", "s_ps", "ss", "mx", "sub", "exp"))
        d_pT_ps, d_pT, d_o_ps, d_om = (sem("d_" + n) for n in ("pT_ps", "pT", "o_ps", "om"))
        l_hc, l_silu, l_hT_ps, l_hT, l_qkv_ps, l_vkqg = (
            sem("l_" + n) for n in ("hc", "silu", "hT_ps", "hT", "qkv_ps", "vkqg"))
        l_ld, l_le, l_oc, l_sq, l_vs, l_std, l_h2, l_ff_ps, l_ffs, l_ff, l_xa = (
            sem("l_" + n) for n in ("ld", "le", "oc", "sq", "vs", "std", "h2", "ff_ps", "ffs", "ff", "xa"))
        l_hp, l_h1 = sem("l_hp"), sem("l_h1")
        flag_rows, flag_all, flag_a, flag_d = (sem("flag_" + n) for n in ("rows", "all", "a", "d"))
        ga_chain = sem("ga_chain")
        ga_in, ga_sum_ps, ga_pos, ga_ix, ga_abs, ga_w, ga_kv_ps, ga_kv = (
            sem("ga_" + n) for n in ("in", "sum_ps", "pos", "ix", "abs", "w", "kv_ps", "kv"))
        ga_samp, ga_add, ga_zero, ga_tr, ga_prod, ga_out = (
            sem("ga_" + n) for n in ("samp", "add", "zero", "tr", "prod", "out"))
        gd_in, gd_mask, gd_m0, gd_kv_ps, gd_k, gd_v = (sem("gd_" + n) for n in ("in", "mask", "m0", "kv_ps", "k", "v"))
        gd_q, gd_s_ps, gd_chain, gd_neg, gd_exp, gd_tr, gd_p, gd_o_ps, gd_o, gd_oT_ps, gd_oT = (
            sem("gd_" + n) for n in ("q", "s_ps", "chain", "neg", "exp", "tr", "p", "o_ps", "o", "oT_ps", "oT"))
        stored = sem("stored")

        PROJ = [s for s in "ABDE" if s in stages]
        BIASED = [s for s in "ADE" if s in stages]
        FFNS = [s for s in "CF" if s in stages]
        CTXT = [s for s in "AE" if s in stages]
        nx = {s: i for i, s in enumerate(stages)}

        def stages_done(eng, n):
            before = stages[:n]
            if before[-1] in "CF":
                eng.wait_ge(e_sum, NE * len([q for q in before if q in "CF"]))
            else:
                eng.wait_ge(x_ready, len([q for q in before if q not in "CF"]))

        block = ctx.enter_context(nc.Block())

        def flagged(eng, ready, tile):
            eng.wait_ge(ready, 1)
            return eng.value_load(tile[0:1, 0:1]) != 0

        lns = [n for n, q in enumerate("ABCDEEEF") if q in stages]
        transposed = [n for n in lns if n not in (LN_E0, LN_E1)]
        xhat_count = lambda n: 4 * lns.index(n) + 4
        xT_count = lambda n: transposed.index(n) + 1

        def vcopy(act, u):
            G, b = u // 4, u % 4
            act.wait_ge(a_prod, u + 1)
            src = BK[:, 5:7, :].rearrange("p a n -> p (a n)")[:, 0:NK * P].rearrange("p (k h r) -> p h k r", k=NK, h=4)
            act.activation(VS[:, b, 4 * G:4 * G + 4, :, :], src[:, :, :, HD:2 * HD], ACT.Copy).then_inc(a_vs, 1)

        sbank = lambda e: bank((0, 1, 2, 7)[e % 4])
        TAIL_AT = 14

        HBANKS = (0, 1, 2, 3, 6, 7)
        hbank = lambda u: bank(HBANKS[u % 6])
        PAIRS = 2 * NE
        before_f = PAIRS if "C" in stages else 0

        loaded = {'ident':16,'pos':64,'rows':16,'crows':16,'sel':32,'decay':48}
        @block.sync
        def _(sp):
            def load(dst, src, s):
                loaded[s] = loaded.get(s, 0) + 16
                sp.dma_start(dst, src).then_inc(loads[s], 16)

            load(X[:, :, :], t["x"], "x")
            load(w_a[:, :], t["w_a"], "w_a")
            load(WIN[:, :, 0:32], t["ctxT"][:, :, S2 - 32:S2], "win")
            load(WIN[:, :, 32:192], t["ctxT"][:, :, 0:160], "win")
            load(cols[:, :], t["cols"], "cols")
            load(w_d[:, :], t["w_d"], "w_d")
            load(TAIL[:, :, :], t["ctxT"][:, :, S2 - P:S2], "tail")
            load(rows[:, EARLY:], t["rows"][:, EARLY:].to_broadcast([P, NROWS - EARLY]), "crows")
            load(MKF, t["mask_q"], "flags")
            load(MKB[:, :, :], t["mask_b"].rearrange("b (p j) -> p b j", p=P), "flags")
            load(pos[:, :], t["c_pos"], "flags")
            load(head16[:, :], t["c_head16"], "flags")
            load(mtail[:, :], t["mask_q"][:, S2 - P:S2], "flags")
            load(w_b[:, :], t["w_b"], "w_b")
            load(head[:, :], t["c_head"], "decay")
            load(w_c[:, :], t["w_c"], "w_c")
            load(w_e[:, :], t["w_e"], "w_e")
            load(w_e2[:, :, :], t["w_e2"], "w_e")
            load(w_f[:, :], t["w_f"], "w_e")
            if "A" in stages:
                with sp.If(flagged(sp, flag_a, FAI)):
                    with sp.Fori(0, B) as b:
                        with sp.Fori(0, S2 // P) as c:
                            sp.wait_ge(ga_kv_ps, 1 + b * (S2 // P) + c)
                            sp.dma_start(GCH, t["ctxT"][:, bass.ds(b, 1), bass.ds(c * P, P)].rearrange("p b n -> p (b n)"))\
                              .then_inc(ga_in, 16)
                    sp.wait_ge(ga_out, 1 + 4 * B)
                sp.wait_ge(a_z, 1)
            else:
                sp.wait_ge(kd_ps, 2)
            sp.wait_ge(flag_d, 1)
            if "C" in stages:
                load(w_c1, t["w_c1"], "w_c1")
            if "F" in stages:
                load(w_f1, t["w_f1"], "w_f1")
                load(w_f2, t["w_f2"], "w_f2")
            if "D" in stages:
                with sp.If(flagged(sp, flag_d, FDI)):
                    sp.wait_ge(d_om, B)
                    sp.dma_start(GMI, t["mask_q"]).then_inc(gd_mask, 16)
                    with sp.Fori(0, B) as b:
                        with sp.Fori(0, S2 // P) as c:
                            sp.wait_ge(gd_kv_ps, 1 + b * (S2 // P) + c)
                            sp.dma_start(GC, t["ctxT"][:, bass.ds(b, 1), bass.ds(c * P, P)].rearrange("p b n -> p (b n)"))\
                              .then_inc(gd_in, 16)
            stages_done(sp, len(stages))
            sp.dma_start(out, X[:, :, :]).then_inc(stored, 16)
            sp.wait_ge(stored, 16)
            if len(stages) < 6:
                for q, v in loaded.items():
                    sp.wait_ge(loads[q], v)

        @block.gpsimd
        def _(pool):
            chain = [0]

            def settle(ins):
                chain[0] += 1
                ins.then_inc(pool_chain, 1)
                pool.wait_ge(pool_chain, chain[0])

            pool.memset(MHALF[:, :], -0.5).then_inc(consts_ready, 1)
            pool.memset(KVW[:, :, 2 * D:2 * D + 16], 0.0).then_inc(consts_ready, 1)
            pool.memset(ones[:, :], 1.0).then_inc(consts_ready, 1)
            pool.wait_ge(consts_ready, 3)

            def power(n):
                pool.wait_ge(ln_var, lns.index(n) + 1)
                pool.tensor_tensor(RSTD[:, :], VE[:, :], MHALF[:, :], ALU.pow).then_inc(ln_rstd, 1)

            def with_bias(n, name):
                stages_done(pool, n) if n else pool.wait_ge(loads["x"], 16)
                pool.wait_ge(loads["rows"], 16) if name == "bo" else pool.wait_ge(loads["crows"], 32)
                pool.tensor_tensor(XB[:, :, :], X[:, :, :], row(name).unsqueeze(1).to_broadcast([P, B, D]),
                                   ALU.add).then_inc(xb_ready, 1)

            def tail():
                pool.wait_ge(flag_rows, 1)
                pool.partition_all_reduce(FLD[:, 1:2], FLD[:, 0:1], P, RMAX).then_inc(flag_all, 1)

            if stages[0] == "A":
                power(LN_A)
            else:
                tail()
            for s in stages:
                if s == "A":
                    for g in (1, 2):
                        pool.wait_ge(a_y, g)
                        settle(pool.tensor_scalar(YW2[:, :], Y[:, g, :], 0.0, -1.0, ALU.is_lt, ALU.mult))
                        settle(pool.tensor_scalar(IX2[:, :], Y[:, g, :], float(S2) / (S2 - 1), None, ALU.mult))
                        settle(pool.tensor_tensor(IX2[:, :], IX2[:, :], YW2[:, :], ALU.add))
                        if g == 1:
                            pool.wait_ge(loads["sel"], 32)
                        settle(pool.tensor_copy(R[0:96, g, :], IX2[:, :]))
                        settle(pool.tensor_tensor(IX2[:, :], IX2[:, :], R[0:96, g, :], ALU.subtract))
                        settle(pool.tensor_copy(Rh2[:, :], IX2[:, :]))
                        settle(pool.tensor_tensor(YW2[:, :], IX2[:, :], Rh2[:, :], ALU.subtract))
                        settle(pool.tensor_copy(R[32:64, g, :], Rh2[32:64, :]))
                        pool.tensor_copy(R[64:96, g, :], YW2[64:96, :]).then_inc(a_r, 1)
                        pool.wait_ge(a_r, g + 1)
                    by_query = mid[:, :].unsqueeze(1).to_broadcast([96, B, P])
                    for g, dst in ((1, YW2), (2, IX2)):
                        ins = pool.tensor_tensor(dst.rearrange("p (b q) -> p b q", b=B),
                                                 Y[:, g, :].rearrange("p (b q) -> p b q", b=B), by_query, ALU.subtract)
                        ins.then_inc(a_dev, 1)
                        pool.wait_ge(a_dev, g)
                    tail()
                    with_bias(nx[s], "bo")
                    pool.wait_ge(flag_rows, 2)
                    pool.partition_all_reduce(FLA[:, 1:2], FLA[:, 0:1], P, RMAX).then_inc(flag_all, 1)
                if s == "B":
                    power(LN_B)
                if s in "CF":
                    power(LN_C if s == "C" else LN_F)
                if s == "D":
                    power(LN_D)
                    with_bias(nx[s], "x_bo")
                    for b in range(B):
                        pool.wait_ge(d_mx, b + 1)
                        ss = SS[:, b % 2]
                        pool.tensor_tensor(ss, ss, MX[:, b].unsqueeze(2).to_broadcast([P, H, P]),
                                           ALU.subtract).then_inc(d_sub, 1)
                if s == "E":
                    power(LN_E0)
                    power(LN_E1)
                    pool.wait_ge(l_h1, 1)
                    pool.tensor_tensor(HP[:, 0:3], HH[:, 0:3], row("conv0").unsqueeze(1).to_broadcast([P, 3, D]),
                                       ALU.mult).then_inc(l_hp, 1)
                    power(LN_E2)
                    pool.wait_ge(l_xa, 1)
                    pool.tensor_tensor(XB[:, :, :], X[:, :, :], CT[:, :, :], ALU.add).then_inc(xb_ready, 1)

        @block.scalar
        def _(act):
            chain = [0]

            def settle(ins):
                chain[0] += 1
                ins.then_inc(act_chain, 1)
                act.wait_ge(act_chain, chain[0])

            def load(dst, src, s):
                act.dma_start(dst, src).then_inc(loads[s], 16)

            load(ident[:, :], t["c_ident"], "ident")
            load(boff[:, :], t["boff"], "pos")
            load(refc[:, :], t["c_ref"], "pos")
            load(loc[:, :], t["c_loc"], "pos")
            load(mid[:, :], t["c_mid"], "pos")
            load(rows[:, 0:EARLY], t["rows"][:, 0:EARLY].to_broadcast([P, EARLY]), "rows")
            load(R[96:99, :, :], t["c_half"].bitcast(BF16), "sel")
            load(SEL[:, :, :], t["c_sel"].bitcast(BF16), "sel")
            load(rope0[:, :, :], t["c_rope0"], "decay")
            load(group[:, :, :], t["c_group"], "decay")
            load(decay[:, :, :], t["c_decay"], "decay")
            load(crows[:, :], t["c_rows"].to_broadcast([P, 1344]), "crows")

            def norm_T(n, bk):
                act.wait_ge(ln_xT_ps, xT_count(n))
                act.activation(XT[:, :], bank(bk), ACT.Copy).then_inc(ln_xT, 1)

            def ctx_T(s, bk):
                k = CTXT.index(s)
                act.wait_ge(ctxT_ps, k + 1)
                act.activation(CTT[:, :], bank(bk), ACT.Copy).then_inc(ctxT_ready, 1)

            def tail():
                act.wait_ge(kd_ps, 1)
                act.activation(kTd[:, :, :], bank(3), ACT.Identity, bias=col("x_bk")).then_inc(kd_ready, 1)

            act.wait_ge(loads["cols"], 16)
            if "A" not in stages:
                tail()
            for s in stages:
                if s == "A":
                    norm_T(LN_A, 5)
                    act.wait_ge(a_q_ps, 1)
                    act.activation(QpT[:, :], bank(6), ACT.Identity, bias=col("bq")).then_inc(a_qT, 1)
                    for e in range(E1):
                        G = e // 20
                        act.wait_ge(a_ix_ps, e + 1)
                        if G >= 2 and e % 20 == 0:
                            act.wait_ge(a_samp_ps, 8 * (G - 1))
                        act.activation(WT[:, G % 2, e % 20 // NK, :, e % NK, :], sbank(e), ACT.Abs)\
                           .then_inc(a_abs, 1)
                        if e == TAIL_AT:
                            tail()
                        if G and e % 20 + 1 in BACK_AT:
                            u = 4 * (G - 1) + BACK_AT.index(e % 20 + 1)
                            if u == 0:
                                act.wait_ge(kd_ps, 2)
                                act.wait_ge(flag_rows, 1)
                            vcopy(act, u)
                    for u in range(12, 16):
                        vcopy(act, u)
                    with act.If(flagged(act, flag_a, FAI)):
                        act.sem_inc(ga_abs, 1)
                        act.wait_ge(ga_pos, 1)
                        with act.Fori(0, B) as b:
                            with act.Fori(0, S2 // P) as c:
                                it = b * (S2 // P) + c
                                act.wait_ge(ga_kv, 1 + 2 * it + 2)
                                for e in range(E1):
                                    if e % 20 == 0:
                                        act.wait_ge(ga_samp, 1 + it * 4 + e // 20)
                                    act.wait_ge(ga_ix, it * E1 + e + 1)
                                    act.activation(GW[:, e % 20 // NK, e % NK, :], BK[:, 0, 0:P], ACT.Abs,
                                                   bias=GPOS).then_inc(ga_abs, 1)
                    act.wait_ge(a_z, 1)
                    act.activation(SCO[:, :, :, :], SCO[:, :, :, :], ACT.Exp).then_inc(a_exp, 1)
                    ctx_T("A", 6)
                if s == "B":
                    norm_T(LN_B, 7)
                    act.wait_ge(b_v_ps, 1)
                    act.activation(vq[:, :, :], bank(4), ACT.Copy).then_inc(b_v, 1)
                    act.wait_ge(b_oc_ps, 1)
                    act.activation(T0[:, :, :], bank(4), ACT.Square).then_inc(b_sq, 1)
                    act.wait_ge(b_var_ps, 1)
                    act.activation(T1[:, :, :], bank(5), ACT.Sqrt, bias=col("eps")).then_inc(b_std, 1)
                if s in "CF":
                    k = FFNS.index(s)
                    norm_T(LN_C if s == "C" else LN_F, 7)
                    act.wait_ge(r_z, k + 1)
                    act.activation(EX[:, :, :], EX[:, :, :], ACT.Exp).then_inc(r_exp, 1)
                    for e in range(NE):
                        n = k * NE + e
                        if s == "C":
                            for p in (2 * e, 2 * e + 1):
                                act.wait_ge(e_h_ps, p + 1)
                                if p >= 4:
                                    act.wait_ge(e_g, p - 3)
                                o = B1COL + 4 * e + 2 + p % 2
                                act.activation(SG[:, e % 2, p % 2, :], hbank(2 * p + 1), ACT.Sigmoid, bias=cols[:, o:o + 1])\
                                   .then_inc(e_act, 1)
                        else:
                            if e >= 2:
                                act.wait_ge(e_y_ps, n - 1)
                            for u in range(4 * e, 4 * e + 4):
                                act.wait_ge(e_h_ps, before_f + u + 1)
                                act.activation(GT[:, e % 2, u % 4, :], hbank(u), ACT.Gelu).then_inc(e_act, 1)
                if s == "D":
                    norm_T(LN_D, 7)
                    act.wait_ge(d_q_ps, 1)
                    act.activation(qT[:, :, :], bank(6), ACT.Identity, bias=col("x_bq")).then_inc(d_q, 1)
                    for b in range(B):
                        act.wait_ge(d_sub, b + 1)
                        act.activation(SS[:, b % 2], SS[:, b % 2], ACT.Exp).then_inc(d_exp, 1)
                        for g in range(4):
                            n = 4 * b + g
                            act.wait_ge(d_pT_ps, n + 1)
                            if b >= 2 and g == 0:
                                act.wait_ge(d_o_ps, b - 1)
                            act.activation(PT[:, b % 2, 4 * g:4 * g + 4, :], bank(4 + n % 2), ACT.Copy)\
                               .then_inc(d_pT, 1)
                    with act.If(flagged(act, flag_d, FDI)):
                        act.sem_inc(gd_k, 1)
                        act.wait_ge(d_om, B)
                        with act.Fori(0, B) as b:
                            with act.Fori(0, S2 // P) as c:
                                it = b * (S2 // P) + c
                                act.wait_ge(gd_kv_ps, 1 + it + 1)
                                act.activation(GK[:, bass.ds(c * P, P)], BK[:, 0, 0:P], ACT.Identity, bias=col("x_bk"))\
                                   .then_inc(gd_k, 1)
                            with act.Fori(0, H) as h:
                                it = b * H + h
                                act.wait_ge(gd_neg, it + 1)
                                act.activation(GSC, GSC, ACT.Exp, bias=GR[:, 0:1], accum_out=GR[:, 1:2]).then_inc(gd_exp, 1)
                                for j in range(4):
                                    act.wait_ge(gd_tr, 4 * it + j + 1)
                                    act.activation(GP[:, 4 * j:4 * j + 4, :], bank(4 + j), ACT.Copy).then_inc(gd_p, 1)
                if s == "E":
                    act.wait_ge(l_hc, 1)
                    act.activation(HH[:, :, :], HH[:, :, :], ACT.Silu).then_inc(l_silu, 1)
                    act.wait_ge(l_hT_ps, 1)
                    act.activation(XT[:, :], bank(7), ACT.Copy).then_inc(l_hT, 1)
                    act.wait_ge(l_qkv_ps, 1)
                    qkvg = BK[:, 0:4, :]
                    act.activation(VV[:, :, :], qkvg[:, :, 128:256], ACT.Copy).then_inc(l_vkqg, 1)
                    act.activation(QK[:, :, 1, :], qkvg[:, :, 64:128], ACT.Copy).then_inc(l_vkqg, 1)
                    act.activation(QK[:, :, 0, :], qkvg[:, :, 0:64], ACT.Silu).then_inc(l_vkqg, 1)
                    act.activation(GS[:, :, :], qkvg[:, :, 256:384], ACT.Silu).then_inc(l_vkqg, 1)
                    act.wait_ge(l_ld, 1)
                    act.activation(LGE[:, :, :, :], LGT[:, :, :, :], ACT.Exp).then_inc(l_le, 1)
                    act.wait_ge(l_oc, 1)
                    act.activation(OQ[:, :, :], OO[:, :, :], ACT.Square).then_inc(l_sq, 1)
                    act.wait_ge(l_vs, 1)
                    act.activation(SM2[:, :, :], SM1[:, :, :], ACT.Sqrt, bias=col("eps"), scale=1.0 / HD)\
                       .then_inc(l_std, 1)
                    ctx_T("E", 7)
                    norm_T(LN_E2, 5)
                    for j, (o, w) in enumerate(FFT):
                        act.wait_ge(l_ff_ps, j + 1)
                        act.activation(HF[0:w, j, :], BK[0:w, j, :], ACT.Silu).then_inc(l_ffs, 1)

        @block.vector
        def _(dve):
            chain = [0]

            def settle(ins):
                chain[0] += 1
                ins.then_inc(dve_chain, 1)
                dve.wait_ge(dve_chain, chain[0])

            def stats(n, src):
                for b in range(B):
                    ins = dve.bn_stats(STAT[:, b, :], src[:, b, :])
                settle(ins)
                for b in range(B):
                    ins = dve.bn_aggr(MV[:, b, :], STAT[:, b, :])
                settle(ins)
                dve.tensor_scalar(VE[:, :], MV[:, :, 1], EPS, None, ALU.add).then_inc(ln_var, 1)

            def norm(n, src, dst, final=True):
                dve.wait_ge(ln_rstd, lns.index(n) + 1)
                for b in range(B):
                    ins = dve.tensor_scalar(dst[:, b, :], src[:, b, :], MV[:, b, 0:1], RSTD[:, b:b + 1],
                                            ALU.subtract, ALU.mult)
                    if final:
                        ins.then_inc(ln_xhat, 1)
                if final:
                    dve.wait_ge(ln_xhat, xhat_count(n))
                else:
                    settle(ins)

            def residual(s, other):
                k = PROJ.index(s)
                dve.wait_ge(proj_ps, k + 1)
                dve.tensor_tensor(X[:, :, :], bank(7), other, ALU.add).then_inc(x_ready, 1)
                stages_done(dve, nx[s] + 1)

            def over(ap, n, axis=1):
                v = ap.unsqueeze(axis)
                shape = list(v.shape)
                shape[axis] = n
                return v.to_broadcast(shape)

            dve.wait_ge(loads["x"], 16)
            if stages[0] == "A":
                stats(LN_A, X)
                norm(LN_A, X, XH)
            def tail():
                dve.wait_ge(loads["flags"], 80)
                dve.tensor_reduce(GNA[:, 0:1], MKF[:, 0:S2 - P], AX.X, ALU.max, apply_absolute_value=True)
                settle(dve.tensor_reduce(GNA[:, 1:2], MKF[:, S2 - P:S2], AX.X, ALU.max, apply_absolute_value=True))
                dve.tensor_scalar(GNA[:, 0:1], GNA[:, 0:1], 0.0, None, ALU.not_equal)
                settle(dve.tensor_scalar(GNA[:, 1:2], GNA[:, 1:2], 0.0, None, ALU.is_equal))
                dve.tensor_tensor(FLD[:, 0:1], GNA[:, 0:1], GNA[:, 1:2], ALU.max).then_inc(flag_rows, 1)

            def tail_values():
                dve.wait_ge(kd_ps, 2)
                dve.wait_ge(loads["crows"], 32)
                dve.tensor_tensor(vd[:, :, :], bank(4).rearrange("p (b n) -> p b n", b=B), over(row("x_bv"), B),
                                  ALU.add).then_inc(vd_ready, 1)

            def tail_flag():
                dve.wait_ge(flag_all, 1)
                if general:
                    dve.memset(FDI[:, :], 1).then_inc(flag_d, 1)
                else:
                    dve.tensor_copy(FDI[:, :], FLD[0:1, 1:2]).then_inc(flag_d, 1)

            def kv_windows(j):
                dve.wait_ge(kvw_ps, j + 1)
                dve.tensor_tensor(KVW[:, 2 * j:2 * j + 2, 0:2 * D], sbank(j).rearrange("p (a n) -> p a n", a=2),
                                  over(row("bkv"), 2), ALU.add).then_inc(kvw_ready, 1)

            if "A" not in stages:
                tail()
                tail_values()
                tail_flag()
            for s in stages:
                if s == "A":
                    dve.wait_ge(loads["rows"], 16)
                    kv_windows(0)
                    dve.wait_ge(loads["pos"], 64)
                    settle(dve.tensor_tensor(ybias[:, :], boff[:, :], refc[:, :], ALU.add))

                    def positions(g):
                        dve.wait_ge(a_off_ps, g + 1)
                        return dve.scalar_tensor_tensor(
                            out=Y[:, g, :].rearrange("p (b q) -> p b q", b=B),
                            in0=BK[0:96, (5, 3, 6)[g], :].rearrange("p (b q) -> p b q", b=B), scalar=ybias[:, g:g + 1],
                            in1=loc[:, :].unsqueeze(1).to_broadcast([96, B, P]), op0=ALU.add, op1=ALU.add)

                    settle(positions(0))
                    settle(dve.tensor_scalar(YW[:, :], Y[:, 0, :], 0.0, -1.0, ALU.is_lt, ALU.mult))
                    settle(dve.scalar_tensor_tensor(out=IX[:, :], in0=Y[:, 0, :], scalar=float(S2) / (S2 - 1),
                                                    in1=YW[:, :], op0=ALU.mult, op1=ALU.add))
                    dve.wait_ge(loads["sel"], 32)
                    settle(dve.tensor_copy(R[0:96, 0, :], IX[:, :]))
                    settle(dve.tensor_tensor(IX[:, :], IX[:, :], R[0:96, 0, :], ALU.subtract))
                    settle(dve.tensor_copy(Rh[:, :], IX[:, :]))
                    settle(dve.tensor_tensor(YW[:, :], IX[:, :], Rh[:, :], ALU.subtract))
                    dve.tensor_copy(R[32:64, 0, :], Rh[32:64, :])
                    dve.tensor_copy(R[64:96, 0, :], YW[64:96, :]).then_inc(a_r, 1)
                    for j in range(1, 4):
                        kv_windows(j)
                    positions(1).then_inc(a_y, 1)
                    positions(2).then_inc(a_y, 1)
                    dve.wait_ge(a_q_ps, 2)
                    dve.tensor_tensor(Qq[:, :, :], bank(4).rearrange("p (b n) -> p b n", b=B), over(row("bq"), B),
                                      ALU.add).then_inc(a_qq, 1)

                    def reach(g):
                        if g == 0:
                            dve.wait_ge(a_r, 1)
                            settle(dve.tensor_tensor(YW[:, :].rearrange("p (b q) -> p b q", b=B),
                                                     Y[:, g, :].rearrange("p (b q) -> p b q", b=B),
                                                     mid[:, :].unsqueeze(1).to_broadcast([96, B, P]), ALU.subtract))
                        else:
                            dve.wait_ge(a_dev, g)
                        settle(dve.tensor_reduce(VM3[:, g:g + 1], (YW, YW2, IX2)[g], AX.X, ALU.max,
                                                 apply_absolute_value=True))

                    def uncovered():
                        settle(dve.tensor_reduce(FLA[:, 0:1], MKB[:, :, :], AX.XY, ALU.max, apply_absolute_value=True))
                        settle(dve.tensor_scalar(FLA[:, 0:1], FLA[:, 0:1], 0.0, None, ALU.not_equal))
                        settle(dve.tensor_reduce(GNA[0:96, 0:1], VM3[:, :], AX.X, ALU.max))
                        settle(dve.tensor_scalar(GNA[0:96, 0:1], GNA[0:96, 0:1], 62.5, None, ALU.is_gt))
                        dve.tensor_tensor(FLA[0:96, 0:1], FLA[0:96, 0:1], GNA[0:96, 0:1], ALU.max).then_inc(flag_rows, 1)

                    def evac(G, i):
                        n = 8 * G + i
                        dve.wait_ge(a_samp_ps, n + 1)
                        if G and i == 0:
                            dve.wait_ge(a_tr_ps, 4 * G)
                        b, hf = i // 2, i % 2
                        dve.tensor_copy(SK[:, b, :, QH * hf:QH * hf + QH],
                                        BK[:, 3 + n % 2, 0:NK * QH].rearrange("p (k q) -> p k q", k=NK))\
                           .then_inc(a_sk, 1)

                    def score(u):
                        G, b = u // 4, u % 4
                        dve.wait_ge(a_tr_ps, u + 1)
                        src = BK[:, 5:7, :].rearrange("p a n -> p (a n)")[:, 0:NK * P]
                        src = src.rearrange("p (k h r) -> p k h r", k=NK, h=4)[:, :, :, 0:HD]
                        qv = Qq[:, b, 32 * G:32 * G + 32].rearrange("p (h d) -> p h d", h=4)
                        dve.wait_ge(a_sco, u) if u else dve.wait_ge(a_qq, 1)
                        dve.tensor_tensor(PRD[:, :, :, :], src, over(qv, NK), ALU.mult).then_inc(a_prod, 1)
                        dve.wait_ge(a_prod, u + 1)
                        dve.tensor_reduce(SCO[:, b, 4 * G:4 * G + 4, :], PRD[:, :, :, :].rearrange("p k h d -> p h k d"),
                                          AX.X, ALU.add).then_inc(a_sco, 1)

                    for e in range(E1):
                        G = e // 20
                        dve.wait_ge(a_abs, e + 1)
                        w = WT[:, G % 2, e % 20 // NK, :, e % NK, :]
                        dve.tensor_scalar(w, w, 1.0, -1.0, ALU.min, ALU.add).then_inc(a_w, 1)
                        if e == 2:
                            reach(0)
                        if e == TAIL_AT:
                            tail_values()
                            tail()
                        if e in (53, 56):
                            reach((0, 53, 56).index(e))
                        if e == 59:
                            tail_flag()
                            uncovered()
                        if G and 0 <= e % 20 + 1 - SAMPLE_AT < 8:
                            evac(G - 1, e % 20 + 1 - SAMPLE_AT)
                        if G and e % 20 + 2 in BACK_AT:
                            score(4 * (G - 1) + BACK_AT.index(e % 20 + 2))
                    for i in range(8):
                        evac(3, i)
                        if i in (4, 6):
                            score(12 + i // 2 - 2)
                    score(14)
                    score(15)
                    dve.wait_ge(a_sco, 16)
                    dve.wait_ge(flag_all, 2)
                    if general:
                        dve.memset(FAI[:, :], 1).then_inc(flag_a, 1)
                    else:
                        dve.tensor_copy(FAI[:, :], FLA[0:1, 1:2]).then_inc(flag_a, 1)
                    dve.wait_ge(a_vs, 16)
                    with dve.If(flagged(dve, flag_a, FAI)):
                        dve.sem_inc(ga_kv, 1)
                        dve.sem_inc(ga_add, 1)
                        dve.sem_inc(ga_prod, 1)
                        dve.sem_inc(ga_out, 1)
                        chain_a = [0]

                        def settle_a(ins):
                            chain_a[0] += 1
                            ins.then_inc(ga_chain, 1)
                            dve.wait_ge(ga_chain, chain_a[0])

                        cnt, L, rL = GSM[:, 0, :], GSM[0:96, 1, :], GSM[0:96, 2, :]
                        by_b = lambda v: v.unsqueeze(2).to_broadcast([96, B, P])
                        gv = lambda a, g: a[:, g, :].rearrange("p (b q) -> p b q", b=B)
                        settle_a(dve.tensor_reduce(cnt, MKB[:, :, :], AX.X, ALU.add))
                        dve.tensor_copy(GSM[:, 3, :], cnt).then_inc(ga_zero, 1)
                        dve.wait_ge(ga_sum_ps, 1)
                        settle_a(dve.tensor_scalar(L, BK[0:96, 0, 0:B], -1.0, float(S2 - 1), ALU.mult, ALU.add))
                        settle_a(dve.reciprocal(rL, L))
                        for g in range(3):
                            gx, gt = gv(GIX, g), gv(GT1, g)
                            settle_a(dve.tensor_tensor(gt, gv(Y, g), by_b(rL), ALU.mult))
                            settle_a(dve.tensor_scalar(gt, gt, 12582912.0, None, ALU.add))
                            settle_a(dve.tensor_scalar(gt, gt, -12582912.0, None, ALU.add))
                            settle_a(dve.tensor_tensor(gt, gt, by_b(L), ALU.mult))
                            settle_a(dve.tensor_tensor(gx, gv(Y, g), gt, ALU.subtract))
                            settle_a(dve.tensor_tensor(gt, gx, by_b(L), ALU.mult))
                            settle_a(dve.tensor_scalar(gt, gt, 0.0, None, ALU.is_lt))
                            settle_a(dve.tensor_tensor(gt, gt, by_b(L), ALU.mult))
                            settle_a(dve.tensor_tensor(gx, gx, gt, ALU.add))
                            settle_a(dve.tensor_scalar(gx, gx, float(S2) / (S2 - 1), -0.5, ALU.mult, ALU.add))
                        dve.memset(GKV[:, 2 * D:2 * D + 16], 0.0).then_inc(ga_pos, 1)
                        with dve.Fori(0, B) as b:
                            dve.wait_ge(ga_prod, 1 + b * 4)
                            dve.memset(GSK, 0.0).then_inc(ga_zero, 1)
                            with dve.Fori(0, S2 // P) as c:
                                it = b * (S2 // P) + c
                                dve.wait_ge(ga_zero, b + 2)
                                dve.wait_ge(ga_samp, 1 + it * 4)
                                dve.wait_ge(ga_kv_ps, 1 + it + 1)
                                dve.tensor_tensor(GKV[:, 0:2 * D], BK[:, 7, 0:2 * D], row("bkv"), ALU.add).then_inc(ga_kv, 1)
                                dve.tensor_copy(GPOS, pos[:, bass.ds(c, 1)]).then_inc(ga_kv, 1)
                                for e in range(E1):
                                    dve.wait_ge(ga_abs, 1 + it * E1 + e + 1)
                                    w = GW[:, e % 20 // NK, e % NK, :]
                                    dve.tensor_scalar(w, w, 1.0, -1.0, ALU.min, ALU.add).then_inc(ga_w, 1)
                                    if e % 20 == 19:
                                        G = e // 20
                                        dve.wait_ge(ga_samp, 1 + it * 4 + G + 1)
                                        dve.wait_ge(ga_add, 1 + it * 4 + G)
                                        dve.tensor_tensor(GSK[:, G, :], GSK[:, G, :], BK[:, 3:5, :].rearrange("p a n -> p (a n)")[:, 0:NK * P],
                                                          ALU.add).then_inc(ga_add, 1)
                            for G in range(4):
                                dve.wait_ge(ga_tr, b * 4 + G + 1)
                                src = BK[:, 5:7, :].rearrange("p a n -> p (a n)")[:, 0:NK * P]
                                src = src.rearrange("p (k h r) -> p k h r", k=NK, h=4)
                                qv = Qq[:, bass.ds(b, 1), 32 * G:32 * G + 32].rearrange("p b (h d) -> p (b h) d", h=4)
                                dve.wait_ge(ga_out, 1 + b * 4 + G)
                                dve.tensor_tensor(PRD[:, :, :, :], src[:, :, :, 0:HD], over(qv, NK), ALU.mult)\
                                   .then_inc(ga_prod, 1)
                                for k in range(NK):
                                    dve.tensor_copy(VS[:, bass.ds(b, 1), 4 * G:4 * G + 4, k, :].rearrange("p b h d -> p (b h) d"),
                                                    src[:, k, :, HD:2 * HD])
                                dve.wait_ge(ga_prod, 1 + b * 4 + G + 1)
                                dve.tensor_reduce(SCO[:, bass.ds(b, 1), 4 * G:4 * G + 4, :].rearrange("p b h k -> p (b h) k"),
                                                  PRD[:, :, :, :].rearrange("p k h d -> p h k d"), AX.X, ALU.add)\
                                   .then_inc(ga_out, 1)
                        dve.wait_ge(ga_out, 1 + 4 * B)
                    z = SCO[:, :, :, :].rearrange("p b h k -> p (b h) k")
                    m1 = SM1[:, :, :].rearrange("p b h -> p (b h)")
                    m2 = SM2[:, :, :].rearrange("p b h -> p (b h)")
                    settle(dve.tensor_scalar(z, z, -0.5 / np.sqrt(HD), None, ALU.mult))
                    settle(dve.tensor_reduce(m1, z, AX.X, ALU.max))
                    dve.tensor_tensor(z, z, over(m1, NK, 2), ALU.subtract).then_inc(a_z, 1)
                    dve.wait_ge(a_exp, 1)
                    settle(dve.tensor_reduce(m1, z, AX.X, ALU.add))
                    settle(dve.reciprocal(m2, m1))
                    settle(dve.tensor_scalar(m1, m2, -0.5, None, ALU.mult))
                    settle(dve.tensor_tensor(z, z, over(m1, NK, 2), ALU.mult))
                    vs = VS.rearrange("p b h k d -> p (b h) k d")
                    pv = PV.rearrange("p b h k d -> p (b h) k d")
                    settle(dve.tensor_tensor(pv, vs, over(z, HD, 3), ALU.mult))
                    dve.tensor_reduce(CT[:, :, :].rearrange("p b (h d) -> p (b h) d", h=H),
                                      pv.rearrange("p n k d -> p n d k"), AX.X, ALU.add).then_inc(ctx_ready, 1)
                    dve.wait_ge(xb_ready, 1)
                    residual("A", XB[:, :, :])
                if s == "B":
                    stats(LN_B, X)
                    norm(LN_B, X, XH)
                    dve.wait_ge(loads["decay"], 64)
                    for j, dst in ((0, qT), (2, kT)):
                        dve.wait_ge(b_qk_ps, j + 1)
                        dve.tensor_tensor(T0[:, :, :], bank(j), over(rope0[:, j, :], B), ALU.mult)
                        dve.wait_ge(b_qk_ps, j + 2)
                        settle(dve.tensor_tensor(T1[:, :, :], bank(j + 1), over(rope0[:, j + 1, :], B), ALU.mult))
                        dve.tensor_tensor(dst[:, :, :], T0[:, :, :], T1[:, :, :], ALU.add)\
                           .then_inc(b_rot, 1)
                        dve.wait_ge(b_rot, 2 if j else 1)

                    def blk(b):
                        if b >= 2:
                            dve.wait_ge(b_s_ps, 4 * (b - 1))
                        dve.tensor_tensor(BLK[:, b % 2], over(qT[:, b, :], 4), over(head[:, :], P, 2), ALU.mult)\
                           .then_inc(b_blk, 1)

                    def extract(b):
                        dve.wait_ge(b_o_ps, b + 1)
                        settle(dve.tensor_tensor(OM, bank(4 + b % 2).rearrange("p (h t) -> p h t", h=4),
                                                 over(head[:, :], P, 2), ALU.mult))
                        dve.tensor_reduce(CT[:, b, :], OM.rearrange("p h t -> p t h"), AX.X, ALU.add)\
                           .then_inc(b_oT, 1)
                        dve.wait_ge(b_oT, b + 1)

                    blk(0)
                    blk(1)
                    for b in range(B):
                        for g in range(4):
                            dve.wait_ge(b_s_ps, 4 * b + g + 1)
                            if b >= 2 and g == 0:
                                dve.wait_ge(b_o_ps, b - 1)
                            dve.tensor_tensor(PT[:, b % 2, 4 * g:4 * g + 4, :], bank(g).rearrange("p (h t) -> p h t", h=4),
                                              decay[:, 4 * g:4 * g + 4, :], ALU.mult).then_inc(b_pt, 1)
                        if b + 2 < B:
                            blk(b + 2)
                        if b:
                            extract(b - 1)
                    extract(B - 1)
                    dve.wait_ge(b_oc_ps, 1)
                    dve.wait_ge(b_std, 1)
                    settle(dve.reciprocal(T1[:, :, :], T1[:, :, :]))
                    settle(dve.tensor_tensor(T1[:, :, :], bank(4), T1[:, :, :], ALU.mult))
                    dve.tensor_scalar(CTT[:, :], T1[:, :, :].rearrange("p b t -> p (b t)"), col("gn_w"), col("gn_b"),
                                      ALU.mult, ALU.add).then_inc(b_on, 1)
                    residual("B", X[:, :, :])
                if s in "CF":
                    k = FFNS.index(s)
                    ln = LN_C if s == "C" else LN_F
                    stats(ln, X)
                    norm(ln, X, XH)
                    dve.wait_ge(r_lg_ps, k + 1)
                    lg = BK[:, 4, 0:B * NE].rearrange("p (b e) -> p b e", b=B)
                    settle(dve.tensor_reduce(S1[:, :], lg, AX.X, ALU.max))
                    dve.tensor_tensor(EX[:, :, :], lg, over(S1[:, :], NE, 2), ALU.subtract).then_inc(r_z, 1)
                    dve.wait_ge(r_exp, k + 1)
                    settle(dve.tensor_reduce(S1[:, :], EX[:, :, :], AX.X, ALU.add))
                    settle(dve.reciprocal(S1[:, :], S1[:, :]))
                    settle(dve.tensor_tensor(PR[:, :, :], EX[:, :, :], over(S1[:, :], NE, 2), ALU.mult))
                    other, own = over(PR[:, :, :], NE, 2), over(PR[:, :, :], NE, 3)
                    dve.tensor_tensor(CMP[:, :, :, :], other, own, ALU.is_gt)
                    settle(dve.tensor_tensor(CMQ[:, :, :, :], other, own, ALU.is_equal))
                    if not k:
                        dve.wait_ge(loads["crows"], 32)
                    before = crows[:, BEFORE].rearrange("p (e f) -> p e f", e=NE)
                    settle(dve.tensor_tensor(CMQ[:, :, :, :], CMQ[:, :, :, :], over(before, B), ALU.mult))
                    settle(dve.tensor_tensor(CMP[:, :, :, :], CMP[:, :, :, :], CMQ[:, :, :, :], ALU.add))
                    settle(dve.tensor_reduce(RK[:, :, :], CMP[:, :, :, :], AX.X, ALU.add))
                    settle(dve.scalar_tensor_tensor(out=PR[:, :, :], in0=RK[:, :, :], scalar=1.5, in1=PR[:, :, :],
                                                    op0=ALU.is_lt, op1=ALU.mult))
                    settle(dve.tensor_reduce(S1[:, :], PR[:, :, :], AX.X, ALU.add))
                    if s == "C":
                        settle(dve.tensor_scalar(S1[:, :], S1[:, :], 1e-9, None, ALU.add))
                    settle(dve.reciprocal(S1[:, :], S1[:, :]))
                    dve.tensor_tensor(CW[:, :, :], PR[:, :, :], over(S1[:, :], NE, 2), ALU.mult).then_inc(r_cw, 1)
                    if s == "C":
                        dve.wait_ge(r_cw, 1)
                        settle(dve.tensor_reduce(S1[:, :], CW[:, :, :], AX.X, ALU.add))
                        for b in range(B):
                            ins = dve.scalar_tensor_tensor(out=X[:, b, :], in0=row("ff_bo"), scalar=S1[:, b:b + 1],
                                                           in1=X[:, b, :], op0=ALU.mult, op1=ALU.add)
                        settle(ins)

                    def weigh(e):
                        n = k * NE + e
                        dve.wait_ge(e_y_ps, n + 1)
                        if n:
                            dve.wait_ge(e_sum, n)
                        elif s != "C":
                            dve.wait_ge(r_cw, k + 1)
                        for b in range(B):
                            ins = dve.scalar_tensor_tensor(out=X[:, b, :], in0=BK[:, 4 + e % 2, b * P:(b + 1) * P],
                                                           scalar=CW[:, b, e:e + 1], in1=X[:, b, :],
                                                           op0=ALU.mult, op1=ALU.add)
                        ins.then_inc(e_sum, 1)

                    dve.wait_ge(r_cw, k + 1)
                    for e in range(NE):
                        n = k * NE + e
                        if s == "C":
                            if e >= 2:
                                dve.wait_ge(e_y_ps, n - 1)
                            for p in (2 * e, 2 * e + 1):
                                dve.wait_ge(e_act, p + 1)
                                ba = cols[:, B1COL + 4 * e + p % 2:B1COL + 4 * e + 1 + p % 2]
                                dve.scalar_tensor_tensor(out=GT[:, e % 2, p % 2, :], in0=hbank(2 * p), scalar=ba,
                                                         in1=SG[:, e % 2, p % 2, :], op0=ALU.add, op1=ALU.mult)\
                                   .then_inc(e_g, 1)
                        if e:
                            weigh(e - 1)
                    weigh(NE - 1)
                    dve.wait_ge(e_sum, k * NE + NE)
                if s == "D":
                    stats(LN_D, X)
                    norm(LN_D, X, XH)
                    settle(dve.tensor_scalar(MB[:, :], mtail[:, :], 0, KEPT, ALU.not_equal, ALU.mult))
                    settle(dve.tensor_scalar(MB[:, :], MB[:, :], NEG, None, ALU.add))
                    dve.wait_ge(kd_ready, 1)

                    def blk(b):
                        if b >= 2:
                            dve.wait_ge(d_s_ps, 4 * (b - 1))
                        dve.tensor_tensor(BLK[:, b % 2], over(kTd[:, b, :], 4), over(head[:, :], P, 2), ALU.mult)\
                           .then_inc(d_blk, 1)

                    def extract(b):
                        dve.wait_ge(d_o_ps, b + 1)
                        dve.tensor_tensor(OM, bank(6).rearrange("p (h t) -> p h t", h=4),
                                          over(head[:, :], P, 2), ALU.mult)
                        settle(dve.tensor_tensor(DN, bank(7).rearrange("p (h t) -> p h t", h=4),
                                                 over(head[:, :], P, 2), ALU.mult))
                        dve.tensor_reduce(T0[:, b, :], OM.rearrange("p h t -> p t h"), AX.X, ALU.add)
                        settle(dve.tensor_reduce(T1[:, b, :], DN.rearrange("p h t -> p t h"), AX.X, ALU.add))
                        settle(dve.reciprocal(T1[:, b, :], T1[:, b, :]))
                        dve.tensor_tensor(CTT[:, b * P:(b + 1) * P], T0[:, b, :], T1[:, b, :], ALU.mult)\
                           .then_inc(d_om, 1)
                        dve.wait_ge(d_om, b + 1)

                    blk(0)
                    blk(1)
                    for b in range(B):
                        for g in range(4):
                            dve.wait_ge(d_s_ps, 4 * b + g + 1)
                            if b >= 2 and g == 0:
                                dve.wait_ge(d_pT_ps, 4 * (b - 1))
                            ins = dve.scalar_tensor_tensor(
                                out=SS[:, b % 2, 4 * g:4 * g + 4, :], in0=bank(g).rearrange("p (h t) -> p h t", h=4),
                                scalar=float(1.0 / np.sqrt(HD)), in1=over(MB[:, :], 4), op0=ALU.mult, op1=ALU.min)
                            ins.then_inc(d_ss, 1)
                        dve.wait_ge(d_ss, 4 * b + 4)
                        dve.tensor_reduce(MX[:, b, :], SS[:, b % 2], AX.X, ALU.max).then_inc(d_mx, 1)
                        if b + 2 < B:
                            blk(b + 2)
                        if b:
                            extract(b - 1)
                    extract(B - 1)
                    with dve.If(flagged(dve, flag_d, FDI)):
                        dve.sem_inc(gd_v, 1)
                        dve.sem_inc(gd_oT, 1)
                        dve.sem_inc(gd_o, 1)
                        dve.wait_ge(gd_mask, 16)
                        dve.tensor_scalar(GM, GMI, 0, KEPT, ALU.not_equal, ALU.mult).then_inc(gd_m0, 1)
                        dve.wait_ge(gd_m0, 1)
                        dve.tensor_scalar(GM, GM, NEG, None, ALU.add).then_inc(gd_m0, 1)
                        dve.wait_ge(gd_m0, 2)
                        with dve.Fori(0, B) as b:
                            with dve.Fori(0, S2 // P) as c:
                                it = b * (S2 // P) + c
                                dve.wait_ge(gd_kv_ps, 1 + it + 1)
                                dve.tensor_tensor(GV[:, bass.ds(c, 1), :].rearrange("p c n -> p (c n)"), BK[:, 1, 0:P],
                                                  row("x_bv"), ALU.add).then_inc(gd_v, 1)
                            with dve.Fori(0, H) as h:
                                it = b * H + h
                                dve.wait_ge(gd_s_ps, 1 + it)
                                dve.tensor_scalar(GQ, qT[:, bass.ds(b, 1), :].rearrange("p b n -> p (b n)"),
                                                  head16[:, bass.ds(h, 1)], None, ALU.mult).then_inc(gd_q, 1)
                                dve.wait_ge(gd_s_ps, 1 + it + 1)
                                dve.scalar_tensor_tensor(out=GSC, in0=BK[:, 0:4, :].rearrange("p a n -> p (a n)"),
                                                         scalar=float(1.0 / np.sqrt(HD)), in1=GM, op0=ALU.mult,
                                                         op1=ALU.min).then_inc(gd_chain, 1)
                                dve.wait_ge(gd_chain, 3 * it + 1)
                                dve.tensor_reduce(GR[:, 2:3], GSC, AX.X, ALU.max).then_inc(gd_chain, 1)
                                dve.wait_ge(gd_chain, 3 * it + 2)
                                dve.tensor_scalar(GR[:, 0:1], GR[:, 2:3], -1.0, None, ALU.mult).then_inc(gd_neg, 1)
                                dve.wait_ge(gd_o_ps, it + 1)
                                dve.reciprocal(GR[:, 3:4], GR[:, 1:2]).then_inc(gd_chain, 1)
                                dve.wait_ge(gd_chain, 3 * it + 3)
                                dve.tensor_scalar(GO[:, bass.ds(h * HD, HD)], BK[:, 0, bass.ds(h * HD, HD)], GR[:, 3:4],
                                                  None, ALU.mult).then_inc(gd_o, 1)
                            dve.wait_ge(gd_oT_ps, b + 1)
                            dve.tensor_copy(CTT[:, bass.ds(b * P, P)], BK[:, 1, 0:P]).then_inc(gd_oT, 1)
                        dve.wait_ge(gd_oT, 1 + B)
                    dve.wait_ge(xb_ready, BIASED.index("D") + 1)
                    residual("D", XB[:, :, :])
                if s == "E":
                    stats(LN_E0, X)
                    norm(LN_E0, X, XN)
                    stats(LN_E1, XN)
                    norm(LN_E1, XN, XH)
                    settle(dve.tensor_tensor(HH[:, :, :], XH[:, :, :], over(row("ln1_w"), B), ALU.mult))
                    dve.tensor_tensor(HH[:, :, :], HH[:, :, :], over(row("ln1_b"), B), ALU.add).then_inc(l_h1, 1)
                    dve.wait_ge(l_h1, 1)
                    settle(dve.tensor_tensor(XH[:, :, :], HH[:, :, :], over(row("conv1"), B), ALU.mult))
                    dve.wait_ge(l_hp, 1)
                    dve.tensor_copy(HH[:, 0, :], XH[:, 0, :])
                    dve.tensor_tensor(HH[:, 1:4, :], XH[:, 1:4, :], HP[:, 0:3, :], ALU.add).then_inc(l_hc, 1)
                    dve.wait_ge(loads["crows"], 32)
                    dve.wait_ge(l_vkqg, 1)
                    rw = rows[:, ROWS["rw"]].rearrange("p (r n) -> p r n", r=2)
                    for r in range(2):
                        ins = dve.tensor_tensor(LP[:, r], VV[:, :, :], over(rw[:, r, :], B), ALU.mult)
                    settle(ins)
                    lg = LGT[:, :, :, :].rearrange("p r b h -> p r (b h)")
                    settle(dve.tensor_reduce(LGT[:, :, :, :].rearrange("p r b h -> p (r b h)"),
                                             LP[:, :, :, :].rearrange("p r b (h d) -> p (r b h) d", h=H), AX.X, ALU.add))
                    settle(dve.tensor_tensor(OH[:, :, :], LGT[:, 0], LGT[:, 1], ALU.is_ge))
                    settle(dve.tensor_tensor(SM1[:, :, :], LGT[:, 0], LGT[:, 1], ALU.max))
                    dve.tensor_tensor(LGT[:, :, :, :], LGT[:, :, :, :], over(SM1[:, :, :], 2), ALU.subtract)\
                       .then_inc(l_ld, 1)
                    settle(dve.tensor_tensor(SMM[:, :, :, :], over(OH[:, :, :], B, 2), over(OH[:, :, :], B, 1), ALU.is_equal))
                    cz = crows[:, CAUSAL1].rearrange("p (l m h) -> p l m h", l=B, m=B)
                    settle(dve.tensor_tensor(SMM[:, :, :, :], SMM[:, :, :, :], cz, ALU.mult))
                    settle(dve.tensor_reduce(OH[:, :, :], SMM[:, :, :, :].rearrange("p l m h -> p l h m"), AX.X, ALU.add))
                    dve.wait_ge(l_le, 1)
                    settle(dve.tensor_tensor(SM1[:, :, :], LGE[:, 0], LGE[:, 1], ALU.add))
                    settle(dve.tensor_tensor(SM1[:, :, :], SM1[:, :, :], OH[:, :, :], ALU.mult))
                    settle(dve.reciprocal(SM2[:, :, :], SM1[:, :, :]))
                    settle(dve.tensor_tensor(SMM[:, :, :, :], SMM[:, :, :, :], over(SM2[:, :, :], B, 2), ALU.mult))
                    dve.wait_ge(l_vkqg, 3)
                    cs = crows[:, ROPE1].rearrange("p (a n) -> p a n", a=2)
                    qk = QK[:, :, :, :].rearrange("p b a n -> p (b a n)")
                    dve.tensor_tensor(QR[:, :, :, :].rearrange("p b a n -> p (b a n)"), qk, cs[:, 0, :], ALU.mult)
                    halves = lambda a: a.rearrange("p (n f i) -> p n f i", f=2, i=2)
                    q2 = Q2[:, :, :, :].rearrange("p b a n -> p (b a n)")
                    for f in range(2):
                        ins = dve.tensor_tensor(halves(q2)[:, :, f, :], halves(qk)[:, :, 1 - f, :],
                                                halves(cs[:, 1, :])[:, :, f, :], ALU.mult)
                    settle(ins)
                    settle(dve.tensor_tensor(QR[:, :, :, :], QR[:, :, :, :], Q2[:, :, :, :], ALU.add))
                    for l in range(B):
                        ins = dve.tensor_tensor(PDT[:, l], over(QR[:, l, 0, :], B), QR[:, :, 1, :], ALU.mult)
                    settle(ins)
                    settle(dve.tensor_reduce(DT[:, :, :, :].rearrange("p l m h -> p (l m h)"),
                                             PDT[:, :, :, :].rearrange("p l m (h d) -> p (l m h) d", h=H), AX.X, ALU.add))
                    settle(dve.tensor_tensor(DT[:, :, :, :], DT[:, :, :, :], SMM[:, :, :, :], ALU.mult))
                    for l in range(B):
                        ins = dve.tensor_tensor(PO[:, l, 0:l + 1].rearrange("p m (h d) -> p (m h) d", h=H),
                                                over(DT[:, l, 0:l + 1, :].rearrange("p m h -> p (m h)"), HD, 2),
                                                VV[:, 0:l + 1, :].rearrange("p m (h d) -> p (m h) d", h=H), ALU.mult)
                    settle(ins)
                    dve.tensor_copy(OO[:, 0, :], PO[:, 0, 0, :])
                    for l in range(1, B):
                        ins = dve.tensor_reduce(OO[:, l, :], PO[:, l, 0:l + 1, :].rearrange("p m n -> p n m"), AX.X, ALU.add)
                    settle(ins)
                    hv = lambda a: a[:, :, :].rearrange("p b (h d) -> p (b h) d", h=H)
                    m1 = SM1[:, :, :].rearrange("p b h -> p (b h)")
                    m2 = SM2[:, :, :].rearrange("p b h -> p (b h)")
                    settle(dve.tensor_reduce(m1, hv(OO), AX.X, ALU.add))
                    settle(dve.tensor_scalar(m2, m1, 1.0 / HD, None, ALU.mult))
                    dve.tensor_tensor(hv(OO), hv(OO), over(m2, HD, 2), ALU.subtract).then_inc(l_oc, 1)
                    dve.wait_ge(l_sq, 1)
                    dve.tensor_reduce(m1, hv(OQ), AX.X, ALU.add).then_inc(l_vs, 1)
                    dve.wait_ge(l_std, 1)
                    settle(dve.reciprocal(m1, m2))
                    settle(dve.tensor_tensor(hv(OO), hv(OO), over(m1, HD, 2), ALU.mult))
                    dve.wait_ge(l_vkqg, 4)
                    dve.tensor_tensor(CT[:, :, :], OO[:, :, :], GS[:, :, :], ALU.mult).then_inc(ctx_ready, 1)
                    dve.wait_ge(proj_ps, PROJ.index("E") + 1)
                    dve.tensor_tensor(CT[:, :, :], bank(6), XN[:, :, :], ALU.add).then_inc(l_xa, 1)
                    dve.wait_ge(l_xa, 1)
                    stats(LN_E2, CT)
                    norm(LN_E2, CT, XH)
                    settle(dve.tensor_tensor(XH[:, :, :], XH[:, :, :], over(row("ln2_w"), B), ALU.mult))
                    dve.tensor_tensor(XH[:, :, :], XH[:, :, :], over(row("ln2_b"), B), ALU.add).then_inc(l_h2, 1)
                    for j, (o, w) in enumerate(FFT):
                        dve.wait_ge(l_ffs, j + 1)
                        dve.wait_ge(l_ff_ps, 3 + j + 1)
                        dve.tensor_tensor(HF[0:w, j, :], BK[0:w, (3, 4, 6)[j], :], HF[0:w, j, :], ALU.mult).then_inc(l_ff, 1)
                    dve.wait_ge(xb_ready, BIASED.index("E") + 1)
                    dve.wait_ge(proj_ps, PROJ.index("E") + 2)
                    dve.tensor_tensor(X[:, :, :], bank(7), XB[:, :, :], ALU.add).then_inc(x_ready, 1)
                    stages_done(dve, nx[s] + 1)

        @block.tensor
        def _(pe):
            def norm_T(n, bk, src=XH):
                for b in range(B):
                    pe.wait_ge(ln_xhat, xhat_count(n) - 3 + b)
                    ins = pe.transpose(BK[:, bk, b * P:(b + 1) * P], src[:, b, :], ident[:, :])
                ins.then_inc(ln_xT_ps, 1)

            def transposes(src, bk, s):
                for b in range(B):
                    ins = pe.transpose(BK[:, bk, b * P:(b + 1) * P], src[:, b, :], ident[:, :])
                ins.then_inc(s, 1)

            def project(w, bk=7):
                for b in range(B):
                    ins = pe.matmul(BK[:, bk, b * P:(b + 1) * P], CTT[:, b * P:(b + 1) * P], w, start=True, stop=True)
                ins.then_inc(proj_ps, 1)

            pe.wait_ge(loads["ident"], 16)
            if stages[0] == "A":
                norm_T(LN_A, 5)
            def tail():
                pe.wait_ge(loads["w_d"], 16)
                pe.wait_ge(loads["tail"], 16)
                pe.matmul(bank(3), w_d[:, 0:D], TAIL.rearrange("p b n -> p (b n)"), start=True, stop=True)\
                  .then_inc(kd_ps, 1)
                for b in range(B):
                    ins = pe.matmul(BK[:, 4, b * P:(b + 1) * P], TAIL[:, b, :], w_d[:, D:2 * D], start=True, stop=True)
                ins.then_inc(kd_ps, 1)

            if "A" not in stages:
                tail()

            for s in stages:
                if s == "A":
                    wq, woff, wo = w_a[:, 256:384], w_a[:, 384:672].rearrange("p (g n) -> p g n", g=3), w_a[:, 672:800]

                    def kv_windows(j):
                        for hf in range(2):
                            ins = pe.matmul(sbank(j)[:, 2 * D * hf:2 * D * hf + 2 * D], WIN[:, j, QH * hf:QH * hf + P],
                                            w_a[:, 0:2 * D], start=True, stop=True)
                        ins.then_inc(kvw_ps, 1)

                    pe.wait_ge(loads["w_a"], 16)
                    pe.wait_ge(ln_xT, xT_count(LN_A))
                    pe.matmul(bank(6), wq, XT[:, :], start=True, stop=True).then_inc(a_q_ps, 1)
                    pe.wait_ge(loads["win"], 32)
                    kv_windows(0)
                    pe.wait_ge(a_qT, 1)
                    for g in range(3):
                        pe.matmul(BK[0:96, (5, 3, 6)[g], :], woff[:, g, :], QpT[:, :], start=True, stop=True)\
                          .then_inc(a_off_ps, 1)
                    for b in range(1, B):
                        kv_windows(b)
                    for b in range(B):
                        ins = pe.matmul(BK[:, 4, b * P:(b + 1) * P], XT[:, b * P:(b + 1) * P], wq, start=True, stop=True)
                    ins.then_inc(a_q_ps, 1)

                    def spread(e):
                        if e < 4:
                            pe.wait_ge(kvw_ready, e + 1)
                        else:
                            pe.wait_ge(a_abs, e - 3)
                        if e % 32 == 0:
                            pe.wait_ge(a_r, e // 32 + 1)
                        pe.matmul(sbank(e), SEL[:, e % 32, :], R[:, e // 32, :], start=True, stop=True)\
                          .then_inc(a_ix_ps, 1)

                    def sample(G, i):
                        if i == 0:
                            pe.wait_ge(a_w, 20 * G + 20)
                        if G == 0 and i == 0:
                            pe.wait_ge(kd_ready, 1)
                            pe.wait_ge(vd_ready, 1)
                        n = 8 * G + i
                        if n >= 2:
                            pe.wait_ge(a_sk, n - 1)
                        for h in range(4):
                            c = 16 * (4 * G + h)
                            ins = pe.matmul(BK[32 * h:32 * h + 32, 3 + n % 2, 0:NK * QH], KVW[:, i, c:c + 32],
                                            WT[:, G % 2, h, i, :, :].rearrange("p k q -> p (k q)"),
                                            start=True, stop=True)
                        ins.then_inc(a_samp_ps, 1)

                    def back(G, b):
                        u = 4 * G + b
                        pe.wait_ge(a_sk, 8 * G + 2 * b + 2)
                        if u:
                            pe.wait_ge(a_vs, u)
                            pe.wait_ge(a_prod, u)
                        for k in range(NK):
                            ins = pe.transpose(BK[:, 5 + k // 4, k % 4 * P:k % 4 * P + P], SK[:, b, k, :],
                                               ident[:, :])
                        ins.then_inc(a_tr_ps, 1)

                    for i in range(20):
                        spread(i)
                        if i == TAIL_AT - 3:
                            pe.wait_ge(a_y, 1)
                            pe.wait_ge(a_qq, 1)
                            tail()
                    for G in range(1, 4):
                        for i in range(20):
                            spread(20 * G + i)
                            if 0 <= i - SAMPLE_AT < 8:
                                sample(G - 1, i - SAMPLE_AT)
                            if i in BACK_AT:
                                back(G - 1, BACK_AT.index(i))
                    for i in range(8):
                        sample(3, i)
                        if i in (3, 5, 7):
                            back(3, (i - 3) // 2)
                    back(3, 3)
                    with pe.If(flagged(pe, flag_a, FAI)):
                        pe.sem_inc(ga_kv_ps, 1)
                        pe.sem_inc(ga_samp, 1)
                        pe.wait_ge(ga_zero, 1)
                        pe.matmul(BK[0:96, 0, 0:B], ones[:, 0:96], GSM[:, 3, :], start=True, stop=True).then_inc(ga_sum_ps, 1)
                        pe.wait_ge(ga_pos, 1)
                        with pe.Fori(0, B) as b:
                            with pe.Fori(0, S2 // P) as c:
                                it = b * (S2 // P) + c
                                pe.wait_ge(ga_in, it * 16 + 16)
                                pe.wait_ge(ga_kv, 1 + 2 * it)
                                pe.matmul(BK[:, 7, 0:2 * D], GCH, w_a[:, 0:2 * D], start=True, stop=True)\
                                  .then_inc(ga_kv_ps, 1)
                                for e in range(E1):
                                    g, i, G = e // 32, e % 32, e // 20
                                    pe.wait_ge(ga_abs, 1 + it * E1 + e)
                                    pe.matmul(BK[:, 0, 0:P], ident[0:96, i:i + 1].to_broadcast([96, P]),
                                              GIX[:, g, bass.ds(b * P, P)], start=True, stop=True).then_inc(ga_ix, 1)
                                    if e % 20 == 19:
                                        pe.wait_ge(ga_kv, 1 + 2 * it + 1)
                                        pe.wait_ge(ga_w, it * E1 + e + 1)
                                        pe.wait_ge(ga_add, 1 + it * 4 + G)
                                        for h in range(4):
                                            for k in range(NK):
                                                o = 16 * (4 * G + h)
                                                ins = pe.matmul(BK[32 * h:32 * h + 32, 3 + k // 4, k % 4 * P:k % 4 * P + P],
                                                                GKV[:, o:o + 32], GW[:, h, k, :], start=True, stop=True)
                                        ins.then_inc(ga_samp, 1)
                            for G in range(4):
                                pe.wait_ge(ga_add, 1 + b * (4 * S2 // P) + 4 * (S2 // P))
                                pe.wait_ge(ga_out, 1 + b * 4 + G)
                                for k in range(NK):
                                    ins = pe.transpose(BK[:, 5 + k // 4, k % 4 * P:k % 4 * P + P],
                                                       GSK[:, G, k * P:(k + 1) * P], ident[:, :])
                                ins.then_inc(ga_tr, 1)
                    pe.wait_ge(ctx_ready, 1)
                    transposes(CT, 6, ctxT_ps)
                    pe.wait_ge(ctxT_ready, 1)
                    pe.wait_ge(vd_ready, 1)
                    project(wo)
                if s == "B":
                    norm_T(LN_B, 7)
                    pe.wait_ge(ln_xT, xT_count(LN_B))
                    pe.wait_ge(loads["w_b"], 16)
                    for j in range(4):
                        pe.matmul(bank(j), w_b[:, j * D:(j + 1) * D], XT[:, :], start=True, stop=True).then_inc(b_qk_ps, 1)
                    for b in range(B):
                        ins = pe.matmul(BK[:, 4, b * P:(b + 1) * P], XT[:, b * P:(b + 1) * P], w_b[:, 4 * D:5 * D],
                                        start=True, stop=True)
                    ins.then_inc(b_v_ps, 1)
                    pe.wait_ge(b_rot, 2)
                    pe.wait_ge(b_v, 1)

                    def scores(b):
                        pe.wait_ge(b_blk, b + 1)
                        for g in range(4):
                            if b:
                                pe.wait_ge(b_pt, 4 * (b - 1) + g + 1)
                            o = 32 * g
                            pe.matmul(bank(g), kT[o:o + 32, b, :], BLK[o:o + 32, b % 2].rearrange("p h t -> p (h t)"),
                                      start=True, stop=True).then_inc(b_s_ps, 1)

                    def values(b):
                        pe.wait_ge(b_pt, 4 * b + 4)
                        if b >= 2:
                            pe.wait_ge(b_oT, b - 1)
                        for g in range(4):
                            o = 32 * g
                            ins = pe.matmul(BK[o:o + 32, 4 + b % 2, :], vq[:, b, o:o + 32],
                                            PT[:, b % 2, 4 * g:4 * g + 4, :].rearrange("p h t -> p (h t)"),
                                            start=True, stop=True)
                        ins.then_inc(b_o_ps, 1)

                    scores(0)
                    for b in range(B):
                        if b + 1 < B:
                            scores(b + 1)
                        values(b)
                    pe.wait_ge(b_oT, 4)
                    ct = CT[:, :, :].rearrange("p b t -> p (b t)")
                    pe.matmul(bank(4), group[:, 0, :], ct, start=True, stop=True).then_inc(b_oc_ps, 1)
                    pe.wait_ge(b_sq, 1)
                    pe.matmul(bank(5), group[:, 1, :], T0[:, :, :].rearrange("p b t -> p (b t)"), start=True, stop=True)\
                      .then_inc(b_var_ps, 1)
                    pe.wait_ge(b_on, 1)
                    project(w_b[:, 5 * D:6 * D])
                if s in "CF":
                    k = FFNS.index(s)
                    ln = LN_C if s == "C" else LN_F
                    norm_T(ln, 7)
                    pe.wait_ge(ln_xT, xT_count(ln))
                    wg = w_c[:, 0:8] if s == "C" else w_f[:, :]
                    w1 = w_c1 if s == "C" else w_f1
                    pe.wait_ge(loads["w_c" if s == "C" else "w_e"], 16 if s == "C" else 48)
                    for b in range(B):
                        ins = pe.matmul(BK[:, 4, b * NE:(b + 1) * NE], XT[:, b * P:(b + 1) * P], wg, start=True, stop=True)
                    ins.then_inc(r_lg_ps, 1)
                    pe.wait_ge(loads["w_c1" if s == "C" else "w_f1"], 16)
                    if s == "F":
                        pe.wait_ge(loads["w_f2"], 16)

                    def up(e):
                        for j in range(4):
                            u = 4 * e + j
                            if s == "C":
                                if j % 2 == 0 and u >= 6:
                                    pe.wait_ge(e_g, u // 2 - 2)
                                o = (4 * e + j // 2 + 2 * (j % 2)) * P
                            else:
                                if u >= 6:
                                    pe.wait_ge(e_act, before_f + u - 5)
                                o = u * P
                            ins = pe.matmul(hbank(u), w1[:, o:o + P], XT[:, :], start=True, stop=True)
                            if s == "F" or j % 2:
                                ins.then_inc(e_h_ps, 1)

                    def down(e):
                        n = k * NE + e
                        m = 2 if s == "C" else 4
                        if n >= 2:
                            pe.wait_ge(e_sum, n - 1)
                        for b in range(B):
                            for j in range(m):
                                if b == 0:
                                    pe.wait_ge(e_g, 2 * e + j + 1) if s == "C" else pe.wait_ge(e_act, before_f + 4 * e + j + 1)
                                w = w_c[:, 8 + j * D:8 + (j + 1) * D] if s == "C" else w_f2[:, (4 * e + j) * D:(4 * e + j + 1) * D]
                                ins = pe.matmul(BK[:, 4 + e % 2, b * P:(b + 1) * P], GT[:, e % 2, j, b * P:(b + 1) * P], w,
                                                start=(j == 0), stop=(j == m - 1))
                        ins.then_inc(e_y_ps, 1)

                    up(0)
                    pe.wait_ge(r_z, k + 1)
                    for e in range(NE):
                        if e + 1 < NE:
                            up(e + 1)
                        down(e)
                if s == "D":
                    norm_T(LN_D, 7)
                    pe.wait_ge(ln_xT, xT_count(LN_D))
                    pe.matmul(bank(6), w_d[:, 2 * D:3 * D], XT[:, :], start=True, stop=True).then_inc(d_q_ps, 1)
                    pe.wait_ge(d_q, 1)

                    def scores(b):
                        pe.wait_ge(d_blk, b + 1)
                        for g in range(4):
                            if b:
                                pe.wait_ge(d_ss, 4 * (b - 1) + g + 1)
                            o = 32 * g
                            pe.matmul(bank(g), qT[o:o + 32, b, :], BLK[o:o + 32, b % 2].rearrange("p h t -> p (h t)"),
                                      start=True, stop=True).then_inc(d_s_ps, 1)

                    def values(b):
                        pe.wait_ge(d_exp, b + 1)
                        for g in range(4):
                            n = 4 * b + g
                            if n >= 2:
                                pe.wait_ge(d_pT, n - 1)
                            for h in range(4):
                                ins = pe.transpose(BK[:, 4 + n % 2, h * P:(h + 1) * P], SS[:, b % 2, 4 * g + h, :], ident[:, :])
                            ins.then_inc(d_pT_ps, 1)
                        pe.wait_ge(d_pT, 4 * b + 4)
                        if b:
                            pe.wait_ge(d_om, b)
                        for dst, w in ((6, None), (7, ones)):
                            for g in range(4):
                                o = 32 * g
                                lhs = vd[:, b, o:o + 32] if w is None else ones[:, 0:32]
                                ins = pe.matmul(BK[o:o + 32, dst, :], lhs,
                                                PT[:, b % 2, 4 * g:4 * g + 4, :].rearrange("p h t -> p (h t)"),
                                                start=True, stop=True)
                        ins.then_inc(d_o_ps, 1)

                    scores(0)
                    for b in range(B):
                        if b + 1 < B:
                            scores(b + 1)
                        values(b)
                    pe.wait_ge(d_om, 4)
                    with pe.If(flagged(pe, flag_d, FDI)):
                        pe.sem_inc(gd_kv_ps, 1)
                        pe.sem_inc(gd_s_ps, 1)
                        pe.wait_ge(gd_m0, 2)
                        with pe.Fori(0, B) as b:
                            with pe.Fori(0, S2 // P) as c:
                                it = b * (S2 // P) + c
                                pe.wait_ge(gd_in, it * 16 + 16)
                                pe.wait_ge(gd_k, 1 + it)
                                pe.wait_ge(gd_v, 1 + it)
                                pe.wait_ge(gd_oT, 1 + b)
                                pe.matmul(BK[:, 0, 0:P], w_d[:, 0:D], GC, start=True, stop=True)
                                pe.matmul(BK[:, 1, 0:P], GC, w_d[:, D:2 * D], start=True, stop=True).then_inc(gd_kv_ps, 1)
                            with pe.Fori(0, H) as h:
                                it = b * H + h
                                pe.wait_ge(gd_k, 1 + b * (S2 // P) + S2 // P)
                                pe.wait_ge(gd_v, 1 + b * (S2 // P) + S2 // P)
                                pe.wait_ge(gd_q, it + 1)
                                pe.wait_ge(gd_o, 1 + it)
                                for j in range(4):
                                    ins = pe.matmul(bank(j), GQ, GK[:, j * 512:(j + 1) * 512], start=True, stop=True)
                                ins.then_inc(gd_s_ps, 1)
                                pe.wait_ge(gd_exp, it + 1)
                                for c in range(S2 // P):
                                    ins = pe.transpose(BK[:, 4 + c // 4, c % 4 * P:c % 4 * P + P], GSC[:, c * P:(c + 1) * P],
                                                       ident[:, :])
                                    if c % 4 == 3:
                                        ins.then_inc(gd_tr, 1)
                                pe.wait_ge(gd_p, 4 * it + 4)
                                for c in range(S2 // P):
                                    ins = pe.matmul(BK[:, 0, 0:D], GP[:, c, :], GV[:, c, :], start=(c == 0),
                                                    stop=(c == S2 // P - 1))
                                ins.then_inc(gd_o_ps, 1)
                            pe.wait_ge(gd_o, 1 + b * H + H)
                            pe.transpose(BK[:, 1, 0:P], GO, ident[:, :]).then_inc(gd_oT_ps, 1)
                        pe.wait_ge(gd_oT, 1 + B)
                    project(w_d[:, 3 * D:4 * D])
                if s == "E":
                    pe.wait_ge(l_silu, 1)
                    transposes(HH, 7, l_hT_ps)
                    pe.wait_ge(l_hT, 1)
                    pe.wait_ge(loads["w_e"], 48)
                    for b in range(B):
                        ins = pe.matmul(BK[:, b, 0:384], XT[:, b * P:(b + 1) * P], w_e[:, 0:384], start=True, stop=True)
                    ins.then_inc(l_qkv_ps, 1)
                    pe.wait_ge(ctx_ready, len([q for q in stages if q in "AE"]))
                    transposes(CT, 7, ctxT_ps)
                    pe.wait_ge(ctxT_ready, len([q for q in stages if q in "AE"]))
                    project(w_e[:, 384:512], 6)
                    pe.wait_ge(l_h2, 1)
                    transposes(XH, 5, ln_xT_ps)
                    pe.wait_ge(ln_xT, xT_count(LN_E2))
                    for c in range(2):
                        for j, (o, w) in enumerate(FFT):
                            bk = j if c == 0 else (3, 4, 6)[j]
                            pe.matmul(BK[0:w, bk, :], w_e[:, 512 + FF * c + o:512 + FF * c + o + w], XT[:, :],
                                      start=True, stop=True).then_inc(l_ff_ps, 1)
                    pe.wait_ge(l_ff, 3)
                    for b in range(B):
                        for j, (o, w) in enumerate(FFT):
                            ins = pe.matmul(BK[:, 7, b * P:(b + 1) * P], HF[0:w, j, b * P:(b + 1) * P], w_e2[0:w, j, :],
                                            start=(j == 0), stop=(j == 2))
                    ins.then_inc(proj_ps, 1)


_OUT = ((P, B, D), "float32")


def kernel(**inputs):
    import concourse.bacc as bacc
    from concourse.bass_utils import run_bass_kernel_spmd

    nc = bacc.Bacc("TRN2", target_bir_lowering=False, num_devices=1)
    arrays = layouts(inputs)
    t = {n: nc.dram_tensor(n + "_dram", a.shape, mybir.dt.from_np(a.dtype), kind="ExternalInput").ap()
         for n, a in arrays.items()}
    out = nc.dram_tensor("out_dram", (P, B, D), F32, kind="ExternalOutput").ap()
    program(nc, t, out)
    r = run_bass_kernel_spmd(nc, [{n + "_dram": a for n, a in arrays.items()}], core_ids=[0])
    return np.ascontiguousarray(r.results[0]["out_dram"].transpose(1, 0, 2))
```

```python
from contextlib import ExitStack

import concourse.bass as bass
import numpy as np
from concourse import mybir

F32 = mybir.dt.float32
BF16 = mybir.dt.bfloat16
I32 = mybir.dt.int32
ALU = mybir.AluOpType
ACT = mybir.ActivationFunctionType
AX = mybir.AxisListType
RMAX = bass.bass_isa.ReduceOp.max

P = 128
B = 4
D = 128
S2 = 2048
H = 16
HD = D // H
NK = 5
E1 = H * NK
QH = 64
NE = 8
HID0 = 256
HID1 = 512
FF = 352
FFT = [(0, 128), (128, 128), (256, 96)]
EPS = 1e-5
NEG = -1e9
KEPT = 3e38
TOK = B * P
SAMPLE_AT = 4
EXP_AT = 3
BACK_AT = (10, 13, 16, 19)
WARM = 13
LN_A, LN_B, LN_C, LN_D, LN_E, LN_E2, LN_F = range(7)
PAIR = (0, 1, 3, 6)


def bf16_bits(a):
    return (np.ascontiguousarray(a).view(np.uint32) >> 16).astype(np.uint16)


def constants():
    c = {}
    c["c_ident"] = np.eye(P, dtype=np.float32)
    m = np.arange(P)
    coord = np.stack([np.where(m < 32, m - 33, m - 32), m + 32])
    sel = np.zeros((99, 32, P), np.float32)
    for i in range(32):
        sel[[i, 32 + i, 64 + i], i, :] = 1.0
    sel[96:98] = -coord[:, None, :]
    sel[98] = -0.5
    half = np.zeros((3, 3, B, 2, QH), np.float32)
    half[0, :, :, 0] = half[1, :, :, 1] = half[2] = 1.0
    c["c_sel"] = bf16_bits(sel)
    c["c_half"] = bf16_bits(half.reshape(3, 3, TOK))
    e = 32 * np.arange(3)[None, :] + (np.arange(96) % 32)[:, None]
    q = np.broadcast_to(np.arange(P), (96, P))
    c["c_place"] = np.concatenate([np.where(e < E1, e % NK - 3, 0), q, q // QH * QH + 31.5], 1).astype(np.float32)
    inv = 1.0 / 10000.0 ** (np.arange(0, HD, 2, dtype=np.float32) / np.float32(HD))
    fr = np.arange(P, dtype=np.float32)[:, None] * inv[None, :].astype(np.float32)
    emb = np.concatenate([fr, fr], 1).astype(np.float32)
    cos, sin = np.cos(emb), np.sin(emb) * np.where(np.arange(HD) < HD // 2, -1, 1)
    cosT, sinT = np.tile(cos.T, (H, 1)), np.tile(sin.T, (H, 1))
    sc = 1.0 / np.sqrt(HD)
    c["c_rope0"] = np.stack([cosT * sc, sinT * sc, cosT, sinT], 1).astype(np.float32)
    gam = 1.0 - 2.0 ** (-5.0 - np.arange(H, dtype=np.float32))
    dist = np.arange(P)[None, :] - np.arange(P)[:, None]
    dec = np.where(dist[:, None] >= 0, gam[None, :, None].astype(np.float64) ** np.maximum(dist, 0)[:, None], 0.0)
    c["c_decay"] = dec.astype(np.float32)
    c["c_pos"] = -(P * np.arange(S2 // P)[None, :] + np.arange(P)[:, None]).astype(np.float32)
    c["c_head16"] = (np.arange(P)[:, None] // HD == np.arange(H)[None, :]).astype(np.float32)
    c["c_head"] = (np.arange(P)[:, None] // HD % 4 == np.arange(4)[None, :]).astype(np.float32)
    g = np.kron(np.eye(H), np.full((HD, HD), 1.0 / HD))
    c["c_group"] = np.stack([np.eye(P) - g, g], 1).astype(np.float32)
    hdk = 4
    inv = 1.0 / 10000.0 ** (np.arange(0, 2, dtype=np.float32) * 2.0 / hdk)
    fr = np.arange(B, dtype=np.float32)[:, None] * inv[None, :].astype(np.float32)
    t = np.zeros((2, B, 2, H, 2, 2), np.float32)
    t[0] = np.cos(fr)[:, None, None, None, :]
    t[1, ..., 0, :] = -np.sin(fr)[:, None, None, :]
    t[1, ..., 1, :] = np.sin(fr)[:, None, None, :]
    t[:, :, 0] *= hdk ** -0.5
    tri = np.arange(NE)[:, None] > np.arange(NE)[None, :]
    c["c_rows"] = np.concatenate([t.reshape(-1), tri.reshape(-1)]).astype(np.float32)[None]
    return c


ROWS = {}
_at = 0
for _n, _w in (("bkv", 256), ("bq", D), ("bo", D), ("ff_bo", D), ("x_bv", D), ("x_bo", D), ("rw", 2 * D)):
    ROWS[_n] = slice(_at, _at + _w)
    _at += _w
NROWS = _at
EARLY = ROWS["bo"].stop
ROPE1 = slice(0, 1024)
BEFORE = slice(1024, 1088)
WE_R, WE_G, WE_O, WE_FF = 256, 288, 416, 544
COLS = {n: i for i, n in enumerate(
    ["bq", "gn_w", "gn_b", "x_bq", "x_bk", "eps", "ln1_w", "ln1_b", "conv0", "conv1", "ln2_w", "ln2_b"])}
B1COL = len(COLS)
NCOLS = B1COL + NE * 4


def layouts(i):
    f = lambda n: np.asarray(i[n])
    a = {}
    a["x"] = f("x").transpose(1, 0, 2)
    ctxT = f("ctx_1024").transpose(2, 0, 1)
    a["ctxT"] = ctxT
    a["mask_b"] = f("mask_BxS2_if0").astype(np.int32)
    a["mask_q"] = f("mask_1x1xSxS2_ik0")[0, 0].astype(np.int32)
    wk = f("L0_xattn_Wk").T.reshape(D, H, 1, HD)
    wv = f("L0_xattn_Wv").T.reshape(D, H, 1, HD)
    wkv = np.concatenate([wk, wv], 2).reshape(D, 2 * D)
    woff = np.concatenate([f("L0_xattn_Woff").T, np.zeros((D, 16), np.float32)], 1).reshape(D, 3, 1, 32)
    woff = np.broadcast_to(woff, (D, 3, 3, 32)).reshape(D, 288)
    a["w_a"] = np.concatenate([wkv, f("L0_xattn_Wq").T, woff, f("L0_xattn_Wo").T], 1)
    boff = np.concatenate([f("L0_xattn_boff"), np.zeros(16, np.float32)]).reshape(3, 1, 32)
    a["boff"] = np.broadcast_to(boff, (3, 3, 32)).reshape(3, 96).T
    rot = lambda w: w.T.reshape(D, H, 2, HD // 2)[:, :, ::-1].reshape(D, D)
    a["w_b"] = np.concatenate([f("L0_attn_Wq").T, rot(f("L0_attn_Wq")), f("L0_attn_Wk").T, rot(f("L0_attn_Wk")),
                               f("L0_attn_Wv").T, f("L0_attn_Wo").T], 1)
    a["w_c"] = np.concatenate([f("L0_ffn_Wg").T, f("L0_ffn_Wo").T.reshape(2, P, D).transpose(1, 0, 2).reshape(P, 2 * D)], 1)
    a["w_c1"] = f("L0_ffn_W1").transpose(2, 0, 1).reshape(D, NE * 2 * HID0)
    a["w_d"] = np.concatenate([f("L1_xattn_W" + n).T for n in "kvqo"], 1)
    a["w_e"] = np.concatenate([f("L1_attn_W" + n) for n in ("q", "k", "v", "g", "out")] + [f("L1_attn_w1"), f("L1_attn_w3")], 1)
    w2 = np.concatenate([f("L1_attn_w2"), np.zeros((3 * P - FF, D), np.float32)]).reshape(3, P, D)
    a["w_e2"] = w2.transpose(1, 0, 2)
    a["w_f"] = f("L1_ffn_router_w").T
    a["w_f1"] = f("L1_ffn_w1").transpose(1, 0, 2).reshape(D, NE * HID1)
    a["w_f2"] = f("L1_ffn_w2").reshape(NE, 4, P, D).transpose(2, 0, 1, 3).reshape(P, NE * 4 * D)
    bkv = np.concatenate([f("L0_xattn_bk").reshape(H, 1, HD), f("L0_xattn_bv").reshape(H, 1, HD)], 1)
    cw = f("L1_attn_conv_w").T
    a["rows"] = np.concatenate([bkv.reshape(-1), f("L0_xattn_bq"), f("L0_xattn_bo"), f("L0_ffn_bo"), f("L1_xattn_bv"), f("L1_xattn_bo"),
                                f("L1_attn_router_w").transpose(2, 0, 1).reshape(-1)])[None]
    cols = [f("L0_xattn_bq"), f("L0_attn_gn_weight"), f("L0_attn_gn_bias"), f("L1_xattn_bq"), f("L1_xattn_bk"),
            np.full(D, EPS, np.float32), f("L1_attn_ln1_w"), f("L1_attn_ln1_b"), cw[0], cw[1],
            f("L1_attn_ln2_w"), f("L1_attn_ln2_b")]
    a["cols"] = np.concatenate([np.stack(cols, 1), f("L0_ffn_b1").reshape(NE * 4, P).T], 1)
    a.update(constants())
    return {k: np.ascontiguousarray(v) for k, v in a.items()}


STAGES = "ABCDEF"


def program(nc, t, out):
    ctx = ExitStack()
    with ctx:
        def sb(name, shape, dt=F32):
            return ctx.enter_context(nc.sbuf_tensor(name, shape, dt))

        def sem(name):
            return ctx.enter_context(nc.semaphore(name))

        FLA = sb("FLA", [P, 2])
        FLD = sb("FLD", [P, 2])
        GNA = sb("GNA", [P, 2])
        FAI = sb("FAI", [1, 1], I32)
        FDI = sb("FDI", [1, 1], I32)
        VM3 = sb("VM3", [96, 3])
        MKB = sb("MKB", [P, B, S2 // P], I32)
        pos = sb("pos_sb", [P, S2 // P])
        head16 = sb("head16_sb", [P, H])
        X = sb("X", [P, B, D])
        XH = sb("XH", [P, B, D])
        XT = sb("XT", [P, TOK])
        XB = sb("XB", [P, B, D])
        STAT = sb("STAT", [P, B, 6])
        MV = sb("MV", [P, B, 2])
        VE = sb("VE", [P, B])
        RSTD = sb("RSTD", [P, B])
        MHALF = sb("MHALF", [P, B])
        ident = sb("ident", [P, P])
        rows = sb("rows_sb", [P, NROWS])
        crows = sb("crows_sb", [P, 1088])
        cols = sb("cols_sb", [P, NCOLS])
        head = sb("head_sb", [P, 4])
        row = lambda n: rows[:, ROWS[n]]
        col = lambda n: cols[:, COLS[n]:COLS[n] + 1]
        w_a = sb("w_a_sb", [P, 256 + D + 288 + D])
        w_b = sb("w_b_sb", [P, 6 * D])
        w_c = sb("w_c_sb", [P, 8 + 2 * D])
        w_d = sb("w_d_sb", [P, 4 * D])
        w_e = sb("w_e_sb", [P, WE_FF + 2 * FF])
        w_e2 = sb("w_e2_sb", [P, 3, D])
        w_f = sb("w_f_sb", [P, 8])
        def room(tile, width):
            at = [0]

            def take(shape):
                n = int(np.prod(shape[1:]))
                v = tile[:, at[0]:at[0] + n]
                at[0] += n
                assert at[0] <= width
                names = "abcd"[:len(shape) - 1]
                return v.rearrange(f"p ({' '.join(names)}) -> p {' '.join(names)}", **dict(zip(names, shape[1:])))

            return take

        SCR = sb("SCR", [P, 5120])
        before_b = room(SCR, 5120)
        KVW = sb("KVW", [P, 2 * B, 2 * D + 16])
        boff = sb("boff_sb", [96, 3])
        ybias = sb("ybias", [96, 3])
        place = sb("place", [96, 3 + 2 * P])
        refc, loc, mid = place[:, 0:3], place[:, 3:3 + P], place[:, 3 + P:3 + 2 * P]
        QpT = before_b([P, TOK])
        Qq = before_b([P, B, D])
        Y = before_b([P, 3, TOK])[0:96]
        YW, YW2 = before_b([P, TOK])[0:96], before_b([P, TOK])[0:96]
        IX, IX2 = before_b([P, TOK])[0:96], before_b([P, TOK])[0:96]
        Rh2 = before_b([P, TOK // 2])[0:96].bitcast(BF16)
        Rh = sb("Rh", [96, TOK], BF16)
        R = sb("R", [99, 3, TOK], BF16)
        SELR = sb("SELR", [P, 2048])
        SEL = SELR[:, :].bitcast(BF16)[0:99].rearrange("p (e m) -> p e m", e=32)
        after_sel = room(SELR, 2048)
        WT = sb("WT", [P, 2, 4, 2 * B, NK, QH])
        KEEP = sb("KEEP", [P, 5120])

        WTF = WT[:, :, :, :, :, :].rearrange("p a h i k q -> p (a h i k q)")
        first = room(WTF, 20480)
        WIN = first([P, B, 192])
        ga = room(WTF, 20480)
        GCH = ga([P, P])
        GKV = ga([P, 2 * D + 16])
        GW = ga([P, 4, NK, P])
        GIX = ga([P, 3, TOK])[0:96]
        GT1 = ga([P, 3, TOK])[0:96]
        GSM = ga([P, 4, B])
        GPOS = ga([P, 1])
        gd = room(WTF, 12288)
        GK = gd([P, S2])
        GV = gd([P, S2 // P, D])
        GSC = gd([P, S2])
        GP = gd([P, S2 // P, P])
        GM = gd([P, S2])
        GMI = GM.bitcast(I32)
        GC = gd([P, P])
        GQ = gd([P, P])
        GO = gd([P, D])
        GR = gd([P, 4])
        later = room(WTF, 20480)
        PT = later([P, 2, H, P])
        keep = room(KEEP, 5120)
        after = room(KEEP, 5120)
        w_c1 = later([P, NE * 2 * HID0])
        after_c = room(w_c1, 4096)
        after_a = room(SCR, 5120)
        GT = later([P, 2, 4, TOK])
        w_f1 = later([P, NE * HID1])
        w_f2 = later([P, NE * 4 * D])
        early = room(KEEP[:, B * NK * P:5120], 5120 - B * NK * P)
        TAIL = early([P, B, P])
        MKF = early([P, S2]).bitcast(I32)
        SK = keep([P, B, NK, P])
        PRD = sb("PRD", [P, NK, 4, HD])
        SCO = sb("SCO", [P, B, H, NK])
        GSK = SK.rearrange("p b k q -> p b (k q)")
        VS = keep([P, B, H, NK * HD]).rearrange("p b h (k d) -> p b h k d", k=NK)
        SM1 = sb("SM1", [P, B, H])
        SM2 = sb("SM2", [P, B, H])
        CT = sb("CT", [P, B, D])
        CTT = sb("CTT", [P, TOK])
        rope0 = sb("rope0", [P, 4, P])
        group = sb("group_sb", [P, 2, P])
        decay = sb("decay", [P, H, P])
        T0 = after([P, B, P])
        T1 = after([P, B, P])
        qT = after([P, B, P])
        kT = after([P, B, P])
        vq = after([P, B, P])
        OM = after([P, 4, P])
        QB = room(SCR, 5120)([P, 2, H, P])
        PR = sb("PR", [P, B, NE])
        EX = sb("EX", [P, B, NE])
        CMP = after_sel([P, B, NE, NE])
        CMQ = after_sel([P, B, NE, NE])
        RK = sb("RK", [P, B, NE])
        S1 = sb("S1", [P, B])
        CW = sb("CW", [P, B, NE])
        SG = room(KVW[:, :, :].rearrange("p i n -> p (i n)"), 2176)([P, 2, 2, TOK])
        PO = SG.rearrange("p a j n -> p (a j n)")[:, 0:10 * D].rearrange("p (i n) -> p i n", i=10)
        mtail = sb("mtail", [P, P], I32)
        MB = sb("MB", [P, P])
        kTd = sb("kTd", [P, B, P])
        vd = sb("vd", [P, B, P])
        SS = GT.rearrange("p a j n -> p (a j n)").rearrange("p (a h k) -> p a h k", a=2, h=H)
        MX = sb("MX", [P, B, H])
        ones = sb("ones", [P, P])
        DN = after([P, 4, P])
        XN = after_c([P, B, D])
        HT = after_c([P, TOK])
        VEX = sb("VEX", [P, B])
        RSTDX = sb("RSTDX", [P, B])
        MIX = sb("MIX", [P, 4])
        QK = after_a([P, B, 2, 64])
        QR = after_a([P, B, 2, 64])
        Q2 = after_a([P, B, 2, 64])
        VV = after_c([P, B, D])
        GS = after_c([P, B, D])
        LGT = sb("LGT", [P, 2, B, H])
        LGE = sb("LGE", [P, 2, B, H])
        PDT = after_a([P, 10, 64])
        NS = after_a([P, B, H])
        OH = sb("OH", [P, B, H])
        SMM = after_a([P, 10, H])
        DT = after_a([P, 10, H])
        OO = after_c([P, B, D])
        OQ = after_c([P, B, D])
        HF = room(decay[:, :, :].rearrange("p h t -> p (h t)"), 2048)([P, 3, TOK])

        BK = ctx.enter_context(nc.psum_tensor("BK", [P, 8, 512], F32))
        bank = lambda i: BK[:, i, :]

        loads = {n: sem("in_" + n) for n in (
            "x", "ident", "rows", "crows", "cols", "w_a", "win", "tail", "pos", "sel", "w_b", "w_c",
            "w_c1", "w_d", "w_e", "w_f1", "w_f2", "decay", "flags")}
        dve_chain = sem("dve_chain")
        act_chain = sem("act_chain")
        pool_chain = sem("pool_chain")
        ln_var, ln_rstd, ln_xhat = sem("ln_var"), sem("ln_rstd"), sem("ln_xhat")
        ln_xT_ps, ln_xT = sem("ln_xT_ps"), sem("ln_xT")
        consts_ready = sem("consts_ready")
        kvw_ps, kvw_ready = sem("kvw_ps"), sem("kvw_ready")
        kd_ps, kd_ready, vd_ready = sem("kd_ps"), sem("kd_ready"), sem("vd_ready")
        a_q_ps, a_qT, a_qq, a_off_ps, a_y, a_r = (sem("a_" + n) for n in ("q_ps", "qT", "qq", "off_ps", "y", "r"))
        a_sk_odd = sem("a_sk_odd")
        a_ix_ps, a_abs, a_w = sem("a_ix_ps"), sem("a_abs"), sem("a_w")
        a_samp_ps, a_sk_even, a_tr_ps, a_prod, a_vs = (sem("a_" + n) for n in ("samp_ps", "sk_even", "tr_ps", "prod", "vs"))
        a_z, a_exp, a_dev, a_sco, a_soft, a_ctx = (sem("a_" + n) for n in ("z", "exp", "dev", "sco", "soft", "ctx"))
        ctx_ready, ctxT_ps, ctxT_ready, proj_ps = (sem(n) for n in ("ctx_ready", "ctxT_ps", "ctxT_ready", "proj_ps"))
        xb_ready, x_ready = sem("xb_ready"), sem("x_ready")
        b_qk_ps, b_v_ps, b_rot, b_v = (sem("b_" + n) for n in ("qk_ps", "v_ps", "rot", "v"))
        b_blk, b_blk3, b_s_ps, b_pt, b_o_ps, b_oT, b_oc_ps = (sem("b_" + n) for n in ("blk", "blk3", "s_ps", "pt", "o_ps", "oT", "oc_ps"))
        b_sq, b_var_ps, b_std, b_on = (sem("b_" + n) for n in ("sq", "var_ps", "std", "on"))
        r_lg_ps, r_z, r_exp, r_cw = (sem("r_" + n) for n in ("lg_ps", "z", "exp", "cw"))
        e_h_ps, e_act, e_g, e_y_ps, e_sum = (sem("e_" + n) for n in ("h_ps", "act", "g", "y_ps", "sum"))
        d_mb, d_q_ps, d_q, d_blk, d_s_ps, d_ss, d_mx, d_exp = (
            sem("d_" + n) for n in ("mb", "q_ps", "q", "blk", "s_ps", "ss", "mx", "exp"))
        d_pT_ps, d_pT, d_o_ps, d_om = (sem("d_" + n) for n in ("pT_ps", "pT", "o_ps", "om"))
        l_hc, l_vex, l_mix, l_qkv_ps, l_qkv, l_rot, l_rstdx = (
            sem("l_" + n) for n in ("hc", "vex", "mix", "qkv_ps", "qkv", "rot", "rstdx"))
        l_ld, l_le, l_oc, l_sq, l_vs, l_std, l_ff_ps, l_ffs, l_ff, l_xa = (
            sem("l_" + n) for n in ("ld", "le", "oc", "sq", "vs", "std", "ff_ps", "ffs", "ff", "xa"))
        flag_rows, flag_all, flag_a, flag_d = (sem("flag_" + n) for n in ("rows", "all", "a", "d"))
        ga_chain = sem("ga_chain")
        ga_in, ga_sum_ps, ga_pos, ga_ix, ga_abs, ga_w, ga_kv_ps, ga_kv = (
            sem("ga_" + n) for n in ("in", "sum_ps", "pos", "ix", "abs", "w", "kv_ps", "kv"))
        ga_samp, ga_add, ga_zero, ga_tr, ga_prod, ga_out, ga_z, ga_exp, ga_ctx = (
            sem("ga_" + n) for n in ("samp", "add", "zero", "tr", "prod", "out", "z", "exp", "ctx"))
        gd_in, gd_mask, gd_m0, gd_kv_ps, gd_k, gd_v = (sem("gd_" + n) for n in ("in", "mask", "m0", "kv_ps", "k", "v"))
        gd_q, gd_s_ps, gd_chain, gd_neg, gd_exp, gd_tr, gd_p, gd_o_ps, gd_o, gd_oT_ps, gd_oT = (
            sem("gd_" + n) for n in ("q", "s_ps", "chain", "neg", "exp", "tr", "p", "o_ps", "o", "oT_ps", "oT"))
        stored = sem("stored")

        PROJ = "ABDE"
        BIASED = "ADE"
        FFNS = "CF"
        CTXT = "AE"
        nx = {s: i for i, s in enumerate(STAGES)}

        def stages_done(eng, n, half=1):
            before = STAGES[:n]
            done = len([q for q in before if (q in "CF") == (before[-1] in "CF")])
            if before[-1] in "CF":
                eng.wait_ge(e_sum, 2 * NE * done - 1 + half)
            else:
                eng.wait_ge(x_ready, 2 * done - 1 + half)

        block = ctx.enter_context(nc.Block())

        def flagged(eng, ready, tile):
            eng.wait_ge(ready, 1)
            return eng.value_load(tile[0:1, 0:1]) != 0

        xhat_count = lambda n: 4 * n + 4
        xT_count = lambda n: n + 1

        def sampled(i, n):
            b, hf = i // 2, i % 2
            return (SK[:, b, :, QH * hf:QH * hf + QH],
                    BK[:, sample_bank(n), 0:NK * QH].rearrange("p (k q) -> p k q", k=NK))

        SPARE_FROM = 26

        def sample_bank(n):
            return (3, 4, 0, 7)[n % 4] if n >= 24 else 3 + n % 2

        def back_banks(u):
            return 1 if u in (13, 15) else 5

        def transposed_unit(u):
            v = BK[:, back_banks(u):back_banks(u) + 2, :].rearrange("p a n -> p (a n)")[:, 0:NK * P]
            return v.rearrange("p (k h r) -> p k h r", k=NK, h=4)

        def vcopy(act, u):
            G, b = u // 4, u % 4
            act.wait_ge(a_prod, u + 1)
            src = transposed_unit(u).rearrange("p k h r -> p h k r")
            act.activation(VS[:, b, 4 * G:4 * G + 4, :, :], src[:, :, :, HD:2 * HD], ACT.Copy).then_inc(a_vs, 1)

        sbank = lambda e: bank((0, 1, 2, 7)[e % 4])
        FLAG_AT = 26
        TAIL_AT = 14

        def halves_of(bk0, bk1):
            return [BK[:, bk, 256 * h:256 * h + 256].rearrange("p (b n) -> p b n", b=2) for h, bk in enumerate((bk0, bk1))]

        HBANKS = (0, 1, 2, 3, 6, 7)
        hbank = lambda u: bank(HBANKS[u % 6])
        PAIRS = 2 * NE
        before_f = PAIRS

        @block.sync
        def _(sp):
            def load(dst, src, s):
                sp.dma_start(dst, src).then_inc(loads[s], 16)

            load(X[:, :, :], t["x"], "x")
            load(w_a[:, :], t["w_a"], "w_a")
            load(boff[:, :], t["boff"], "pos")
            load(place[:, :], t["c_place"], "pos")
            load(cols[:, :], t["cols"], "cols")
            load(WIN[:, :, 0:32], t["ctxT"][:, :, S2 - 32:S2], "win")
            load(WIN[:, :, 32:192], t["ctxT"][:, :, 0:160], "win")
            load(w_d[:, :], t["w_d"], "w_d")
            load(TAIL[:, :, :], t["ctxT"][:, :, S2 - P:S2], "tail")
            load(rows[:, EARLY:], t["rows"][:, EARLY:].to_broadcast([P, NROWS - EARLY]), "crows")
            load(MKF, t["mask_q"], "flags")
            load(MKB[:, :, :], t["mask_b"].rearrange("b (p j) -> p b j", p=P), "flags")
            load(pos[:, :], t["c_pos"], "flags")
            load(head16[:, :], t["c_head16"], "flags")
            load(mtail[:, :], t["mask_q"][:, S2 - P:S2], "flags")
            load(w_b[:, :], t["w_b"], "w_b")
            load(head[:, :], t["c_head"], "decay")
            load(w_c[:, :], t["w_c"], "w_c")
            load(w_e[:, 0:WE_R], t["w_e"][:, 0:WE_R], "w_e")
            load(w_e[:, WE_G:], t["w_e"][:, WE_R:], "w_e")
            load(w_e2[:, :, :], t["w_e2"], "w_e")
            load(w_f[:, :], t["w_f"], "w_e")
            with sp.If(flagged(sp, flag_a, FAI)):
                with sp.Fori(0, B) as b:
                    with sp.Fori(0, S2 // P) as c:
                        sp.wait_ge(ga_kv_ps, 1 + b * (S2 // P) + c)
                        sp.dma_start(GCH, t["ctxT"][:, bass.ds(b, 1), bass.ds(c * P, P)].rearrange("p b n -> p (b n)"))\
                          .then_inc(ga_in, 16)
                sp.wait_ge(ga_out, 1 + 4 * B)
            sp.wait_ge(a_samp_ps, 32)
            sp.wait_ge(flag_d, 1)
            load(w_c1, t["w_c1"], "w_c1")
            load(w_f1, t["w_f1"], "w_f1")
            load(w_f2, t["w_f2"], "w_f2")
            with sp.If(flagged(sp, flag_d, FDI)):
                sp.wait_ge(d_om, B)
                sp.dma_start(GMI, t["mask_q"]).then_inc(gd_mask, 16)
                with sp.Fori(0, B) as b:
                    with sp.Fori(0, S2 // P) as c:
                        sp.wait_ge(gd_kv_ps, 1 + b * (S2 // P) + c)
                        sp.dma_start(GC, t["ctxT"][:, bass.ds(b, 1), bass.ds(c * P, P)].rearrange("p b n -> p (b n)"))\
                          .then_inc(gd_in, 16)
            stages_done(sp, len(STAGES))
            sp.dma_start(out, X[:, :, :]).then_inc(stored, 16)
            sp.wait_ge(stored, 16)

        @block.gpsimd
        def _(pool):
            chain = [0]

            def settle(ins):
                chain[0] += 1
                ins.then_inc(pool_chain, 1)
                pool.wait_ge(pool_chain, chain[0])

            pool.memset(MHALF[:, :], -0.5).then_inc(consts_ready, 1)
            pool.memset(KVW[:, :, 2 * D:2 * D + 16], 0.0).then_inc(consts_ready, 1)
            pool.memset(ones[:, :], 1.0).then_inc(consts_ready, 1)
            pool.wait_ge(consts_ready, 3)

            def power(n):
                for h in range(2):
                    pool.wait_ge(ln_var, 2 * n + 1 + h)
                    pair = slice(2 * h, 2 * h + 2)
                    pool.tensor_tensor(RSTD[:, pair], VE[:, pair], MHALF[:, pair], ALU.pow).then_inc(ln_rstd, 1)

            def with_bias(n, name):
                stages_done(pool, n) if n else pool.wait_ge(loads["x"], 16)
                pool.wait_ge(loads["rows"], 16) if name == "bo" else pool.wait_ge(loads["crows"], 32)
                pool.tensor_tensor(XB[:, :, :], X[:, :, :], row(name).unsqueeze(1).to_broadcast([P, B, D]),
                                   ALU.add).then_inc(xb_ready, 1)

            def tail():
                pool.wait_ge(flag_rows, 1)
                pool.partition_all_reduce(FLD[:, 1:2], FLD[:, 0:1], P, RMAX).then_inc(flag_all, 1)

            power(LN_A)
            for s in STAGES:
                if s == "A":
                    for g in (1, 2):
                        pool.wait_ge(a_y, g)
                        settle(pool.tensor_scalar(YW2[:, :], Y[:, g, :], 0.0, -1.0, ALU.is_lt, ALU.mult))
                        settle(pool.tensor_scalar(IX2[:, :], Y[:, g, :], float(S2) / (S2 - 1), None, ALU.mult))
                        settle(pool.tensor_tensor(IX2[:, :], IX2[:, :], YW2[:, :], ALU.add))
                        if g == 1:
                            pool.wait_ge(loads["sel"], 32)
                        settle(pool.tensor_copy(R[0:96, g, :], IX2[:, :]))
                        settle(pool.tensor_tensor(IX2[:, :], IX2[:, :], R[0:96, g, :], ALU.subtract))
                        settle(pool.tensor_copy(Rh2[:, :], IX2[:, :]))
                        settle(pool.tensor_tensor(YW2[:, :], IX2[:, :], Rh2[:, :], ALU.subtract))
                        settle(pool.tensor_copy(R[32:64, g, :], Rh2[32:64, :]))
                        pool.tensor_copy(R[64:96, g, :], YW2[64:96, :]).then_inc(a_r, 1)
                        pool.wait_ge(a_r, g + 1)
                    by_query = mid.unsqueeze(1).to_broadcast([96, B, P])
                    for g, dst in ((1, YW2), (2, IX2)):
                        ins = pool.tensor_tensor(dst.rearrange("p (b q) -> p b q", b=B),
                                                 Y[:, g, :].rearrange("p (b q) -> p b q", b=B), by_query, ALU.subtract)
                        ins.then_inc(a_dev, 1)
                        pool.wait_ge(a_dev, g)
                    tail()
                    with_bias(nx[s], "bo")
                    pool.wait_ge(flag_rows, 2)
                    pool.partition_all_reduce(FLA[:, 1:2], FLA[:, 0:1], P, RMAX).then_inc(flag_all, 1)
                if s == "B":
                    power(LN_B)
                    pool.wait_ge(b_rot, 1)
                    pool.wait_ge(loads["flags"], 80)
                    for b in range(B):
                        if b >= 2:
                            pool.wait_ge(b_s_ps, 4 * (b - 1))
                        pool.tensor_tensor(QB[:, b % 2, 12:16, :], qT[:, b, :].unsqueeze(1).to_broadcast([P, 4, P]),
                                           head16[:, 12:16].unsqueeze(2).to_broadcast([P, 4, P]), ALU.mult)\
                            .then_inc(b_blk3, 1)
                if s in "CF":
                    power(LN_C if s == "C" else LN_F)
                if s == "D":
                    def keys(b):
                        for g in range(4):
                            pool.tensor_tensor(QB[:, b % 2, 4 * g:4 * g + 4, :], kTd[:, b, :].unsqueeze(1).to_broadcast([P, 4, P]),
                                               head16[:, 4 * g:4 * g + 4].unsqueeze(2).to_broadcast([P, 4, P]), ALU.mult)\
                                .then_inc(d_blk, 1)

                    pool.wait_ge(b_s_ps, 16)
                    pool.wait_ge(kd_ready, 1)
                    keys(0)
                    keys(1)
                    power(LN_D)
                    with_bias(nx[s], "x_bo")
                    for b in (2, 3):
                        pool.wait_ge(d_s_ps, 4 * (b - 1))
                        keys(b)
                if s == "E":
                    power(LN_E)
                    pool.wait_ge(l_vex, 1)
                    pool.tensor_tensor(RSTDX[:, :], VEX[:, :], MHALF[:, :], ALU.pow).then_inc(l_rstdx, 1)
                    pool.wait_ge(loads["crows"], 32)
                    pool.wait_ge(l_qkv, 3)
                    cs = crows[:, ROPE1].rearrange("p (a n) -> p a n", a=2)
                    qk = QK[:, :, :, :].rearrange("p b a n -> p (b a n)")
                    q2 = Q2[:, :, :, :].rearrange("p b a n -> p (b a n)")
                    halves = lambda a: a.rearrange("p (n f i) -> p n f i", f=2, i=2)
                    settle(pool.tensor_tensor(QR[:, :, :, :].rearrange("p b a n -> p (b a n)"), qk, cs[:, 0, :], ALU.mult))
                    for f in range(2):
                        settle(pool.tensor_tensor(halves(q2)[:, :, f, :], halves(qk)[:, :, 1 - f, :],
                                                  halves(cs[:, 1, :])[:, :, f, :], ALU.mult))
                    pool.tensor_tensor(QR[:, :, :, :], QR[:, :, :, :], Q2[:, :, :, :], ALU.add).then_inc(l_rot, 1)
                    power(LN_E2)
                    pool.wait_ge(l_xa, 2)
                    pool.tensor_tensor(XB[:, :, :], X[:, :, :], CT[:, :, :], ALU.add).then_inc(xb_ready, 1)

        @block.scalar
        def _(act):
            chain = [0]

            def settle(ins):
                chain[0] += 1
                ins.then_inc(act_chain, 1)
                act.wait_ge(act_chain, chain[0])

            def load(dst, src, s):
                act.dma_start(dst, src).then_inc(loads[s], 16)

            load(ident[:, :], t["c_ident"], "ident")
            load(rows[:, 0:EARLY], t["rows"][:, 0:EARLY].to_broadcast([P, EARLY]), "rows")
            load(R[96:99, :, :], t["c_half"].bitcast(BF16), "sel")
            load(SEL[:, :, :], t["c_sel"].bitcast(BF16), "sel")

            def norm_T(n, bk):
                act.wait_ge(ln_xT_ps, xT_count(n))
                act.activation(XT[:, :], bank(bk), ACT.Copy).then_inc(ln_xT, 1)

            def ctx_T(s, bk):
                k = CTXT.index(s)
                act.wait_ge(ctxT_ps, k + 1)
                act.activation(CTT[:, :], bank(bk), ACT.Copy, scale=-0.5 if s == "A" else 1.0).then_inc(ctxT_ready, 1)

            def tail():
                act.wait_ge(kd_ps, 1)
                act.activation(kTd[:, :, :], bank(3), ACT.Identity, bias=col("x_bk")).then_inc(kd_ready, 1)

            for s in STAGES:
                if s == "A":
                    norm_T(LN_A, 5)
                    act.wait_ge(loads["cols"], 16)
                    act.wait_ge(a_q_ps, 1)
                    act.activation(QpT[:, :], bank(6), ACT.Identity, bias=col("bq")).then_inc(a_qT, 1)
                    load(rope0[:, :, :], t["c_rope0"], "decay")
                    load(group[:, :, :], t["c_group"], "decay")
                    load(decay[:, :, :], t["c_decay"], "decay")
                    load(crows[:, :], t["c_rows"].to_broadcast([P, 1088]), "crows")

                    def evac(G, i):
                        n = 8 * G + i
                        act.wait_ge(a_samp_ps, n + 1)
                        if G and i == 1:
                            act.wait_ge(a_tr_ps, 4 * G)
                        dst, src = sampled(i, n)
                        act.activation(dst, src, ACT.Copy).then_inc(a_sk_odd, 1)

                    def exponentials(G):
                        act.wait_ge(a_z, G + 1)
                        z = SCO[:, :, 4 * G:4 * G + 4, :]
                        act.activation(z, z, ACT.Exp).then_inc(a_exp, 1)

                    for e in range(E1):
                        G = e // 20
                        act.wait_ge(a_ix_ps, e + 1)
                        if G >= 2 and e % 20 == 0:
                            act.wait_ge(a_samp_ps, 8 * (G - 1))
                        act.activation(WT[:, G % 2, e % 20 // NK, :, e % NK, :], sbank(e), ACT.Abs)\
                           .then_inc(a_abs, 1)
                        if e == TAIL_AT:
                            tail()
                        if G and e % 20 in BACK_AT:
                            u = 4 * (G - 1) + BACK_AT.index(e % 20)
                            if u == 0:
                                act.wait_ge(kd_ps, 2)
                                act.wait_ge(flag_rows, 1)
                            vcopy(act, u)
                        if G and e % 20 - SAMPLE_AT in (1, 3, 5, 7):
                            evac(G - 1, e % 20 - SAMPLE_AT)
                        if G >= 2 and e % 20 == EXP_AT:
                            exponentials(G - 2)
                    exponentials(2)
                    evac(3, 1)
                    evac(3, 3)
                    vcopy(act, 12)
                    evac(3, 5)
                    vcopy(act, 13)
                    evac(3, 7)
                    vcopy(act, 14)
                    vcopy(act, 15)
                    exponentials(3)
                    with act.If(flagged(act, flag_a, FAI)):
                        act.sem_inc(ga_abs, 1)
                        act.wait_ge(ga_pos, 1)
                        with act.Fori(0, B) as b:
                            with act.Fori(0, S2 // P) as c:
                                it = b * (S2 // P) + c
                                act.wait_ge(ga_kv, 1 + 2 * it + 2)
                                for e in range(E1):
                                    if e % 20 == 0:
                                        act.wait_ge(ga_samp, 1 + it * 4 + e // 20)
                                    act.wait_ge(ga_ix, it * E1 + e + 1)
                                    act.activation(GW[:, e % 20 // NK, e % NK, :], BK[:, 0, 0:P], ACT.Abs,
                                                   bias=GPOS).then_inc(ga_abs, 1)
                        act.wait_ge(ga_z, 1)
                        act.activation(SCO[:, :, :, :], SCO[:, :, :, :], ACT.Exp).then_inc(ga_exp, 1)
                    ctx_T("A", 6)
                if s == "B":
                    norm_T(LN_B, 7)
                    act.wait_ge(b_v_ps, 1)
                    act.activation(vq[:, :, :], bank(4), ACT.Copy).then_inc(b_v, 1)
                    act.wait_ge(b_rot, 1)
                    act.wait_ge(loads["flags"], 80)
                    for b in range(B):
                        if b >= 2:
                            act.wait_ge(b_s_ps, 4 * (b - 1))
                        for h in range(12):
                            ins = act.activation(QB[:, b % 2, h, :], qT[:, b, :], ACT.Copy, scale=head16[:, h:h + 1])
                            if h % 4 == 3:
                                ins.then_inc(b_blk, 1)
                    act.wait_ge(b_oc_ps, 1)
                    act.activation(T0[:, :, :], bank(4), ACT.Square).then_inc(b_sq, 1)
                    act.wait_ge(b_var_ps, 1)
                    act.activation(T1[:, :, :], bank(5), ACT.Sqrt, bias=col("eps")).then_inc(b_std, 1)
                if s in "CF":
                    k = FFNS.index(s)
                    norm_T(LN_C if s == "C" else LN_F, 7)
                    act.wait_ge(r_z, k + 1)
                    act.activation(EX[:, :, :], EX[:, :, :], ACT.Exp).then_inc(r_exp, 1)
                    for e in range(NE):
                        n = k * NE + e
                        if s == "C":
                            for p in (2 * e, 2 * e + 1):
                                act.wait_ge(e_h_ps, p + 1)
                                if p >= 4:
                                    act.wait_ge(e_g, p - 3)
                                o = B1COL + 4 * e + 2 + p % 2
                                act.activation(SG[:, e % 2, p % 2, :], hbank(2 * p + 1), ACT.Sigmoid, bias=cols[:, o:o + 1])\
                                   .then_inc(e_act, 1)
                        else:
                            if e >= 2:
                                act.wait_ge(e_y_ps, n - 1)
                            for u in range(4 * e, 4 * e + 4):
                                act.wait_ge(e_h_ps, before_f + u + 1)
                                act.activation(GT[:, e % 2, u % 4, :], hbank(u), ACT.Gelu).then_inc(e_act, 1)
                if s == "D":
                    norm_T(LN_D, 7)
                    act.wait_ge(d_q_ps, 1)
                    act.activation(qT[:, :, :], bank(6), ACT.Identity, bias=col("x_bq")).then_inc(d_q, 1)
                    for b in range(B):
                        for g in range(4):
                            n = 4 * b + g
                            act.wait_ge(d_mx, n + 1)
                            for h in range(4 * g, 4 * g + 4):
                                ins = act.activation(SS[:, b % 2, h, :], SS[:, b % 2, h, :], ACT.Exp, scale=-1.0,
                                                     bias=MX[:, b, h:h + 1])
                            ins.then_inc(d_exp, 1)
                        for g in range(4):
                            n = 4 * b + g
                            act.wait_ge(d_pT_ps, n + 1)
                            if b >= 2 and g == 0:
                                act.wait_ge(d_o_ps, b - 1)
                            act.activation(PT[:, b % 2, 4 * g:4 * g + 4, :], bank(4 + n % 2), ACT.Copy)\
                               .then_inc(d_pT, 1)
                    with act.If(flagged(act, flag_d, FDI)):
                        act.sem_inc(gd_k, 1)
                        act.wait_ge(d_om, B)
                        with act.Fori(0, B) as b:
                            with act.Fori(0, S2 // P) as c:
                                it = b * (S2 // P) + c
                                act.wait_ge(gd_kv_ps, 1 + it + 1)
                                act.activation(GK[:, bass.ds(c * P, P)], BK[:, 0, 0:P], ACT.Identity, bias=col("x_bk"))\
                                   .then_inc(gd_k, 1)
                            with act.Fori(0, H) as h:
                                it = b * H + h
                                act.wait_ge(gd_neg, it + 1)
                                act.activation(GSC, GSC, ACT.Exp, bias=GR[:, 0:1], accum_out=GR[:, 1:2]).then_inc(gd_exp, 1)
                                for j in range(4):
                                    act.wait_ge(gd_tr, 4 * it + j + 1)
                                    act.activation(GP[:, 4 * j:4 * j + 4, :], bank(4 + j), ACT.Copy).then_inc(gd_p, 1)
                if s == "E":
                    act.wait_ge(l_hc, 1)
                    act.activation(XT[:, :], HT, ACT.Silu).then_inc(ln_xT, 1)
                    act.wait_ge(l_qkv_ps, 1)
                    qkvg = BK[:, 0:4, :]
                    act.activation(LGT[:, :, :, :].rearrange("p r b h -> p b r h"),
                                   qkvg[:, :, WE_R:WE_G].rearrange("p b (r h) -> p b r h", r=2), ACT.Copy).then_inc(l_qkv, 1)
                    act.activation(QK[:, :, 1, :], qkvg[:, :, 64:128], ACT.Copy).then_inc(l_qkv, 1)
                    act.activation(QK[:, :, 0, :], qkvg[:, :, 0:64], ACT.Silu).then_inc(l_qkv, 1)
                    act.activation(VV[:, :, :], qkvg[:, :, 128:256], ACT.Copy).then_inc(l_qkv, 1)
                    act.activation(GS[:, :, :], qkvg[:, :, WE_G:WE_O], ACT.Silu).then_inc(l_qkv, 1)
                    act.wait_ge(l_ld, 1)
                    act.activation(LGE[:, :, :, :], LGT[:, :, :, :], ACT.Exp).then_inc(l_le, 1)
                    act.wait_ge(l_oc, 1)
                    act.activation(OQ[:, :, :], OO[:, :, :], ACT.Square).then_inc(l_sq, 1)
                    act.wait_ge(l_vs, 1)
                    act.activation(SM2[:, :, :], SM1[:, :, :], ACT.Sqrt, bias=col("eps"), scale=1.0 / HD)\
                       .then_inc(l_std, 1)
                    ctx_T("E", 7)
                    act.wait_ge(ln_xT_ps, xT_count(LN_E2))
                    act.activation(XT[:, :], bank(5), ACT.Identity, scale=col("ln2_w"), bias=col("ln2_b")).then_inc(ln_xT, 1)
                    for j, (o, w) in enumerate(FFT):
                        act.wait_ge(l_ff_ps, 2 * j + 1)
                        act.activation(HF[0:w, j, :], BK[0:w, j, :], ACT.Silu).then_inc(l_ffs, 1)

        @block.vector
        def _(dve):
            chain = [0]

            def settle(ins):
                chain[0] += 1
                ins.then_inc(dve_chain, 1)
                dve.wait_ge(dve_chain, chain[0])

            def mark(ins):
                chain[0] += 1
                ins.then_inc(dve_chain, 1)
                return chain[0]

            def stats(n, src, ready=None):
                done = []
                for h in range(2):
                    if ready:
                        ready(h)
                    for b in (2 * h, 2 * h + 1):
                        ins = dve.bn_stats(STAT[:, b, :], src[:, b, :])
                    done.append(mark(ins))
                for h in range(2):
                    dve.wait_ge(dve_chain, done[h])
                    for b in (2 * h, 2 * h + 1):
                        ins = dve.bn_aggr(MV[:, b, :], STAT[:, b, :])
                    done.append(mark(ins))
                for h in range(2):
                    dve.wait_ge(dve_chain, done[2 + h])
                    pair = slice(2 * h, 2 * h + 2)
                    if n == LN_E:
                        ins = dve.tensor_scalar(VE[:, pair], MV[:, pair, 1], 1.0 + EPS, EPS * EPS, ALU.mult, ALU.add)
                    else:
                        ins = dve.tensor_scalar(VE[:, pair], MV[:, pair, 1], EPS, None, ALU.add)
                    ins.then_inc(ln_var, 1)
                if n == LN_E:
                    dve.tensor_scalar(VEX[:, :], MV[:, :, 1], EPS, None, ALU.add).then_inc(l_vex, 1)

            def norm(n, src, dst):
                for b in range(B):
                    if b % 2 == 0:
                        dve.wait_ge(ln_rstd, 2 * n + 1 + b // 2)
                    ins = dve.tensor_scalar(dst[:, b, :], src[:, b, :], MV[:, b, 0:1], RSTD[:, b:b + 1],
                                            ALU.subtract, ALU.mult)
                    ins.then_inc(ln_xhat, 1)
                dve.wait_ge(ln_xhat, xhat_count(n))

            def of_stage(s):
                return (lambda h: stages_done(dve, nx[s], h)) if nx[s] else None

            def mixing_weights():
                w, c0, c1 = (cols[:, COLS[n]:COLS[n] + 1] for n in ("ln1_w", "conv0", "conv1"))
                wb = cols[:, COLS["ln1_w"]:COLS["ln1_w"] + 2]
                dve.tensor_scalar(MIX[:, 0:2], wb, c1, None, ALU.mult)
                settle(dve.tensor_scalar(MIX[:, 2:4], wb, c0, None, ALU.mult))
                dve.tensor_tensor(MIX[:, 3:4], MIX[:, 3:4], MIX[:, 1:2], ALU.add)
                dve.wait_ge(loads["w_e"], 64)
                dve.wait_ge(loads["crows"], 32)
                rw = rows[:, ROWS["rw"]].rearrange("p (r n) -> p r n", r=2)
                settle(dve.tensor_tensor(HF[:, 0:2, 0:D], over(w_e[:, D:2 * D], 2), rw, ALU.mult))
                dve.tensor_reduce(w_e[:, WE_R:WE_G].rearrange("p (r h) -> p r h", r=2),
                                  HF[:, 0:2, 0:D].rearrange("p r (h d) -> p r h d", h=H), AX.X, ALU.add).then_inc(l_mix, 1)
                dve.wait_ge(l_mix, 1)

            def residual(s, other):
                for h in range(2):
                    pair = slice(2 * h, 2 * h + 2)
                    dve.wait_ge(proj_ps, 2 * PROJ.index(s) + 1 + h)
                    dve.tensor_tensor(X[:, pair, :], halves_of(7, 5)[h], other[:, pair, :], ALU.add).then_inc(x_ready, 1)

            def over(ap, n, axis=1):
                v = ap.unsqueeze(axis)
                shape = list(v.shape)
                shape[axis] = n
                return v.to_broadcast(shape)

            dve.wait_ge(loads["x"], 16)
            stats(LN_A, X)
            norm(LN_A, X, XH)
            def tail():
                dve.wait_ge(loads["flags"], 80)
                dve.tensor_reduce(GNA[:, 0:1], MKF[:, 0:S2 - P], AX.X, ALU.max, apply_absolute_value=True)
                settle(dve.tensor_reduce(GNA[:, 1:2], MKF[:, S2 - P:S2], AX.X, ALU.max, apply_absolute_value=True))
                dve.tensor_scalar(GNA[:, 0:1], GNA[:, 0:1], 0.0, None, ALU.not_equal)
                settle(dve.tensor_scalar(GNA[:, 1:2], GNA[:, 1:2], 0.0, None, ALU.is_equal))
                dve.tensor_tensor(FLD[:, 0:1], GNA[:, 0:1], GNA[:, 1:2], ALU.max).then_inc(flag_rows, 1)

            def tail_values():
                dve.wait_ge(kd_ps, 2)
                dve.wait_ge(loads["crows"], 32)
                dve.tensor_tensor(vd[:, :, :], bank(4).rearrange("p (b n) -> p b n", b=B), over(row("x_bv"), B),
                                  ALU.add).then_inc(vd_ready, 1)

            def tail_flag():
                dve.wait_ge(flag_all, 1)
                dve.tensor_copy(FDI[:, :], FLD[0:1, 1:2]).then_inc(flag_d, 1)

            def kv_windows(j):
                dve.wait_ge(kvw_ps, j + 1)
                dve.tensor_tensor(KVW[:, 2 * j:2 * j + 2, 0:2 * D], sbank(j).rearrange("p (a n) -> p a n", a=2),
                                  over(row("bkv"), 2), ALU.add).then_inc(kvw_ready, 1)

            for s in STAGES:
                if s == "A":
                    dve.wait_ge(loads["rows"], 16)
                    kv_windows(0)
                    dve.wait_ge(loads["pos"], 32)
                    settle(dve.tensor_tensor(ybias[:, :], boff[:, :], refc, ALU.add))

                    def positions(g):
                        dve.wait_ge(a_off_ps, g + 1)
                        return dve.scalar_tensor_tensor(
                            out=Y[:, g, :].rearrange("p (b q) -> p b q", b=B),
                            in0=BK[0:96, (5, 3, 6)[g], :].rearrange("p (b q) -> p b q", b=B), scalar=ybias[:, g:g + 1],
                            in1=loc.unsqueeze(1).to_broadcast([96, B, P]), op0=ALU.add, op1=ALU.add)

                    settle(positions(0))
                    settle(dve.tensor_scalar(YW[:, :], Y[:, 0, :], 0.0, -1.0, ALU.is_lt, ALU.mult))
                    settle(dve.scalar_tensor_tensor(out=IX[:, :], in0=Y[:, 0, :], scalar=float(S2) / (S2 - 1),
                                                    in1=YW[:, :], op0=ALU.mult, op1=ALU.add))
                    dve.wait_ge(loads["sel"], 32)
                    settle(dve.tensor_copy(R[0:96, 0, :], IX[:, :]))
                    settle(dve.tensor_tensor(IX[:, :], IX[:, :], R[0:96, 0, :], ALU.subtract))
                    settle(dve.tensor_copy(Rh[:, :], IX[:, :]))
                    settle(dve.tensor_tensor(YW[:, :], IX[:, :], Rh[:, :], ALU.subtract))
                    dve.tensor_copy(R[32:64, 0, :], Rh[32:64, :])
                    dve.tensor_copy(R[64:96, 0, :], YW[64:96, :]).then_inc(a_r, 1)
                    for j in range(1, 4):
                        kv_windows(j)
                    positions(1).then_inc(a_y, 1)
                    positions(2).then_inc(a_y, 1)
                    dve.wait_ge(a_q_ps, 2)
                    dve.tensor_tensor(Qq[:, :, :], bank(4).rearrange("p (b n) -> p b n", b=B), over(row("bq"), B),
                                      ALU.add).then_inc(a_qq, 1)

                    def reach(g):
                        if g == 0:
                            dve.wait_ge(a_r, 1)
                            settle(dve.tensor_tensor(YW[:, :].rearrange("p (b q) -> p b q", b=B),
                                                     Y[:, g, :].rearrange("p (b q) -> p b q", b=B),
                                                     mid.unsqueeze(1).to_broadcast([96, B, P]), ALU.subtract))
                        else:
                            dve.wait_ge(a_dev, g)
                        settle(dve.tensor_reduce(VM3[:, g:g + 1], (YW, YW2, IX2)[g], AX.X, ALU.max,
                                                 apply_absolute_value=True))

                    def uncovered():
                        settle(dve.tensor_reduce(FLA[:, 0:1], MKB[:, :, :], AX.XY, ALU.max, apply_absolute_value=True))
                        settle(dve.tensor_scalar(FLA[:, 0:1], FLA[:, 0:1], 0.0, None, ALU.not_equal))
                        settle(dve.tensor_reduce(GNA[0:96, 0:1], VM3[:, :], AX.X, ALU.max))
                        settle(dve.tensor_scalar(GNA[0:96, 0:1], GNA[0:96, 0:1], 62.5, None, ALU.is_gt))
                        dve.tensor_tensor(FLA[0:96, 0:1], FLA[0:96, 0:1], GNA[0:96, 0:1], ALU.max).then_inc(flag_rows, 1)

                    def evac(G, i):
                        n = 8 * G + i
                        dve.wait_ge(a_samp_ps, n + 1)
                        if G and i == 0:
                            dve.wait_ge(a_tr_ps, 4 * G)
                        dst, src = sampled(i, n)
                        dve.tensor_copy(dst, src).then_inc(a_sk_even, 1)

                    def score(u):
                        G, b = u // 4, u % 4
                        dve.wait_ge(a_tr_ps, u + 1)
                        src = transposed_unit(u)[:, :, :, 0:HD]
                        qv = Qq[:, b, 32 * G:32 * G + 32].rearrange("p (h d) -> p h d", h=4)
                        dve.wait_ge(a_sco, u) if u else dve.wait_ge(a_qq, 1)
                        dve.tensor_tensor(PRD[:, :, :, :], src, over(qv, NK), ALU.mult).then_inc(a_prod, 1)
                        dve.wait_ge(a_prod, u + 1)
                        dve.tensor_reduce(SCO[:, b, 4 * G:4 * G + 4, :], PRD[:, :, :, :].rearrange("p k h d -> p h k d"),
                                          AX.X, ALU.add).then_inc(a_sco, 1)

                    def soften(G, step):
                        z, m1, m2 = (v[:, :, 4 * G:4 * G + 4] for v in (SCO, SM1, SM2))
                        if step == 0:
                            dve.wait_ge(a_sco, 4 * G + 4)
                            dve.tensor_scalar(z, z, -0.5 / np.sqrt(HD), None, ALU.mult).then_inc(a_soft, 1)
                        if step == 1:
                            dve.wait_ge(a_soft, 6 * G + 1)
                            dve.tensor_reduce(m1, z, AX.X, ALU.max).then_inc(a_soft, 1)
                        if step == 2:
                            dve.wait_ge(a_soft, 6 * G + 2)
                            dve.tensor_tensor(z, z, over(m1, NK, 3), ALU.subtract).then_inc(a_z, 1)
                        if step == 3:
                            dve.wait_ge(a_exp, G + 1)
                            dve.tensor_reduce(m1, z, AX.X, ALU.add).then_inc(a_soft, 1)
                        if step == 4:
                            dve.wait_ge(a_soft, 6 * G + 3)
                            dve.reciprocal(m2, m1).then_inc(a_soft, 1)
                        if step == 5:
                            dve.wait_ge(a_soft, 6 * G + 4)
                            dve.tensor_tensor(z, z, over(m2, NK, 3), ALU.mult).then_inc(a_soft, 1)
                        if step == 6:
                            dve.wait_ge(a_soft, 6 * G + 5)
                            dve.wait_ge(a_vs, 4 * G + 4)
                            for b in range(B):
                                v = VS[:, b, 4 * G:4 * G + 4]
                                ins = dve.tensor_tensor(v, v, over(z[:, b], HD, 3), ALU.mult)
                            ins.then_inc(a_soft, 1)
                        if step == 7:
                            dve.wait_ge(a_soft, 6 * G + 6)
                            for b in range(B):
                                ins = dve.tensor_reduce(CT[:, b, 32 * G:32 * G + 32].rearrange("p (h d) -> p h d", h=4),
                                                        VS[:, b, 4 * G:4 * G + 4].rearrange("p h k d -> p h d k"),
                                                        AX.X, ALU.add)
                            ins.then_inc(a_ctx, 1)

                    for e in range(E1):
                        G = e // 20
                        dve.wait_ge(a_abs, e + 1)
                        w = WT[:, G % 2, e % 20 // NK, :, e % NK, :]
                        dve.tensor_scalar(w, w, 1.0, -1.0, ALU.min, ALU.add).then_inc(a_w, 1)
                        if e == 2:
                            reach(0)
                        if e == TAIL_AT:
                            tail_values()
                        if e == FLAG_AT:
                            tail()
                        if e in (53, 56):
                            reach((0, 53, 56).index(e))
                        if e == 59:
                            tail_flag()
                            uncovered()
                        if e == 65:
                            dve.wait_ge(flag_all, 2)
                            dve.tensor_copy(FAI[:, :], FLA[0:1, 1:2]).then_inc(flag_a, 1)
                        if G and e % 20 + 1 - SAMPLE_AT in (0, 2, 4, 6):
                            evac(G - 1, e % 20 + 1 - SAMPLE_AT)
                        if G and e % 20 + 2 in BACK_AT:
                            score(4 * (G - 1) + BACK_AT.index(e % 20 + 2))
                        if G and e % 20 in (17, 18, 19):
                            soften(G - 1, e % 20 - 17)
                        if G >= 2 and 3 <= e % 20 - EXP_AT + 2 <= 7:
                            soften(G - 2, e % 20 - EXP_AT + 2)
                    evac(3, 0)
                    soften(2, 3)
                    evac(3, 2)
                    soften(2, 4)
                    score(12)
                    evac(3, 4)
                    score(13)
                    evac(3, 6)
                    soften(2, 5)
                    score(14)
                    soften(2, 6)
                    score(15)
                    soften(2, 7)
                    for step in range(8):
                        soften(3, step)
                    with dve.If(flagged(dve, flag_a, FAI)):
                        dve.sem_inc(ga_kv, 1)
                        dve.sem_inc(ga_add, 1)
                        dve.sem_inc(ga_prod, 1)
                        dve.sem_inc(ga_out, 1)
                        chain_a = [0]

                        def settle_a(ins):
                            chain_a[0] += 1
                            ins.then_inc(ga_chain, 1)
                            dve.wait_ge(ga_chain, chain_a[0])

                        cnt, L, rL = GSM[:, 0, :], GSM[0:96, 1, :], GSM[0:96, 2, :]
                        by_b = lambda v: v.unsqueeze(2).to_broadcast([96, B, P])
                        gv = lambda a, g: a[:, g, :].rearrange("p (b q) -> p b q", b=B)
                        settle_a(dve.tensor_reduce(cnt, MKB[:, :, :], AX.X, ALU.add))
                        dve.tensor_copy(GSM[:, 3, :], cnt).then_inc(ga_zero, 1)
                        dve.wait_ge(ga_sum_ps, 1)
                        settle_a(dve.tensor_scalar(L, BK[0:96, 0, 0:B], -1.0, float(S2 - 1), ALU.mult, ALU.add))
                        settle_a(dve.reciprocal(rL, L))
                        for g in range(3):
                            gx, gt = gv(GIX, g), gv(GT1, g)
                            settle_a(dve.tensor_tensor(gt, gv(Y, g), by_b(rL), ALU.mult))
                            settle_a(dve.tensor_scalar(gt, gt, 12582912.0, None, ALU.add))
                            settle_a(dve.tensor_scalar(gt, gt, -12582912.0, None, ALU.add))
                            settle_a(dve.tensor_tensor(gt, gt, by_b(L), ALU.mult))
                            settle_a(dve.tensor_tensor(gx, gv(Y, g), gt, ALU.subtract))
                            settle_a(dve.tensor_tensor(gt, gx, by_b(L), ALU.mult))
                            settle_a(dve.tensor_scalar(gt, gt, 0.0, None, ALU.is_lt))
                            settle_a(dve.tensor_tensor(gt, gt, by_b(L), ALU.mult))
                            settle_a(dve.tensor_tensor(gx, gx, gt, ALU.add))
                            settle_a(dve.tensor_scalar(gx, gx, float(S2) / (S2 - 1), -0.5, ALU.mult, ALU.add))
                        dve.memset(GKV[:, 2 * D:2 * D + 16], 0.0).then_inc(ga_pos, 1)
                        with dve.Fori(0, B) as b:
                            dve.wait_ge(ga_prod, 1 + b * 4)
                            dve.memset(GSK, 0.0).then_inc(ga_zero, 1)
                            with dve.Fori(0, S2 // P) as c:
                                it = b * (S2 // P) + c
                                dve.wait_ge(ga_zero, b + 2)
                                dve.wait_ge(ga_samp, 1 + it * 4)
                                dve.wait_ge(ga_kv_ps, 1 + it + 1)
                                dve.tensor_tensor(GKV[:, 0:2 * D], BK[:, 7, 0:2 * D], row("bkv"), ALU.add).then_inc(ga_kv, 1)
                                dve.tensor_copy(GPOS, pos[:, bass.ds(c, 1)]).then_inc(ga_kv, 1)
                                for e in range(E1):
                                    dve.wait_ge(ga_abs, 1 + it * E1 + e + 1)
                                    w = GW[:, e % 20 // NK, e % NK, :]
                                    dve.tensor_scalar(w, w, 1.0, -1.0, ALU.min, ALU.add).then_inc(ga_w, 1)
                                    if e % 20 == 19:
                                        G = e // 20
                                        dve.wait_ge(ga_samp, 1 + it * 4 + G + 1)
                                        dve.wait_ge(ga_add, 1 + it * 4 + G)
                                        dve.tensor_tensor(GSK[:, G, :], GSK[:, G, :], BK[:, 3:5, :].rearrange("p a n -> p (a n)")[:, 0:NK * P],
                                                          ALU.add).then_inc(ga_add, 1)
                            for G in range(4):
                                dve.wait_ge(ga_tr, b * 4 + G + 1)
                                src = BK[:, 5:7, :].rearrange("p a n -> p (a n)")[:, 0:NK * P]
                                src = src.rearrange("p (k h r) -> p k h r", k=NK, h=4)
                                qv = Qq[:, bass.ds(b, 1), 32 * G:32 * G + 32].rearrange("p b (h d) -> p (b h) d", h=4)
                                dve.wait_ge(ga_out, 1 + b * 4 + G)
                                dve.tensor_tensor(PRD[:, :, :, :], src[:, :, :, 0:HD], over(qv, NK), ALU.mult)\
                                   .then_inc(ga_prod, 1)
                                for k in range(NK):
                                    dve.tensor_copy(VS[:, bass.ds(b, 1), 4 * G:4 * G + 4, k, :].rearrange("p b h d -> p (b h) d"),
                                                    src[:, k, :, HD:2 * HD])
                                dve.wait_ge(ga_prod, 1 + b * 4 + G + 1)
                                dve.tensor_reduce(SCO[:, bass.ds(b, 1), 4 * G:4 * G + 4, :].rearrange("p b h k -> p (b h) k"),
                                                  PRD[:, :, :, :].rearrange("p k h d -> p h k d"), AX.X, ALU.add)\
                                   .then_inc(ga_out, 1)
                        dve.wait_ge(ga_out, 1 + 4 * B)
                        z = SCO[:, :, :, :].rearrange("p b h k -> p (b h) k")
                        m1 = SM1[:, :, :].rearrange("p b h -> p (b h)")
                        m2 = SM2[:, :, :].rearrange("p b h -> p (b h)")
                        settle_a(dve.tensor_scalar(z, z, -0.5 / np.sqrt(HD), None, ALU.mult))
                        settle_a(dve.tensor_reduce(m1, z, AX.X, ALU.max))
                        dve.tensor_tensor(z, z, over(m1, NK, 2), ALU.subtract).then_inc(ga_z, 1)
                        dve.wait_ge(ga_exp, 1)
                        settle_a(dve.tensor_reduce(m1, z, AX.X, ALU.add))
                        settle_a(dve.reciprocal(m2, m1))
                        settle_a(dve.tensor_tensor(z, z, over(m2, NK, 2), ALU.mult))
                        vs = VS.rearrange("p b h k d -> p (b h) k d")
                        settle_a(dve.tensor_tensor(vs, vs, over(z, HD, 3), ALU.mult))
                        dve.tensor_reduce(CT[:, :, :].rearrange("p b (h d) -> p (b h) d", h=H),
                                          vs.rearrange("p n k d -> p n d k"), AX.X, ALU.add).then_inc(ga_ctx, 1)
                    dve.wait_ge(xb_ready, 1)
                    residual("A", XB)
                if s == "B":
                    stats(LN_B, X, of_stage(s))
                    norm(LN_B, X, XH)
                    dve.wait_ge(loads["decay"], 64)
                    for j, dst in ((0, qT), (2, kT)):
                        dve.wait_ge(b_qk_ps, j + 1)
                        dve.tensor_tensor(T0[:, :, :], bank(j), over(rope0[:, j, :], B), ALU.mult)
                        dve.wait_ge(b_qk_ps, j + 2)
                        settle(dve.tensor_tensor(T1[:, :, :], bank(j + 1), over(rope0[:, j + 1, :], B), ALU.mult))
                        dve.tensor_tensor(dst[:, :, :], T0[:, :, :], T1[:, :, :], ALU.add)\
                           .then_inc(b_rot, 1)
                        dve.wait_ge(b_rot, 2 if j else 1)

                    def extract(b):
                        dve.wait_ge(b_o_ps, b + 1)
                        settle(dve.tensor_tensor(OM, bank(4 + b % 2).rearrange("p (h t) -> p h t", h=4),
                                                 over(head[:, :], P, 2), ALU.mult))
                        dve.tensor_reduce(CT[:, b, :], OM.rearrange("p h t -> p t h"), AX.X, ALU.add)\
                           .then_inc(b_oT, 1)
                        dve.wait_ge(b_oT, b + 1)

                    for b in range(B):
                        for g in range(4):
                            dve.wait_ge(b_s_ps, 4 * b + g + 1)
                            if b >= 2 and g == 0:
                                dve.wait_ge(b_o_ps, b - 1)
                            dve.tensor_tensor(PT[:, b % 2, 4 * g:4 * g + 4, :], bank(g).rearrange("p (h t) -> p h t", h=4),
                                              decay[:, 4 * g:4 * g + 4, :], ALU.mult).then_inc(b_pt, 1)
                        if b:
                            extract(b - 1)
                    extract(B - 1)
                    dve.wait_ge(b_oc_ps, 1)
                    dve.wait_ge(b_std, 1)
                    settle(dve.reciprocal(T1[:, :, :], T1[:, :, :]))
                    settle(dve.tensor_tensor(T1[:, :, :], bank(4), T1[:, :, :], ALU.mult))
                    dve.tensor_scalar(CTT[:, :], T1[:, :, :].rearrange("p b t -> p (b t)"), col("gn_w"), col("gn_b"),
                                      ALU.mult, ALU.add).then_inc(b_on, 1)
                    residual("B", X)
                if s in "CF":
                    k = FFNS.index(s)
                    ln = LN_C if s == "C" else LN_F
                    stats(ln, X, of_stage(s))
                    norm(ln, X, XH)
                    dve.wait_ge(r_lg_ps, k + 1)
                    lg = BK[:, 4, 0:B * NE].rearrange("p (b e) -> p b e", b=B)
                    settle(dve.tensor_reduce(S1[:, :], lg, AX.X, ALU.max))
                    dve.tensor_tensor(EX[:, :, :], lg, over(S1[:, :], NE, 2), ALU.subtract).then_inc(r_z, 1)
                    dve.wait_ge(r_exp, k + 1)
                    settle(dve.tensor_reduce(S1[:, :], EX[:, :, :], AX.X, ALU.add))
                    settle(dve.reciprocal(S1[:, :], S1[:, :]))
                    settle(dve.tensor_tensor(PR[:, :, :], EX[:, :, :], over(S1[:, :], NE, 2), ALU.mult))
                    other, own = over(PR[:, :, :], NE, 2), over(PR[:, :, :], NE, 3)
                    dve.tensor_tensor(CMP[:, :, :, :], other, own, ALU.is_gt)
                    settle(dve.tensor_tensor(CMQ[:, :, :, :], other, own, ALU.is_equal))
                    if not k:
                        dve.wait_ge(loads["crows"], 32)
                    before = crows[:, BEFORE].rearrange("p (e f) -> p e f", e=NE)
                    settle(dve.tensor_tensor(CMQ[:, :, :, :], CMQ[:, :, :, :], over(before, B), ALU.mult))
                    settle(dve.tensor_tensor(CMP[:, :, :, :], CMP[:, :, :, :], CMQ[:, :, :, :], ALU.add))
                    settle(dve.tensor_reduce(RK[:, :, :], CMP[:, :, :, :], AX.X, ALU.add))
                    settle(dve.scalar_tensor_tensor(out=PR[:, :, :], in0=RK[:, :, :], scalar=1.5, in1=PR[:, :, :],
                                                    op0=ALU.is_lt, op1=ALU.mult))
                    settle(dve.tensor_reduce(S1[:, :], PR[:, :, :], AX.X, ALU.add))
                    if s == "C":
                        settle(dve.tensor_scalar(S1[:, :], S1[:, :], 1e-9, None, ALU.add))
                    settle(dve.reciprocal(S1[:, :], S1[:, :]))
                    dve.tensor_tensor(CW[:, :, :], PR[:, :, :], over(S1[:, :], NE, 2), ALU.mult).then_inc(r_cw, 1)
                    if s == "C":
                        dve.wait_ge(r_cw, 1)
                        settle(dve.tensor_reduce(S1[:, :], CW[:, :, :], AX.X, ALU.add))
                        for b in range(B):
                            ins = dve.scalar_tensor_tensor(out=X[:, b, :], in0=row("ff_bo"), scalar=S1[:, b:b + 1],
                                                           in1=X[:, b, :], op0=ALU.mult, op1=ALU.add)
                        settle(ins)

                    def weigh(e):
                        n = k * NE + e
                        dve.wait_ge(e_y_ps, n + 1)
                        if n:
                            dve.wait_ge(e_sum, 2 * n)
                        for b in range(B):
                            ins = dve.scalar_tensor_tensor(out=X[:, b, :], in0=BK[:, 4 + e % 2, b * P:(b + 1) * P],
                                                           scalar=CW[:, b, e:e + 1], in1=X[:, b, :],
                                                           op0=ALU.mult, op1=ALU.add)
                            if b % 2:
                                ins.then_inc(e_sum, 1)

                    dve.wait_ge(r_cw, k + 1)
                    for e in range(NE):
                        n = k * NE + e
                        if s == "C":
                            if e >= 2:
                                dve.wait_ge(e_y_ps, n - 1)
                            for p in (2 * e, 2 * e + 1):
                                dve.wait_ge(e_act, p + 1)
                                ba = cols[:, B1COL + 4 * e + p % 2:B1COL + 4 * e + 1 + p % 2]
                                dve.scalar_tensor_tensor(out=GT[:, e % 2, p % 2, :], in0=hbank(2 * p), scalar=ba,
                                                         in1=SG[:, e % 2, p % 2, :], op0=ALU.add, op1=ALU.mult)\
                                   .then_inc(e_g, 1)
                        if e:
                            weigh(e - 1)
                        if s == "C" and e == 3:
                            mixing_weights()
                    weigh(NE - 1)
                if s == "D":
                    stats(LN_D, X, of_stage(s))
                    norm(LN_D, X, XH)
                    settle(dve.tensor_scalar(MB[:, :], mtail[:, :], 0, -KEPT, ALU.not_equal, ALU.mult))
                    settle(dve.tensor_scalar(MB[:, :], MB[:, :], -NEG, None, ALU.add))

                    def extract(b):
                        dve.wait_ge(d_o_ps, b + 1)
                        dve.tensor_tensor(OM, bank(6).rearrange("p (h t) -> p h t", h=4),
                                          over(head[:, :], P, 2), ALU.mult)
                        settle(dve.tensor_tensor(DN, bank(7).rearrange("p (h t) -> p h t", h=4),
                                                 over(head[:, :], P, 2), ALU.mult))
                        dve.tensor_reduce(T0[:, b, :], OM.rearrange("p h t -> p t h"), AX.X, ALU.add)
                        settle(dve.tensor_reduce(T1[:, b, :], DN.rearrange("p h t -> p t h"), AX.X, ALU.add))
                        settle(dve.reciprocal(T1[:, b, :], T1[:, b, :]))
                        dve.tensor_tensor(CTT[:, b * P:(b + 1) * P], T0[:, b, :], T1[:, b, :], ALU.mult)\
                           .then_inc(d_om, 1)
                        dve.wait_ge(d_om, b + 1)

                    def least(n):
                        b, g = n // 4, n % 4
                        dve.wait_ge(d_ss, n + 1)
                        dve.tensor_reduce(MX[:, b, 4 * g:4 * g + 4], SS[:, b % 2, 4 * g:4 * g + 4, :], AX.X, ALU.min)\
                           .then_inc(d_mx, 1)

                    for b in range(B):
                        for g in range(4):
                            dve.wait_ge(d_s_ps, 4 * b + g + 1)
                            if b >= 2:
                                dve.wait_ge(d_pT_ps, 4 * (b - 2) + g + 1)
                            ins = dve.scalar_tensor_tensor(
                                out=SS[:, b % 2, 4 * g:4 * g + 4, :], in0=bank(g).rearrange("p (h t) -> p h t", h=4),
                                scalar=float(-1.0 / np.sqrt(HD)), in1=over(MB[:, :], 4), op0=ALU.mult, op1=ALU.max)
                            ins.then_inc(d_ss, 1)
                            if g:
                                least(4 * b + g - 1)
                        least(4 * b + 3)
                        if b:
                            extract(b - 1)
                    extract(B - 1)
                    with dve.If(flagged(dve, flag_d, FDI)):
                        dve.sem_inc(gd_v, 1)
                        dve.sem_inc(gd_oT, 1)
                        dve.sem_inc(gd_o, 1)
                        dve.wait_ge(gd_mask, 16)
                        dve.tensor_scalar(GM, GMI, 0, KEPT, ALU.not_equal, ALU.mult).then_inc(gd_m0, 1)
                        dve.wait_ge(gd_m0, 1)
                        dve.tensor_scalar(GM, GM, NEG, None, ALU.add).then_inc(gd_m0, 1)
                        dve.wait_ge(gd_m0, 2)
                        with dve.Fori(0, B) as b:
                            with dve.Fori(0, S2 // P) as c:
                                it = b * (S2 // P) + c
                                dve.wait_ge(gd_kv_ps, 1 + it + 1)
                                dve.tensor_tensor(GV[:, bass.ds(c, 1), :].rearrange("p c n -> p (c n)"), BK[:, 1, 0:P],
                                                  row("x_bv"), ALU.add).then_inc(gd_v, 1)
                            with dve.Fori(0, H) as h:
                                it = b * H + h
                                dve.wait_ge(gd_s_ps, 1 + it)
                                dve.tensor_scalar(GQ, qT[:, bass.ds(b, 1), :].rearrange("p b n -> p (b n)"),
                                                  head16[:, bass.ds(h, 1)], None, ALU.mult).then_inc(gd_q, 1)
                                dve.wait_ge(gd_s_ps, 1 + it + 1)
                                dve.scalar_tensor_tensor(out=GSC, in0=BK[:, 0:4, :].rearrange("p a n -> p (a n)"),
                                                         scalar=float(1.0 / np.sqrt(HD)), in1=GM, op0=ALU.mult,
                                                         op1=ALU.min).then_inc(gd_chain, 1)
                                dve.wait_ge(gd_chain, 3 * it + 1)
                                dve.tensor_reduce(GR[:, 2:3], GSC, AX.X, ALU.max).then_inc(gd_chain, 1)
                                dve.wait_ge(gd_chain, 3 * it + 2)
                                dve.tensor_scalar(GR[:, 0:1], GR[:, 2:3], -1.0, None, ALU.mult).then_inc(gd_neg, 1)
                                dve.wait_ge(gd_o_ps, it + 1)
                                dve.reciprocal(GR[:, 3:4], GR[:, 1:2]).then_inc(gd_chain, 1)
                                dve.wait_ge(gd_chain, 3 * it + 3)
                                dve.tensor_scalar(GO[:, bass.ds(h * HD, HD)], BK[:, 0, bass.ds(h * HD, HD)], GR[:, 3:4],
                                                  None, ALU.mult).then_inc(gd_o, 1)
                            dve.wait_ge(gd_oT_ps, b + 1)
                            dve.tensor_copy(CTT[:, bass.ds(b * P, P)], BK[:, 1, 0:P]).then_inc(gd_oT, 1)
                        dve.wait_ge(gd_oT, 1 + B)
                    dve.wait_ge(xb_ready, BIASED.index("D") + 1)
                    residual("D", XB)
                if s == "E":
                    stats(LN_E, X, of_stage(s))
                    norm(LN_E, X, XH)
                    dve.wait_ge(ln_xT_ps, xT_count(LN_E))
                    dve.tensor_scalar(HT[:, 0:P], BK[:, 7, 0:P], MIX[:, 0:1], MIX[:, 1:2], ALU.mult, ALU.add)
                    settle(dve.tensor_scalar(HT[:, P:TOK], BK[:, 7, P:TOK], MIX[:, 0:1], MIX[:, 3:4], ALU.mult, ALU.add))
                    dve.scalar_tensor_tensor(out=HT[:, P:TOK], in0=BK[:, 7, 0:TOK - P], scalar=MIX[:, 2:3],
                                             in1=HT[:, P:TOK], op0=ALU.mult, op1=ALU.add).then_inc(l_hc, 1)
                    dve.wait_ge(l_rstdx, 1)
                    for b in range(B):
                        ins = dve.tensor_scalar(XN[:, b, :], X[:, b, :], MV[:, b, 0:1], RSTDX[:, b:b + 1],
                                                ALU.subtract, ALU.mult)
                    settle(ins)
                    dve.wait_ge(l_qkv, 1)
                    dve.tensor_tensor(OH[:, :, :], LGT[:, 0], LGT[:, 1], ALU.is_ge)
                    settle(dve.tensor_tensor(SM1[:, :, :], LGT[:, 0], LGT[:, 1], ALU.max))
                    dve.tensor_tensor(LGT[:, :, :, :], LGT[:, :, :, :], over(SM1[:, :, :], 2), ALU.subtract)\
                       .then_inc(l_ld, 1)
                    for l in range(B):
                        pairs = SMM[:, PAIR[l]:PAIR[l] + l + 1, :]
                        ins = dve.tensor_tensor(pairs, over(OH[:, l, :], l + 1), OH[:, 0:l + 1, :], ALU.is_equal)
                    settle(ins)
                    dve.tensor_copy(NS[:, 0, :], SMM[:, 0, :])
                    for l in range(1, B):
                        pairs = SMM[:, PAIR[l]:PAIR[l] + l + 1, :]
                        ins = dve.tensor_reduce(NS[:, l, :], pairs.rearrange("p m h -> p h m"), AX.X, ALU.add)
                    settle(ins)
                    dve.wait_ge(l_le, 1)
                    settle(dve.tensor_tensor(SM1[:, :, :], LGE[:, 0], LGE[:, 1], ALU.add))
                    settle(dve.tensor_tensor(SM1[:, :, :], SM1[:, :, :], NS[:, :, :], ALU.mult))
                    settle(dve.reciprocal(SM2[:, :, :], SM1[:, :, :]))
                    for l in range(B):
                        pairs = SMM[:, PAIR[l]:PAIR[l] + l + 1, :]
                        ins = dve.tensor_tensor(pairs, pairs, over(SM2[:, l, :], l + 1), ALU.mult)
                    settle(ins)
                    dve.wait_ge(l_rot, 1)
                    for l in range(B):
                        ins = dve.tensor_tensor(PDT[:, PAIR[l]:PAIR[l] + l + 1, :], over(QR[:, l, 0, :], l + 1),
                                                QR[:, 0:l + 1, 1, :], ALU.mult)
                    settle(ins)
                    settle(dve.tensor_reduce(DT[:, :, :].rearrange("p i h -> p (i h)"),
                                             PDT[:, :, :].rearrange("p i (h d) -> p (i h) d", h=H), AX.X, ALU.add))
                    settle(dve.tensor_tensor(DT[:, :, :], DT[:, :, :], SMM[:, :, :], ALU.mult))
                    dve.wait_ge(l_qkv, 4)
                    for l in range(B):
                        pairs = slice(PAIR[l], PAIR[l] + l + 1)
                        ins = dve.tensor_tensor(PO[:, pairs].rearrange("p m (h d) -> p (m h) d", h=H),
                                                over(DT[:, pairs, :].rearrange("p m h -> p (m h)"), HD, 2),
                                                VV[:, 0:l + 1, :].rearrange("p m (h d) -> p (m h) d", h=H), ALU.mult)
                    settle(ins)
                    dve.tensor_copy(OO[:, 0, :], PO[:, 0, :])
                    for l in range(1, B):
                        ins = dve.tensor_reduce(OO[:, l, :], PO[:, PAIR[l]:PAIR[l] + l + 1, :].rearrange("p m n -> p n m"),
                                                AX.X, ALU.add)
                    settle(ins)
                    hv = lambda a: a[:, :, :].rearrange("p b (h d) -> p (b h) d", h=H)
                    m1 = SM1[:, :, :].rearrange("p b h -> p (b h)")
                    m2 = SM2[:, :, :].rearrange("p b h -> p (b h)")
                    settle(dve.tensor_reduce(m1, hv(OO), AX.X, ALU.add))
                    settle(dve.tensor_scalar(m2, m1, 1.0 / HD, None, ALU.mult))
                    dve.tensor_tensor(hv(OO), hv(OO), over(m2, HD, 2), ALU.subtract).then_inc(l_oc, 1)
                    dve.wait_ge(l_sq, 1)
                    dve.tensor_reduce(m1, hv(OQ), AX.X, ALU.add).then_inc(l_vs, 1)
                    dve.wait_ge(l_qkv, 5)
                    settle(dve.tensor_tensor(OO[:, :, :], OO[:, :, :], GS[:, :, :], ALU.mult))
                    dve.wait_ge(l_std, 1)
                    settle(dve.reciprocal(m1, m2))
                    dve.tensor_tensor(hv(CT), hv(OO), over(m1, HD, 2), ALU.mult).then_inc(ctx_ready, 1)
                    for h in range(2):
                        pair = slice(2 * h, 2 * h + 2)
                        dve.wait_ge(proj_ps, 2 * PROJ.index("E") + 1 + h)
                        dve.tensor_tensor(CT[:, pair, :], halves_of(6, 7)[h], XN[:, pair, :], ALU.add).then_inc(l_xa, 1)
                    stats(LN_E2, CT, lambda h: dve.wait_ge(l_xa, 1 + h))
                    norm(LN_E2, CT, XH)
                    for j, (o, w) in enumerate(FFT):
                        dve.wait_ge(l_ffs, j + 1)
                        dve.wait_ge(l_ff_ps, 2 * j + 2)
                        dve.tensor_tensor(HF[0:w, j, :], BK[0:w, (3, 4, 6)[j], :], HF[0:w, j, :], ALU.mult).then_inc(l_ff, 1)
                    dve.wait_ge(xb_ready, BIASED.index("E") + 1)
                    for h in range(2):
                        pair = slice(2 * h, 2 * h + 2)
                        dve.wait_ge(proj_ps, 2 * PROJ.index("E") + 3 + h)
                        dve.tensor_tensor(X[:, pair, :], halves_of(7, 5)[h], XB[:, pair, :], ALU.add).then_inc(x_ready, 1)

        @block.tensor
        def _(pe):
            def norm_T(n, bk, src=XH):
                for b in range(B):
                    pe.wait_ge(ln_xhat, xhat_count(n) - 3 + b)
                    ins = pe.transpose(BK[:, bk, b * P:(b + 1) * P], src[:, b, :], ident[:, :])
                ins.then_inc(ln_xT_ps, 1)

            def transposes(src, bk, s):
                for b in range(B):
                    ins = pe.transpose(BK[:, bk, b * P:(b + 1) * P], src[:, b, :], ident[:, :])
                ins.then_inc(s, 1)

            def stay_warm(bk, n=WARM):
                for _ in range(n):
                    pe.matmul(BK[:, bk, 0:P], ident[:, :], ident[:, :], start=True, stop=True)

            def project(w, banks=(7, 5)):
                for b in range(B):
                    ins = pe.matmul(BK[:, banks[b // 2], b * P:(b + 1) * P], CTT[:, b * P:(b + 1) * P], w, start=True, stop=True)
                    if b % 2:
                        ins.then_inc(proj_ps, 1)

            pe.wait_ge(loads["ident"], 16)
            norm_T(LN_A, 5)
            def tail():
                pe.wait_ge(loads["w_d"], 16)
                pe.wait_ge(loads["tail"], 16)
                pe.matmul(bank(3), w_d[:, 0:D], TAIL.rearrange("p b n -> p (b n)"), start=True, stop=True)\
                  .then_inc(kd_ps, 1)
                for b in range(B):
                    ins = pe.matmul(BK[:, 4, b * P:(b + 1) * P], TAIL[:, b, :], w_d[:, D:2 * D], start=True, stop=True)
                ins.then_inc(kd_ps, 1)


            for s in STAGES:
                if s == "A":
                    wq, woff, wo = w_a[:, 256:384], w_a[:, 384:672].rearrange("p (g n) -> p g n", g=3), w_a[:, 672:800]

                    def kv_windows(j):
                        for hf in range(2):
                            ins = pe.matmul(sbank(j)[:, 2 * D * hf:2 * D * hf + 2 * D], WIN[:, j, QH * hf:QH * hf + P],
                                            w_a[:, 0:2 * D], start=True, stop=True)
                        ins.then_inc(kvw_ps, 1)

                    pe.wait_ge(loads["w_a"], 16)
                    pe.wait_ge(ln_xT, xT_count(LN_A))
                    pe.matmul(bank(6), wq, XT[:, :], start=True, stop=True).then_inc(a_q_ps, 1)
                    pe.wait_ge(loads["win"], 32)
                    kv_windows(0)
                    pe.wait_ge(a_qT, 1)
                    for g in range(3):
                        pe.matmul(BK[0:96, (5, 3, 6)[g], :], woff[:, g, :], QpT[:, :], start=True, stop=True)\
                          .then_inc(a_off_ps, 1)
                    for b in range(1, B):
                        kv_windows(b)
                    for b in range(B):
                        ins = pe.matmul(BK[:, 4, b * P:(b + 1) * P], XT[:, b * P:(b + 1) * P], wq, start=True, stop=True)
                    ins.then_inc(a_q_ps, 1)

                    def spread(e):
                        if e < 4:
                            pe.wait_ge(kvw_ready, e + 1)
                        else:
                            pe.wait_ge(a_abs, e - 3)
                        if e % 32 == 0:
                            pe.wait_ge(a_r, e // 32 + 1)
                        pe.matmul(sbank(e), SEL[:, e % 32, :], R[:, e // 32, :], start=True, stop=True)\
                          .then_inc(a_ix_ps, 1)

                    def sample(G, i):
                        if i == 0:
                            pe.wait_ge(a_w, 20 * G + 20)
                        if G == 0 and i == 0:
                            pe.wait_ge(kd_ready, 1)
                            pe.wait_ge(vd_ready, 1)
                        n = 8 * G + i
                        if n >= 2:
                            pe.wait_ge(a_sk_odd if i % 2 else a_sk_even, n // 2 - 1 if n >= SPARE_FROM else n // 2)
                        if n == SPARE_FROM:
                            pe.wait_ge(a_abs, E1)
                        for h in range(4):
                            c = 16 * (4 * G + h)
                            ins = pe.matmul(BK[32 * h:32 * h + 32, sample_bank(n), 0:NK * QH], KVW[:, i, c:c + 32],
                                            WT[:, G % 2, h, i, :, :].rearrange("p k q -> p (k q)"),
                                            start=True, stop=True)
                        ins.then_inc(a_samp_ps, 1)

                    def back(G, b):
                        u = 4 * G + b
                        pe.wait_ge(a_sk_even, 4 * G + b + 1)
                        pe.wait_ge(a_sk_odd, 4 * G + b + 1)
                        done = u if u < 13 else (0, 13, 14)[u - 13]
                        if done:
                            pe.wait_ge(a_vs, done)
                            pe.wait_ge(a_prod, done)
                        for k in range(NK):
                            ins = pe.transpose(BK[:, back_banks(u) + k // 4, k % 4 * P:k % 4 * P + P], SK[:, b, k, :],
                                               ident[:, :])
                        ins.then_inc(a_tr_ps, 1)

                    for i in range(20):
                        spread(i)
                        if i == TAIL_AT - 3:
                            pe.wait_ge(a_y, 1)
                            pe.wait_ge(a_qq, 1)
                            tail()
                    for G in range(1, 4):
                        for i in range(20):
                            spread(20 * G + i)
                            if 0 <= i - SAMPLE_AT < 8:
                                sample(G - 1, i - SAMPLE_AT)
                            if i in BACK_AT:
                                back(G - 1, BACK_AT.index(i))
                    for i in range(8):
                        sample(3, i)
                        if i in (3, 5, 7):
                            back(3, (i - 3) // 2)
                    back(3, 3)
                    pe.wait_ge(a_ctx, 4)
                    with pe.If(flagged(pe, flag_a, FAI)):
                        pe.sem_inc(ga_kv_ps, 1)
                        pe.sem_inc(ga_samp, 1)
                        pe.wait_ge(ga_zero, 1)
                        pe.matmul(BK[0:96, 0, 0:B], ones[:, 0:96], GSM[:, 3, :], start=True, stop=True).then_inc(ga_sum_ps, 1)
                        pe.wait_ge(ga_pos, 1)
                        with pe.Fori(0, B) as b:
                            with pe.Fori(0, S2 // P) as c:
                                it = b * (S2 // P) + c
                                pe.wait_ge(ga_in, it * 16 + 16)
                                pe.wait_ge(ga_kv, 1 + 2 * it)
                                pe.matmul(BK[:, 7, 0:2 * D], GCH, w_a[:, 0:2 * D], start=True, stop=True)\
                                  .then_inc(ga_kv_ps, 1)
                                for e in range(E1):
                                    g, i, G = e // 32, e % 32, e // 20
                                    pe.wait_ge(ga_abs, 1 + it * E1 + e)
                                    pe.matmul(BK[:, 0, 0:P], ident[0:96, i:i + 1].to_broadcast([96, P]),
                                              GIX[:, g, bass.ds(b * P, P)], start=True, stop=True).then_inc(ga_ix, 1)
                                    if e % 20 == 19:
                                        pe.wait_ge(ga_kv, 1 + 2 * it + 1)
                                        pe.wait_ge(ga_w, it * E1 + e + 1)
                                        pe.wait_ge(ga_add, 1 + it * 4 + G)
                                        for h in range(4):
                                            for k in range(NK):
                                                o = 16 * (4 * G + h)
                                                ins = pe.matmul(BK[32 * h:32 * h + 32, 3 + k // 4, k % 4 * P:k % 4 * P + P],
                                                                GKV[:, o:o + 32], GW[:, h, k, :], start=True, stop=True)
                                        ins.then_inc(ga_samp, 1)
                            for G in range(4):
                                pe.wait_ge(ga_add, 1 + b * (4 * S2 // P) + 4 * (S2 // P))
                                pe.wait_ge(ga_out, 1 + b * 4 + G)
                                for k in range(NK):
                                    ins = pe.transpose(BK[:, 5 + k // 4, k % 4 * P:k % 4 * P + P],
                                                       GSK[:, G, k * P:(k + 1) * P], ident[:, :])
                                ins.then_inc(ga_tr, 1)
                        pe.wait_ge(ga_ctx, 1)
                    transposes(CT, 6, ctxT_ps)
                    pe.wait_ge(ctxT_ready, 1)
                    pe.wait_ge(vd_ready, 1)
                    project(wo)
                if s == "B":
                    stay_warm(3)
                    norm_T(LN_B, 7)
                    pe.wait_ge(ln_xT, xT_count(LN_B))
                    pe.wait_ge(loads["w_b"], 16)
                    for j in range(4):
                        pe.matmul(bank(j), w_b[:, j * D:(j + 1) * D], XT[:, :], start=True, stop=True).then_inc(b_qk_ps, 1)
                    for b in range(B):
                        ins = pe.matmul(BK[:, 4, b * P:(b + 1) * P], XT[:, b * P:(b + 1) * P], w_b[:, 4 * D:5 * D],
                                        start=True, stop=True)
                    ins.then_inc(b_v_ps, 1)
                    pe.wait_ge(b_rot, 2)
                    pe.wait_ge(b_v, 1)

                    def scores(b):
                        for g in range(4):
                            pe.wait_ge(b_blk, 3 * b + g + 1) if g < 3 else pe.wait_ge(b_blk3, b + 1)
                            if b:
                                pe.wait_ge(b_pt, 4 * (b - 1) + g + 1)
                            pe.matmul(bank(g), kT[:, b, :], QB[:, b % 2, 4 * g:4 * g + 4].rearrange("p h t -> p (h t)"),
                                      start=True, stop=True).then_inc(b_s_ps, 1)

                    def values(b):
                        pe.wait_ge(b_pt, 4 * b + 4)
                        if b >= 2:
                            pe.wait_ge(b_oT, b - 1)
                        for g in range(4):
                            o = 32 * g
                            ins = pe.matmul(BK[o:o + 32, 4 + b % 2, :], vq[:, b, o:o + 32],
                                            PT[:, b % 2, 4 * g:4 * g + 4, :].rearrange("p h t -> p (h t)"),
                                            start=True, stop=True)
                        ins.then_inc(b_o_ps, 1)

                    scores(0)
                    for b in range(B):
                        if b + 1 < B:
                            scores(b + 1)
                        values(b)
                    pe.wait_ge(b_oT, 4)
                    ct = CT[:, :, :].rearrange("p b t -> p (b t)")
                    pe.matmul(bank(4), group[:, 0, :], ct, start=True, stop=True).then_inc(b_oc_ps, 1)
                    pe.wait_ge(b_sq, 1)
                    pe.matmul(bank(5), group[:, 1, :], T0[:, :, :].rearrange("p b t -> p (b t)"), start=True, stop=True)\
                      .then_inc(b_var_ps, 1)
                    stay_warm(0, 12)
                    pe.wait_ge(b_on, 1)
                    project(w_b[:, 5 * D:6 * D])
                if s in "CF":
                    k = FFNS.index(s)
                    ln = LN_C if s == "C" else LN_F
                    stay_warm(3)
                    norm_T(ln, 7)
                    pe.wait_ge(ln_xT, xT_count(ln))
                    wg = w_c[:, 0:8] if s == "C" else w_f[:, :]
                    w1 = w_c1 if s == "C" else w_f1
                    pe.wait_ge(loads["w_c" if s == "C" else "w_e"], 16 if s == "C" else 64)
                    for b in range(B):
                        ins = pe.matmul(BK[:, 4, b * NE:(b + 1) * NE], XT[:, b * P:(b + 1) * P], wg, start=True, stop=True)
                    ins.then_inc(r_lg_ps, 1)
                    pe.wait_ge(loads["w_c1" if s == "C" else "w_f1"], 16)
                    if s == "F":
                        pe.wait_ge(loads["w_f2"], 16)

                    def up(e):
                        for j in range(4):
                            u = 4 * e + j
                            if s == "C":
                                if j % 2 == 0 and u >= 6:
                                    pe.wait_ge(e_g, u // 2 - 2)
                                o = (4 * e + j // 2 + 2 * (j % 2)) * P
                            else:
                                if u >= 6:
                                    pe.wait_ge(e_act, before_f + u - 5)
                                o = u * P
                            ins = pe.matmul(hbank(u), w1[:, o:o + P], XT[:, :], start=True, stop=True)
                            if s == "F" or j % 2:
                                ins.then_inc(e_h_ps, 1)

                    def down(e):
                        n = k * NE + e
                        m = 2 if s == "C" else 4
                        if n >= 2:
                            pe.wait_ge(e_sum, 2 * n - 2)
                        for b in range(B):
                            for j in range(m):
                                if b == 0:
                                    pe.wait_ge(e_g, 2 * e + j + 1) if s == "C" else pe.wait_ge(e_act, before_f + 4 * e + j + 1)
                                w = w_c[:, 8 + j * D:8 + (j + 1) * D] if s == "C" else w_f2[:, (4 * e + j) * D:(4 * e + j + 1) * D]
                                ins = pe.matmul(BK[:, 4 + e % 2, b * P:(b + 1) * P], GT[:, e % 2, j, b * P:(b + 1) * P], w,
                                                start=(j == 0), stop=(j == m - 1))
                        ins.then_inc(e_y_ps, 1)

                    up(0)
                    pe.wait_ge(r_z, k + 1)
                    for e in range(NE):
                        if e + 1 < NE:
                            up(e + 1)
                        down(e)
                if s == "D":
                    stay_warm(3)
                    norm_T(LN_D, 7)
                    pe.wait_ge(ln_xT, xT_count(LN_D))
                    pe.matmul(bank(6), w_d[:, 2 * D:3 * D], XT[:, :], start=True, stop=True).then_inc(d_q_ps, 1)
                    pe.wait_ge(d_q, 1)

                    def scores(b):
                        for g in range(4):
                            pe.wait_ge(d_blk, 4 * b + g + 1)
                            if b:
                                pe.wait_ge(d_ss, 4 * (b - 1) + g + 1)
                            pe.matmul(bank(g), qT[:, b, :], QB[:, b % 2, 4 * g:4 * g + 4].rearrange("p h t -> p (h t)"),
                                      start=True, stop=True).then_inc(d_s_ps, 1)

                    def values(b):
                        for g in range(4):
                            n = 4 * b + g
                            pe.wait_ge(d_exp, n + 1)
                            if n >= 2:
                                pe.wait_ge(d_pT, n - 1)
                            for h in range(4):
                                ins = pe.transpose(BK[:, 4 + n % 2, h * P:(h + 1) * P], SS[:, b % 2, 4 * g + h, :], ident[:, :])
                            ins.then_inc(d_pT_ps, 1)
                        pe.wait_ge(d_pT, 4 * b + 4)
                        if b:
                            pe.wait_ge(d_om, b)
                        for dst, w in ((6, None), (7, ones)):
                            for g in range(4):
                                o = 32 * g
                                lhs = vd[:, b, o:o + 32] if w is None else ones[:, 0:32]
                                ins = pe.matmul(BK[o:o + 32, dst, :], lhs,
                                                PT[:, b % 2, 4 * g:4 * g + 4, :].rearrange("p h t -> p (h t)"),
                                                start=True, stop=True)
                        ins.then_inc(d_o_ps, 1)

                    scores(0)
                    for b in range(B):
                        if b + 1 < B:
                            scores(b + 1)
                        values(b)
                    pe.wait_ge(d_om, 4)
                    with pe.If(flagged(pe, flag_d, FDI)):
                        pe.sem_inc(gd_kv_ps, 1)
                        pe.sem_inc(gd_s_ps, 1)
                        pe.wait_ge(gd_m0, 2)
                        with pe.Fori(0, B) as b:
                            with pe.Fori(0, S2 // P) as c:
                                it = b * (S2 // P) + c
                                pe.wait_ge(gd_in, it * 16 + 16)
                                pe.wait_ge(gd_k, 1 + it)
                                pe.wait_ge(gd_v, 1 + it)
                                pe.wait_ge(gd_oT, 1 + b)
                                pe.matmul(BK[:, 0, 0:P], w_d[:, 0:D], GC, start=True, stop=True)
                                pe.matmul(BK[:, 1, 0:P], GC, w_d[:, D:2 * D], start=True, stop=True).then_inc(gd_kv_ps, 1)
                            with pe.Fori(0, H) as h:
                                it = b * H + h
                                pe.wait_ge(gd_k, 1 + b * (S2 // P) + S2 // P)
                                pe.wait_ge(gd_v, 1 + b * (S2 // P) + S2 // P)
                                pe.wait_ge(gd_q, it + 1)
                                pe.wait_ge(gd_o, 1 + it)
                                for j in range(4):
                                    ins = pe.matmul(bank(j), GQ, GK[:, j * 512:(j + 1) * 512], start=True, stop=True)
                                ins.then_inc(gd_s_ps, 1)
                                pe.wait_ge(gd_exp, it + 1)
                                for c in range(S2 // P):
                                    ins = pe.transpose(BK[:, 4 + c // 4, c % 4 * P:c % 4 * P + P], GSC[:, c * P:(c + 1) * P],
                                                       ident[:, :])
                                    if c % 4 == 3:
                                        ins.then_inc(gd_tr, 1)
                                pe.wait_ge(gd_p, 4 * it + 4)
                                for c in range(S2 // P):
                                    ins = pe.matmul(BK[:, 0, 0:D], GP[:, c, :], GV[:, c, :], start=(c == 0),
                                                    stop=(c == S2 // P - 1))
                                ins.then_inc(gd_o_ps, 1)
                            pe.wait_ge(gd_o, 1 + b * H + H)
                            pe.transpose(BK[:, 1, 0:P], GO, ident[:, :]).then_inc(gd_oT_ps, 1)
                        pe.wait_ge(gd_oT, 1 + B)
                    project(w_d[:, 3 * D:4 * D])
                if s == "E":
                    stay_warm(3)
                    norm_T(LN_E, 7)
                    pe.wait_ge(ln_xT, xT_count(LN_E))
                    pe.wait_ge(loads["w_e"], 64)
                    pe.wait_ge(l_mix, 1)
                    for b in range(B):
                        ins = pe.matmul(BK[:, b, 0:WE_O], XT[:, b * P:(b + 1) * P], w_e[:, 0:WE_O], start=True, stop=True)
                    ins.then_inc(l_qkv_ps, 1)
                    pe.wait_ge(ctx_ready, 1)
                    transposes(CT, 7, ctxT_ps)
                    pe.wait_ge(ctxT_ready, len([q for q in STAGES if q in "AE"]))
                    project(w_e[:, WE_O:WE_FF], (6, 7))
                    stay_warm(3)
                    norm_T(LN_E2, 5)
                    pe.wait_ge(ln_xT, xT_count(LN_E2))
                    for j, (o, w) in enumerate(FFT):
                        for c in range(2):
                            bk = j if c == 0 else (3, 4, 6)[j]
                            o2 = WE_FF + FF * c + o
                            pe.matmul(BK[0:w, bk, :], w_e[:, o2:o2 + w], XT[:, :], start=True, stop=True).then_inc(l_ff_ps, 1)
                    pe.wait_ge(l_ff, 3)
                    for b in range(B):
                        for j, (o, w) in enumerate(FFT):
                            ins = pe.matmul(BK[:, (7, 5)[b // 2], b * P:(b + 1) * P], HF[0:w, j, b * P:(b + 1) * P],
                                            w_e2[0:w, j, :], start=(j == 0), stop=(j == 2))
                        if b % 2:
                            ins.then_inc(proj_ps, 1)


_OUT = ((P, B, D), "float32")


def kernel(**inputs):
    import concourse.bacc as bacc
    from concourse.bass_utils import run_bass_kernel_spmd

    nc = bacc.Bacc("TRN2", target_bir_lowering=False, num_devices=1)
    arrays = layouts(inputs)
    t = {n: nc.dram_tensor(n + "_dram", a.shape, mybir.dt.from_np(a.dtype), kind="ExternalInput").ap()
         for n, a in arrays.items()}
    out = nc.dram_tensor("out_dram", (P, B, D), F32, kind="ExternalOutput").ap()
    program(nc, t, out)
    r = run_bass_kernel_spmd(nc, [{n + "_dram": a for n, a in arrays.items()}], core_ids=[0])
    return np.ascontiguousarray(r.results[0]["out_dram"].transpose(1, 0, 2))
```
